# Optimizing a Trainium2 kernel written in Bass

```python
import numpy as np
import jax
import jax.numpy as jnp

def _softmax(x, axis=-1):
    return jax.nn.softmax(x, axis=axis)

def _gelu(x):
    return jax.nn.gelu(x, approximate=True)

def _silu(x):
    return jax.nn.silu(x)

def _sigmoid(x):
    return jax.nn.sigmoid(x)

def _layernorm(x, axis=-1, eps=1e-05):
    m = jnp.mean(x, axis=axis, keepdims=True)
    v = jnp.var(x, axis=axis, keepdims=True)
    return (x - m) / jnp.sqrt(v + eps)

def _scatter_add(tgt, idx, src, axis=0):
    return tgt.at[idx].add(src)

def _segment_sum(src, seg, n):
    return jax.ops.segment_sum(src, seg, n)
kernel_name = 'mk_prb_d4_jaxref_r8_7eb6db'

def setup_inputs(seed: int=0):
    np.random.seed(seed)
    _w = jnp.asarray

    def _L0_attn_setup():
        import jax, jax.numpy as jnp
        import numpy as np
        B, S, HID = (2, 512, 512)
        H, HKV, D = (32, 8, 128)
        G = H // HKV
        EPS = 1e-06

        def _reference_tuple_inner(hidden_states, Wq, bq, Wk, bk, Wv, bv, Wo, M, z):
            b, s, _ = hidden_states.shape
            q = (hidden_states @ Wq.T + bq).reshape(b, s, H, D)
            k = (hidden_states @ Wk.T + bk).reshape(b, s, HKV, D)
            v = (hidden_states @ Wv.T + bv).reshape(b, s, HKV, D)
            sig_q = jax.nn.elu(q) + 1.0
            sig_k = jax.nn.elu(k) + 1.0
            q_sel = sig_q[:, :, ::G, :]
            num = jnp.einsum('bshd,hde->bshe', q_sel, M)
            den = jnp.einsum('bshd,hd->bsh', q_sel, z)[..., None] + EPS
            retrieved = num / den
            out_heads = jnp.repeat(retrieved, G, axis=2)
            output = out_heads.reshape(b, s, H * D) @ Wo.T
            M_new = M + jnp.einsum('bshd,bshe->hde', sig_k, v)
            z_new = z + sig_k.sum(axis=(0, 1))
            return (output, M_new, z_new)
        key = jax.random.key(seed)
        ks = jax.random.split(key, 10)
        s = 0.02
        return {'hidden_states': jax.random.normal(ks[0], (B, S, HID), jnp.float32), 'Wq': jax.random.normal(ks[1], (H * D, HID), jnp.float32) * s, 'bq': jnp.zeros((H * D,), jnp.float32), 'Wk': jax.random.normal(ks[2], (HKV * D, HID), jnp.float32) * s, 'bk': jnp.zeros((HKV * D,), jnp.float32), 'Wv': jax.random.normal(ks[3], (HKV * D, HID), jnp.float32) * s, 'bv': jnp.zeros((HKV * D,), jnp.float32), 'Wo': jax.random.normal(ks[4], (HID, H * D), jnp.float32) * s, 'M': jax.random.normal(ks[5], (HKV, D, D), jnp.float32), 'z': jax.random.uniform(ks[6], (HKV, D), jnp.float32) * 100.0 + 1.0}
    _L0_attn_in = _L0_attn_setup()

    def _L0_ffn_setup():
        import jax, jax.numpy as jnp
        import numpy as np
        R = 16
        NUM_EXPERTS = 8
        TOP_K = 2
        LORA_ALPHA = 32
        SCALING = LORA_ALPHA / R
        key = jax.random.key(seed)
        ks = jax.random.split(key, 6)
        d_in, d_out = (512, 512)
        x = jax.random.normal(ks[0], (4, 256, d_in), dtype=jnp.float32)
        W_base = jax.random.normal(ks[1], (d_out, d_in), dtype=jnp.float32) * 0.02
        b_base = jax.random.normal(ks[2], (d_out,), dtype=jnp.float32) * 0.02
        W_router = jax.random.normal(ks[3], (NUM_EXPERTS, d_in), dtype=jnp.float32) * 0.01
        A = jax.random.normal(ks[4], (NUM_EXPERTS, R, d_in), dtype=jnp.float32) * 0.02
        B = jax.random.normal(ks[5], (NUM_EXPERTS, d_out, R), dtype=jnp.float32) * 0.02
        return {'x': x, 'W_base': W_base, 'b_base': b_base, 'W_router': W_router, 'A': A, 'B': B}
    _L0_ffn_in = _L0_ffn_setup()

    def _L1_attn_setup():
        import jax, jax.numpy as jnp
        import numpy as np
        import math
        FACTOR = 1
        key = jax.random.key(seed)
        x = jax.random.normal(key, (8, 64, 512), dtype=jnp.float32)
        return {'x': x}
    _L1_attn_in = _L1_attn_setup()

    def _L1_ffn_setup():
        import jax, jax.numpy as jnp
        import numpy as np
        B_, S, D_IN, D_OUT = (4, 256, 512, 512)
        N, RANK, ALPHA = (8, 16, 32)
        SCALE = ALPHA / RANK
        key = jax.random.key(seed)
        kx, ka, kb, kw, kbias = jax.random.split(key, 5)
        x = jax.random.normal(kx, (B_, S, D_IN), dtype=jnp.float32)
        lora_A = jax.random.normal(ka, (N, RANK, D_IN), dtype=jnp.float32) * (1.0 / np.sqrt(D_IN))
        lora_B = jax.random.normal(kb, (N, D_OUT, RANK), dtype=jnp.float32) * (1.0 / np.sqrt(RANK))
        W = jax.random.normal(kw, (D_OUT, D_IN), dtype=jnp.float32) * (1.0 / np.sqrt(D_IN))
        bias = jax.random.normal(kbias, (D_OUT,), dtype=jnp.float32) * 0.01
        lora_weights = jnp.full((N,), 1.0 / N, dtype=jnp.float32)
        return {'x': x, 'lora_A': lora_A, 'lora_B': lora_B, 'W': W, 'bias': bias, 'lora_weights': lora_weights}
    _L1_ffn_in = _L1_ffn_setup()

    def _L2_attn_setup():
        import jax, jax.numpy as jnp
        import numpy as np
        N_HEADS = 32
        N_KV_HEADS = 8
        DIM = 512
        HEAD_DIM = DIM // N_HEADS
        N_REP = N_HEADS // N_KV_HEADS
        ROPE_THETA = 10000.0

        def _apply_rope(x):
            seq = x.shape[2]
            hd = x.shape[-1]
            inv_freq = 1.0 / ROPE_THETA ** (jnp.arange(0, hd, 2, dtype=jnp.float32) / hd)
            angles = jnp.arange(seq, dtype=jnp.float32)[:, None] * inv_freq[None, :]
            cos = jnp.cos(angles)[None, None]
            sin = jnp.sin(angles)[None, None]
            x1 = x[..., 0::2]
            x2 = x[..., 1::2]
            r1 = x1 * cos - x2 * sin
            r2 = x1 * sin + x2 * cos
            return jnp.stack([r1, r2], axis=-1).reshape(x.shape)
        key = jax.random.key(seed)
        k1, k2, k3 = jax.random.split(key, 3)
        bs, seq = (1, 256)
        x = jax.random.normal(k1, (bs, seq, DIM), dtype=jnp.float32)
        w_qkv = jax.random.normal(k2, (DIM, HEAD_DIM * (N_HEADS + 2 * N_KV_HEADS)), dtype=jnp.float32) * 0.02
        w_o = jax.random.normal(k3, (N_HEADS * HEAD_DIM, DIM), dtype=jnp.float32) * 0.02
        return {'x': x, 'w_qkv': w_qkv, 'w_o': w_o}
    _L2_attn_in = _L2_attn_setup()

    def _L2_ffn_setup():
        import jax, jax.numpy as jnp
        import numpy as np
        IN_F = 512
        OUT_F = 512
        N_CLUSTERS = 64
        THRESHOLD = 0.01
        TEMPERATURE = 0.1
        BATCH, SEQ = (4, 256)
        key = jax.random.key(seed)
        k1, k2, k3, k4, k5 = jax.random.split(key, 5)
        s = 1.0 / np.sqrt(IN_F)
        return {'input': jax.random.normal(k1, (BATCH, SEQ, IN_F), dtype=jnp.float32), 'weight': jax.random.normal(k2, (OUT_F, IN_F), dtype=jnp.float32) * s, 'bias': jax.random.uniform(k3, (OUT_F,), dtype=jnp.float32, minval=-s, maxval=s), 'centroids': jax.random.normal(k4, (N_CLUSTERS, IN_F), dtype=jnp.float32) * s, 'assignments': jax.random.randint(k5, (OUT_F,), 0, N_CLUSTERS, dtype=jnp.int32)}
    _L2_ffn_in = _L2_ffn_setup()

    def _L3_attn_setup():
        import math
        import jax, jax.numpy as jnp
        import numpy as np

        def _rope_tables(T, h, dtype):
            pos = jnp.arange(T, dtype=jnp.float32)
            thetas = 1.0 / 10000.0 ** (jnp.arange(0, h, 2, dtype=jnp.float32) / h)
            pt = jnp.outer(pos, thetas)
            pt = jnp.concatenate([pt, pt], axis=-1)
            return (jnp.sin(pt).astype(dtype), jnp.cos(pt).astype(dtype))

        def _apply_rope(x, sin, cos):
            h = x.shape[-1]
            rot = jnp.concatenate([-x[..., h // 2:], x[..., :h // 2]], axis=-1)
            return x * cos + rot * sin
        key = jax.random.key(seed)
        ks = jax.random.split(key, 5)
        B, T, C = (2, 256, 512)
        s = 1.0 / math.sqrt(C)
        return {'x': jax.random.normal(ks[0], (B, T, C), dtype=jnp.float32), 'wq': jax.random.normal(ks[1], (C, C), dtype=jnp.float32) * s, 'wk': jax.random.normal(ks[2], (C, C), dtype=jnp.float32) * s, 'wv': jax.random.normal(ks[3], (C, C), dtype=jnp.float32) * s, 'wo': jax.random.normal(ks[4], (C, C), dtype=jnp.float32) * s}
    _L3_attn_in = _L3_attn_setup()

    def _L3_ffn_setup():
        import jax, jax.numpy as jnp
        import numpy as np
        DIM = 512
        INTER = 128
        E = 16
        GROUPS = 4
        LIM = 2
        K = 2
        SHARED_INTER = 2 * INTER
        SCALE = 1.0
        key = jax.random.key(seed)
        ks = jax.random.split(key, 16)

        def n(k, shape, s=0.02):
            return jax.random.normal(k, shape, jnp.float32) * s
        return {'x': jax.random.normal(ks[0], (1, 256, DIM), jnp.float32), 'router_w': n(ks[1], (DIM, E)), 'router_b': n(ks[2], (E,)), 'router_bias': n(ks[3], (E,), 1.0), 'ew1': n(ks[4], (E, DIM, INTER)), 'eb1': n(ks[5], (E, INTER)), 'ew2': n(ks[6], (E, DIM, INTER)), 'eb2': n(ks[7], (E, INTER)), 'ew3': n(ks[8], (E, INTER, DIM)), 'eb3': n(ks[9], (E, DIM)), 'sw1': n(ks[10], (DIM, SHARED_INTER)), 'sb1': n(ks[11], (SHARED_INTER,)), 'sw2': n(ks[12], (DIM, SHARED_INTER)), 'sb2': n(ks[13], (SHARED_INTER,)), 'sw3': n(ks[14], (SHARED_INTER, DIM)), 'sb3': n(ks[15], (DIM,))}
    _L3_ffn_in = _L3_ffn_setup()
    _d = {'L0_attn_hidden_states': _L0_attn_in['hidden_states'], 'L0_attn_Wq': _L0_attn_in['Wq'], 'L0_attn_bq': _L0_attn_in['bq'], 'L0_attn_Wk': _L0_attn_in['Wk'], 'L0_attn_bk': _L0_attn_in['bk'], 'L0_attn_Wv': _L0_attn_in['Wv'], 'L0_attn_bv': _L0_attn_in['bv'], 'L0_attn_Wo': _L0_attn_in['Wo'], 'L0_attn_M': _L0_attn_in['M'], 'L0_attn_z': _L0_attn_in['z'], 'L0_ffn_W_base': _L0_ffn_in['W_base'], 'L0_ffn_b_base': _L0_ffn_in['b_base'], 'L0_ffn_W_router': _L0_ffn_in['W_router'], 'L0_ffn_A': _L0_ffn_in['A'], 'L0_ffn_B': _L0_ffn_in['B'], 'L1_ffn_lora_A': _L1_ffn_in['lora_A'], 'L1_ffn_lora_B': _L1_ffn_in['lora_B'], 'L1_ffn_W': _L1_ffn_in['W'], 'L1_ffn_bias': _L1_ffn_in['bias'], 'L1_ffn_lora_weights': _L1_ffn_in['lora_weights'], 'L2_attn_w_qkv': _L2_attn_in['w_qkv'], 'L2_attn_w_o': _L2_attn_in['w_o'], 'L2_ffn_weight': _L2_ffn_in['weight'], 'L2_ffn_bias': _L2_ffn_in['bias'], 'L2_ffn_centroids': _L2_ffn_in['centroids'], 'L2_ffn_assignments': _L2_ffn_in['assignments'], 'L3_attn_wq': _L3_attn_in['wq'], 'L3_attn_wk': _L3_attn_in['wk'], 'L3_attn_wv': _L3_attn_in['wv'], 'L3_attn_wo': _L3_attn_in['wo'], 'L3_ffn_router_w': _L3_ffn_in['router_w'], 'L3_ffn_router_b': _L3_ffn_in['router_b'], 'L3_ffn_router_bias': _L3_ffn_in['router_bias'], 'L3_ffn_ew1': _L3_ffn_in['ew1'], 'L3_ffn_eb1': _L3_ffn_in['eb1'], 'L3_ffn_ew2': _L3_ffn_in['ew2'], 'L3_ffn_eb2': _L3_ffn_in['eb2'], 'L3_ffn_ew3': _L3_ffn_in['ew3'], 'L3_ffn_eb3': _L3_ffn_in['eb3'], 'L3_ffn_sw1': _L3_ffn_in['sw1'], 'L3_ffn_sb1': _L3_ffn_in['sb1'], 'L3_ffn_sw2': _L3_ffn_in['sw2'], 'L3_ffn_sb2': _L3_ffn_in['sb2'], 'L3_ffn_sw3': _L3_ffn_in['sw3'], 'L3_ffn_sb3': _L3_ffn_in['sb3']}
    _x0 = _d['L0_attn_hidden_states']
    _d['L0_attn_hidden_states'] = jax.random.normal(jax.random.fold_in(jax.random.key(seed), 1), (4, 512, 512), dtype=_x0.dtype)
    del _x0
    return _d

def reference(L0_attn_hidden_states, L0_attn_Wq, L0_attn_bq, L0_attn_Wk, L0_attn_bk, L0_attn_Wv, L0_attn_bv, L0_attn_Wo, L0_attn_M, L0_attn_z, L0_ffn_W_base, L0_ffn_b_base, L0_ffn_W_router, L0_ffn_A, L0_ffn_B, L1_ffn_lora_A, L1_ffn_lora_B, L1_ffn_W, L1_ffn_bias, L1_ffn_lora_weights, L2_attn_w_qkv, L2_attn_w_o, L2_ffn_weight, L2_ffn_bias, L2_ffn_centroids, L2_ffn_assignments, L3_attn_wq, L3_attn_wk, L3_attn_wv, L3_attn_wo, L3_ffn_router_w, L3_ffn_router_b, L3_ffn_router_bias, L3_ffn_ew1, L3_ffn_eb1, L3_ffn_ew2, L3_ffn_eb2, L3_ffn_ew3, L3_ffn_eb3, L3_ffn_sw1, L3_ffn_sb1, L3_ffn_sw2, L3_ffn_sb2, L3_ffn_sw3, L3_ffn_sb3):

    def _L0_attn_ref(hidden_states, Wq, bq, Wk, bk, Wv, bv, Wo, M, z):
        import jax, jax.numpy as jnp
        import numpy as np
        B, S, HID = (2, 512, 512)
        H, HKV, D = (32, 8, 128)
        G = H // HKV
        EPS = 1e-06

        def _reference_tuple_inner(hidden_states, Wq, bq, Wk, bk, Wv, bv, Wo, M, z):
            b, s, _ = hidden_states.shape
            q = (hidden_states @ Wq.T + bq).reshape(b, s, H, D)
            k = (hidden_states @ Wk.T + bk).reshape(b, s, HKV, D)
            v = (hidden_states @ Wv.T + bv).reshape(b, s, HKV, D)
            sig_q = jax.nn.elu(q) + 1.0
            sig_k = jax.nn.elu(k) + 1.0
            q_sel = sig_q[:, :, ::G, :]
            num = jnp.einsum('bshd,hde->bshe', q_sel, M)
            den = jnp.einsum('bshd,hd->bsh', q_sel, z)[..., None] + EPS
            retrieved = num / den
            out_heads = jnp.repeat(retrieved, G, axis=2)
            output = out_heads.reshape(b, s, H * D) @ Wo.T
            M_new = M + jnp.einsum('bshd,bshe->hde', sig_k, v)
            z_new = z + sig_k.sum(axis=(0, 1))
            return (output, M_new, z_new)
        return _reference_tuple_inner(hidden_states, Wq, bq, Wk, bk, Wv, bv, Wo, M, z)[0]

    def _L0_ffn_ref(x, W_base, b_base, W_router, A, B):
        import jax, jax.numpy as jnp
        import numpy as np
        R = 16
        NUM_EXPERTS = 8
        TOP_K = 2
        LORA_ALPHA = 32
        SCALING = LORA_ALPHA / R
        orig_shape = x.shape
        d_in = x.shape[-1]
        x_flat = x.reshape(-1, d_in)
        logits = x_flat @ W_router.T
        probs = jax.nn.softmax(logits, axis=-1)
        topk_probs, topk_idx = jax.lax.top_k(probs, TOP_K)
        topk_probs = topk_probs / jnp.sum(topk_probs, axis=-1, keepdims=True)
        onehot = jax.nn.one_hot(topk_idx, NUM_EXPERTS, dtype=x.dtype)
        combine = jnp.einsum('nk,nke->ne', topk_probs, onehot)
        h = jnp.einsum('nd,erd->ner', x_flat, A)
        hw = h * combine[:, :, None]
        expert_out = jnp.einsum('ner,eor->no', hw, B) * SCALING
        base_out = x_flat @ W_base.T + b_base
        out = base_out + expert_out
        return out.reshape(*orig_shape[:-1], W_base.shape[0])

    def _L1_attn_ref(x):
        import jax, jax.numpy as jnp
        import numpy as np
        import math
        FACTOR = 1
        B, C, L = x.shape
        xh = x[:, None]
        f = jnp.fft.rfft(xh, axis=-1)
        corr = jnp.fft.irfft(f * jnp.conj(f), n=L, axis=-1)
        top_k = int(FACTOR * math.log(L))
        weights, delay = jax.lax.top_k(corr, top_k)
        tmp_corr = jax.nn.softmax(weights, axis=-1)
        init_index = jnp.arange(L)
        idx = (init_index[None, None, None, None, :] + delay[..., None]) % L
        pattern = jnp.take_along_axis(xh[:, :, :, None, :], idx, axis=-1)
        delays_agg = jnp.sum(pattern * tmp_corr[..., None], axis=-2)
        return delays_agg[:, 0]

    def _L1_ffn_ref(x, lora_A, lora_B, W, bias, lora_weights):
        import jax, jax.numpy as jnp
        import numpy as np
        B_, S, D_IN, D_OUT = (4, 256, 512, 512)
        N, RANK, ALPHA = (8, 16, 32)
        SCALE = ALPHA / RANK
        h = jnp.einsum('bsd,nrd->nbsr', x, lora_A)
        coef = (SCALE * lora_weights)[:, None, None]
        lora_out = jnp.einsum('nbsr,nor->bso', h, lora_B * coef)
        base = jnp.einsum('bsd,od->bso', x, W) + bias
        return base + lora_out

    def _L2_attn_ref(x, w_qkv, w_o):
        import jax, jax.numpy as jnp
        import numpy as np
        N_HEADS = 32
        N_KV_HEADS = 8
        DIM = 512
        HEAD_DIM = DIM // N_HEADS
        N_REP = N_HEADS // N_KV_HEADS
        ROPE_THETA = 10000.0

        def _apply_rope(x):
            seq = x.shape[2]
            hd = x.shape[-1]
            inv_freq = 1.0 / ROPE_THETA ** (jnp.arange(0, hd, 2, dtype=jnp.float32) / hd)
            angles = jnp.arange(seq, dtype=jnp.float32)[:, None] * inv_freq[None, :]
            cos = jnp.cos(angles)[None, None]
            sin = jnp.sin(angles)[None, None]
            x1 = x[..., 0::2]
            x2 = x[..., 1::2]
            r1 = x1 * cos - x2 * sin
            r2 = x1 * sin + x2 * cos
            return jnp.stack([r1, r2], axis=-1).reshape(x.shape)
        bs, seq, _ = x.shape
        qkv = x @ w_qkv
        q_sz = N_HEADS * HEAD_DIM
        kv_sz = N_KV_HEADS * HEAD_DIM
        xq = qkv[..., :q_sz].reshape(bs, seq, N_HEADS, HEAD_DIM).transpose(0, 2, 1, 3)
        xk = qkv[..., q_sz:q_sz + kv_sz].reshape(bs, seq, N_KV_HEADS, HEAD_DIM).transpose(0, 2, 1, 3)
        xv = qkv[..., q_sz + kv_sz:].reshape(bs, seq, N_KV_HEADS, HEAD_DIM).transpose(0, 2, 1, 3)
        xq = _apply_rope(xq)
        xk = _apply_rope(xk)
        keys = jnp.repeat(xk, N_REP, axis=1)
        values = jnp.repeat(xv, N_REP, axis=1)
        scale = 1.0 / jnp.sqrt(jnp.float32(HEAD_DIM))
        scores = jnp.einsum('bhsd,bhtd->bhst', xq, keys) * scale
        causal = jnp.tril(jnp.ones((seq, seq), dtype=bool))[None, None]
        scores = jnp.where(causal, scores, -jnp.inf)
        probs = jax.nn.softmax(scores, axis=-1)
        out = jnp.einsum('bhst,bhtd->bhsd', probs, values)
        out = out.transpose(0, 2, 1, 3).reshape(bs, seq, N_HEADS * HEAD_DIM)
        return out @ w_o

    def _L2_ffn_ref(input, weight, bias, centroids, assignments):
        import jax, jax.numpy as jnp
        import numpy as np
        IN_F = 512
        OUT_F = 512
        N_CLUSTERS = 64
        THRESHOLD = 0.01
        TEMPERATURE = 0.1
        BATCH, SEQ = (4, 256)
        shape = input.shape
        x = input.reshape(-1, shape[-1])
        dots = jax.nn.softmax(x @ centroids.T / TEMPERATURE, axis=-1)
        hits = dots > THRESHOLD
        query_sel = jnp.any(hits, axis=1)
        cluster_sel = jnp.any(hits, axis=0)
        row_sel = cluster_sel[assignments]
        dense = x @ weight.T + bias
        out = jnp.where(query_sel[:, None] & row_sel[None, :], dense, jnp.zeros((), dense.dtype))
        return out.reshape(*shape[:-1], -1)

    def _L3_attn_ref(x, wq, wk, wv, wo):
        import math
        import jax, jax.numpy as jnp
        import numpy as np

        def _rope_tables(T, h, dtype):
            pos = jnp.arange(T, dtype=jnp.float32)
            thetas = 1.0 / 10000.0 ** (jnp.arange(0, h, 2, dtype=jnp.float32) / h)
            pt = jnp.outer(pos, thetas)
            pt = jnp.concatenate([pt, pt], axis=-1)
            return (jnp.sin(pt).astype(dtype), jnp.cos(pt).astype(dtype))

        def _apply_rope(x, sin, cos):
            h = x.shape[-1]
            rot = jnp.concatenate([-x[..., h // 2:], x[..., :h // 2]], axis=-1)
            return x * cos + rot * sin
        B, T, C = x.shape
        n_head = 32
        h = C // n_head

        def proj(w):
            y = jnp.einsum('btc,dc->btd', x, w)
            return y.reshape(B, T, n_head, h).transpose(0, 2, 1, 3)
        q, k, v = (proj(wq), proj(wk), proj(wv))
        sin, cos = _rope_tables(T, h, x.dtype)
        q = _apply_rope(q, sin, cos)
        k = _apply_rope(k, sin, cos)
        scores = jnp.einsum('bnth,bnsh->bnts', q, k) * (1.0 / math.sqrt(h))
        causal = jnp.tril(jnp.ones((T, T), dtype=bool))
        scores = jnp.where(causal, scores, -jnp.inf)
        attn = jax.nn.softmax(scores, axis=-1)
        out = jnp.einsum('bnts,bnsh->bnth', attn, v)
        out = out.transpose(0, 2, 1, 3).reshape(B, T, C)
        return jnp.einsum('btc,dc->btd', out, wo)

    def _L3_ffn_ref(x, router_w, router_b, router_bias, ew1, eb1, ew2, eb2, ew3, eb3, sw1, sb1, sw2, sb2, sw3, sb3):
        import jax, jax.numpy as jnp
        import numpy as np
        DIM = 512
        INTER = 128
        E = 16
        GROUPS = 4
        LIM = 2
        K = 2
        SHARED_INTER = 2 * INTER
        SCALE = 1.0
        shape = x.shape
        xt = x.reshape(-1, DIM)
        T = xt.shape[0]
        logits = xt @ router_w + router_b
        scores = jax.nn.softmax(logits.astype(jnp.float32), axis=-1) + router_bias
        g = scores.reshape(T, GROUPS, E // GROUPS)
        _, gidx = jax.lax.top_k(g.max(axis=-1), LIM)
        keep = jnp.zeros((T, GROUPS), bool).at[jnp.arange(T)[:, None], gidx].set(True)
        masked = jnp.where(keep[:, :, None], g, -jnp.inf).reshape(T, E)
        _, idx = jax.lax.top_k(masked, K)
        vals = (jnp.take_along_axis(scores, idx, axis=1) * SCALE).astype(x.dtype)
        gate = jnp.zeros((T, E), x.dtype).at[jnp.arange(T)[:, None], idx].add(vals)

        def step(y, p):
            w1, b1, w2, b2, w3, b3, ge = p
            h = jax.nn.silu(xt @ w1 + b1) * (xt @ w2 + b2)
            return (y + ge[:, None] * (h @ w3 + b3), None)
        y, _ = jax.lax.scan(step, jnp.zeros_like(xt), (ew1, eb1, ew2, eb2, ew3, eb3, gate.T))
        z = jax.nn.silu(xt @ sw1 + sb1) * (xt @ sw2 + sb2) @ sw3 + sb3
        return (y + z).reshape(shape)
    x = L0_attn_hidden_states
    xn = _layernorm(x, axis=-1)
    x = x + _L0_attn_ref(xn, L0_attn_Wq, L0_attn_bq, L0_attn_Wk, L0_attn_bk, L0_attn_Wv, L0_attn_bv, L0_attn_Wo, L0_attn_M, L0_attn_z) + _L0_ffn_ref(xn, L0_ffn_W_base, L0_ffn_b_base, L0_ffn_W_router, L0_ffn_A, L0_ffn_B)
    xn = _layernorm(x, axis=-1)
    x = x + _L1_attn_ref(xn) + _L1_ffn_ref(xn, L1_ffn_lora_A, L1_ffn_lora_B, L1_ffn_W, L1_ffn_bias, L1_ffn_lora_weights)
    xn = _layernorm(x, axis=-1)
    x = x + _L2_attn_ref(xn, L2_attn_w_qkv, L2_attn_w_o) + _L2_ffn_ref(xn, L2_ffn_weight, L2_ffn_bias, L2_ffn_centroids, L2_ffn_assignments)
    xn = _layernorm(x, axis=-1)
    x = x + _L3_attn_ref(xn, L3_attn_wq, L3_attn_wk, L3_attn_wv, L3_attn_wo) + _L3_ffn_ref(xn, L3_ffn_router_w, L3_ffn_router_b, L3_ffn_router_bias, L3_ffn_ew1, L3_ffn_eb1, L3_ffn_ew2, L3_ffn_eb2, L3_ffn_ew3, L3_ffn_eb3, L3_ffn_sw1, L3_ffn_sb1, L3_ffn_sw2, L3_ffn_sb2, L3_ffn_sw3, L3_ffn_sb3)
    return x

_drawn_inputs = setup_inputs


def setup_inputs(seed=0):
    import zlib

    import numpy as np

    out = dict(_drawn_inputs(seed))
    spreads = {'L0_attn_bq': (0.0, 2.0),
     'L0_attn_bk': (0.0, 0.1),
     'L0_attn_bv': (0.0, 0.1),
     'L1_ffn_lora_weights': (0.125, 0.6)}
    factors = {'L0_attn_Wq': 8.0,
     'L0_attn_Wo': 8.0,
     'L0_attn_M': 8.0,
     'L0_attn_z': 200.0,
     'L0_ffn_b_base': 3.438,
     'L1_ffn_bias': 8.0,
     'L2_attn_w_qkv': 6.365,
     'L2_attn_w_o': 6.308,
     'L2_ffn_bias': 6.226,
     'L3_ffn_router_w': 48.304,
     'L3_ffn_router_b': 64.0,
     'L3_ffn_eb1': 64.0,
     'L3_ffn_eb2': 64.0,
     'L3_ffn_eb3': 31.853,
     'L3_ffn_sw1': 4.916,
     'L3_ffn_sb1': 64.0,
     'L3_ffn_sw2': 4.828,
     'L3_ffn_sb2': 64.0,
     'L3_ffn_sw3': 4.81,
     'L3_ffn_sb3': 200.0,
     'L3_attn_wq': 16.37,
     'L3_attn_wk': 19.469,
     'L3_ffn_router_bias': 2.838,
     'L3_ffn_ew1': 6.958,
     'L3_ffn_ew2': 6.788,
     'L3_ffn_ew3': 6.355,
     'L3_attn_wv': 5.526,
     'L3_attn_wo': 5.541}
    for name, (base, spread) in spreads.items():
        noise = np.random.default_rng([zlib.crc32(name.encode()), seed]).standard_normal(out[name].shape)
        drawn = base * np.exp(spread * noise) if base else spread * noise
        out[name] = jnp.asarray(drawn.astype(out[name].dtype))
    for name, factor in factors.items():
        out[name] = (out[name] * factor).astype(out[name].dtype)
    return out
```

```python
from contextlib import ExitStack

import numpy as np
import concourse.bass as bass
from concourse import mybir

F32 = mybir.dt.float32
F32R = mybir.dt.float32r
BF16 = mybir.dt.bfloat16
I32 = mybir.dt.int32
ALU = mybir.AluOpType
ACT = mybir.ActivationFunctionType
AX_X = mybir.AxisListType.X

P = 128
D = 512
NB = 4
S = 512
NT = S // P
KC = D // P
LN_EPS = 1e-5
BIG = 3.0e38


class Semaphores:

    def __init__(self, ctx, nc, tag):
        self.nc, self.tag, self.held = nc, tag, []
        ctx.callback(self.give_back)

    def __call__(self, name):
        self.held.append(self.nc.alloc_semaphore(self.tag + name))
        return self.held[-1]

    def give_back(self):
        self.nc.clear_and_free_semaphores(self.held)
        self.nc.all_engine_barrier()


class Chain:

    def __init__(self, eng, sem, per=0, turn=0):
        self.eng, self.sem, self.base, self.n, self.per = eng, sem, turn * per, 0, per

    def __call__(self, ins):
        self.n += 1
        ins.then_inc(self.sem, 1)
        self.eng.wait_ge(self.sem, self.base + self.n)

    def end(self):
        assert self.n == self.per, (self.sem, self.n, self.per)


class Normed:

    def __init__(self, ctx, nc, tag, ident, banks, sem):
        def sb(name, shape, dt=F32):
            return ctx.enter_context(nc.sbuf_tensor(tag + name, shape, dt))

        self.ident, self.banks = ident, banks
        self.x = sb("X", [P, NT, D])
        self.xn = sb("XN", [P, NT, D])
        self.xt = sb("XT", [P, KC, S])
        self.moments = sb("ST", [P, NT, 6])
        self.mv = sb("MV", [P, NT, 2])
        self.ve = sb("VE", [P, NT])
        self.half = sb("HALF", [P, NT])
        self.rs = sb("RS", [P, NT])
        self.hold = sb("HOLD", [P, 1])
        self.half_set = sem("half_set")
        self.x_loaded = sem("x_loaded")
        self.moments_ready = sem("moments_ready")
        self.stats_ready = sem("stats_ready")
        self.var_ready = sem("var_ready")
        self.rstd_ready = sem("rstd_ready")
        self.xn_ready = sem("xn_ready")
        self.xt_psum = sem("xt_psum")
        self.xt_ready = sem("xt_ready")

    def vector_part(self, dve, b):
        dve.wait_ge(self.x_loaded, b * 16 + 16)
        for t in range(NT):
            dve.bn_stats(self.moments[:, t], self.x[:, t]).then_inc(self.moments_ready, 1)
        dve.wait_ge(self.moments_ready, b * NT + NT)
        dve.memset(self.hold[:], 0.0)
        for t in range(NT):
            dve.bn_aggr(self.mv[:, t], self.moments[:, t]).then_inc(self.stats_ready, 1)
        dve.wait_ge(self.stats_ready, b * NT + NT)
        dve.tensor_scalar(self.ve[:], self.mv[:, :, 1], LN_EPS, None, ALU.add).then_inc(self.var_ready, 1)
        dve.wait_ge(self.rstd_ready, b + 1)
        for t in range(NT):
            dve.tensor_scalar(self.xn[:, t], self.x[:, t], self.mv[:, t, 0:1], self.rs[:, t:t + 1], ALU.subtract,
                              ALU.mult).then_inc(self.xn_ready, 1)

    def pool_setup(self, pool):
        pool.memset(self.half[:], -0.5).then_inc(self.half_set, 1)
        pool.wait_ge(self.half_set, 1)

    def pool_part(self, pool, b):
        pool.wait_ge(self.var_ready, b + 1)
        pool.tensor_tensor(self.rs[:], self.ve[:], self.half[:], ALU.pow).then_inc(self.rstd_ready, 1)

    def tensor_part(self, pe, b):
        for c in range(KC):
            if c >= 2:
                pe.wait_ge(self.xt_ready, b * KC + c - 1)
            for t in range(NT):
                if c == 0:
                    pe.wait_ge(self.xn_ready, b * NT + t + 1)
                ins = pe.transpose(self.banks[:, c % 2, t * P:(t + 1) * P], self.xn[:, t, c * P:(c + 1) * P],
                                   self.ident[:])
            ins.then_inc(self.xt_psum, 1)

    def scalar_part(self, act, b):
        for c in range(KC):
            act.wait_ge(self.xt_psum, b * KC + c + 1)
            act.activation(self.xt[:, c], self.banks[:, c % 2], ACT.Copy).then_inc(self.xt_ready, 1)

H0, R0 = 8, P
G0 = 4
NE0 = 8
TOPB = 14


def layer0(nc, x_in, x_out, wq, bq, zb, mt, wo, wb, bb, wr, la, lb, sel, ident_d):
    with ExitStack() as ctx:
        def sb(name, shape, dt=F32):
            return ctx.enter_context(nc.sbuf_tensor("a_" + name, shape, dt))

        def ps(name, shape, dt=F32):
            return ctx.enter_context(nc.psum_tensor("a_" + name, shape, dt))

        sem = Semaphores(ctx, nc, "a_")

        x_v = x_in.rearrange("b (t p) d -> b p t d", p=P)
        y_v = x_out.rearrange("b (t p) d -> b p t d", p=P)

        WQ = sb("WQ", [P, KC, H0 * P])
        WB = sb("WB", [P, KC, D])
        MW = sb("MW", [P, H0, D])
        MT = sb("MT", [P, H0, P])
        WO = sb("WO", [P, 2, G0, D])
        ZB = sb("ZB", [P, H0, P])
        ZC = sb("ZC", [P, H0])
        BQ = sb("BQ", [P, H0])
        WR = sb("WR", [P, KC, NE0])
        LA = sb("LA", [P, KC, R0])
        LB = sb("LB", [P, D])
        SEL = sb("SEL", [NE0, R0])
        BB = sb("BB", [P, D])
        ident = sb("ident", [P, P])
        X = sb("X", [P, NT, D])
        XN = sb("XN", [P, NT, D])
        XT = sb("XT", [P, KC, S])
        HT = sb("HT", [P, S])
        ST = sb("ST", [P, NT, 6])
        MV = sb("MV", [P, NT, 2])
        VE = sb("VE", [P, NT])
        HALF = sb("HALF", [P, NT])
        RS = sb("RS", [P, NT])
        LG = sb("LG", [P, NT, TOPB])
        LR = sb("LR", [P, NT, TOPB])
        TOP = sb("TOP", [P, NT, 8])
        NM = sb("NM", [P, NT])
        EG = sb("EG", [P, NT, NE0])
        EM = sb("EM", [P, NT, NE0])
        CS = sb("CS", [P, NT])
        CR = sb("CR", [P, NT])
        CB = sb("CB", [P, NT, NE0])
        CT = sb("CT", [NE0, S])
        NEG = sb("NEG", [P, 2, S])
        EX = sb("EX", [P, 2, S])
        RL = sb("RL", [P, 2, S])
        SG = sb("SG", [P, 2, S])
        DN = sb("DN", [P, 2, S])
        SN = sb("SN", [P, 2, S])

        HOLD = sb("HOLD", [P, 1])

        pT = ps("pT", [P, 2, S])
        pQ = ps("pQ", [P, 2, S])
        pO = ps("pO", [P, NT, S])

        w_in = sem("w_in")
        wo_in = [sem("wo_in_even"), sem("wo_in_odd")]
        wo_used = sem("wo_used")
        mw_done = sem("mw_done")
        mw_copied = sem("mw_copied")
        x_loaded = sem("x_loaded")
        stats_ready = sem("stats_ready")
        var_ready = sem("var_ready")
        rstd_ready = sem("rstd_ready")
        xn_ready = sem("xn_ready")
        xt_psum = sem("xt_psum")
        xt_ready = sem("xt_ready")
        router_psum = sem("router_psum")
        top_ready = sem("top_ready")
        shift_ready = sem("shift_ready")
        gates_exp = sem("gates_exp")
        comb_ready = sem("comb_ready")
        comb_psum = sem("comb_psum")
        comb_copied = sem("comb_copied")
        lora_psum = sem("lora_psum")
        lora_copied = sem("lora_copied")
        spread_psum = sem("spread_psum")
        lora_ready = sem("lora_ready")
        q_psum = sem("q_psum")
        neg_ready = sem("neg_ready")
        exp_ready = sem("exp_ready")
        relu_ready = sem("relu_ready")
        sig_ready = sem("sig_ready")
        den_psum = sem("den_psum")
        sign_ready = sem("sign_ready")
        out_psum = sem("out_psum")
        y_ready = sem("y_ready")
        xb_ready = sem("xb_ready")
        y_stored = sem("y_stored")
        dve_step = sem("dve_step")
        pool_step = sem("pool_step")
        pads_set = sem("pads_set")
        ones_set = sem("ones_set")
        zb_ready = sem("zb_ready")

        DVE_PER = NT + 6
        block = ctx.enter_context(nc.Block())

        @block.sync
        def _(sp):
            sp.dma_start(ident[:], ident_d).then_inc(w_in, 16)
            sp.dma_start(MT[:], mt).then_inc(w_in, 16)
            sp.dma_start(WB[:], wb).then_inc(w_in, 16)
            sp.dma_start(WR[:], wr).then_inc(w_in, 16)
            sp.dma_start(LA[:], la).then_inc(w_in, 16)
            sp.dma_start(LB[:], lb).then_inc(w_in, 16)
            sp.dma_start(SEL[:], sel).then_inc(w_in, 16)
            sp.dma_start(ZC[:], zb).then_inc(w_in, 16)
            sp.dma_start(BQ[:], bq).then_inc(w_in, 16)
            sp.dma_start(WQ[:], wq).then_inc(w_in, 16)
            sp.dma_start(BB[:], bb.partition_broadcast(P)).then_inc(w_in, 16)
            with sp.Fori(0, NB) as b:
                sp.wait_ge(y_stored, b * 16 + 16)
                sp.dma_start(X[:], x_v[bass.ds(b, 1)].rearrange("b p t d -> (b p) t d")).then_inc(x_loaded, 16)
                sp.wait_ge(y_ready, b * NT + NT)
                sp.dma_start(y_v[bass.ds(b, 1)].rearrange("b p t d -> (b p) t d"), X[:]).then_inc(y_stored, 16)
            sp.wait_ge(y_stored, 16 * NB + 16)

        @block.scalar
        def _(act):
            for h in range(H0):
                if h >= 2:
                    act.wait_ge(wo_used, h - 1)
                act.dma_start(WO[:, h % 2], wo[:, h]).then_inc(wo_in[h % 2], 16)
                if h >= 1:
                    act.wait_ge(mw_done, h)
                    act.activation(MW[:, h - 1], pO[:, 2 + (h - 1) % 2], ACT.Copy).then_inc(mw_copied, 1)
            act.wait_ge(mw_done, H0)
            act.activation(MW[:, H0 - 1], pO[:, 2 + (H0 - 1) % 2], ACT.Copy).then_inc(mw_copied, 1)
            with act.Fori(0, NB) as b:
                for c in range(KC):
                    act.wait_ge(xt_psum, b * KC + c + 1)
                    act.activation(XT[:, c], pT[:, c % 2], ACT.Copy).then_inc(xt_ready, 1)
                act.wait_ge(shift_ready, b + 1)
                for t in range(NT):
                    ins = act.activation(EG[:, t], LG[:, t, 0:NE0], ACT.Exp, bias=NM[:, t:t + 1])
                ins.then_inc(gates_exp, 1)
                act.wait_ge(lora_psum, b + 1)
                act.activation(HT[:], pQ[:, 1], ACT.Copy).then_inc(lora_copied, 1)
                for h in range(H0):
                    act.wait_ge(q_psum, b * H0 + h + 1)
                    act.activation(RL[:, h % 2], pQ[:, 0], ACT.Relu, bias=BQ[:, h:h + 1]).then_inc(relu_ready, 1)
                    act.wait_ge(neg_ready, b * H0 + h + 1)
                    act.activation(EX[:, h % 2], NEG[:, h % 2], ACT.Exp).then_inc(exp_ready, 1)

        @block.gpsimd
        def _(pool):
            pool.wait_ge(w_in, 11 * 16)
            pool.memset(HALF[:], -0.5).then_inc(pads_set, 1)
            pool.memset(LG[:, :, NE0:TOPB], BIG).then_inc(pads_set, 1)
            pool.wait_ge(pads_set, 2)
            pool.sem_inc(y_stored, 16)
            with pool.Fori(0, NB) as b:
                pool.wait_ge(var_ready, b + 1)
                pool.tensor_tensor(RS[:], VE[:], HALF[:], ALU.pow).then_inc(rstd_ready, 1)
                for t in range(NT):
                    pool.wait_ge(xn_ready, b * NT + t + 1)
                    pool.tensor_tensor(X[:, t], X[:, t], BB[:], ALU.add).then_inc(xb_ready, 1)

        @block.vector
        def _(dve):
            dve.memset(ZB[:], 1.0).then_inc(ones_set, 1)
            dve.wait_ge(ones_set, 1)
            dve.wait_ge(pads_set, 2)
            dve.wait_ge(w_in, 11 * 16)
            for h in range(H0):
                dve.tensor_scalar(ZB[:, h], ZB[:, h], ZC[:, h:h + 1], None, ALU.mult).then_inc(zb_ready, 1)
            with dve.Fori(0, NB) as b:
                link = Chain(dve, dve_step, DVE_PER, b)
                dve.wait_ge(x_loaded, b * 16 + 16)
                for t in range(NT):
                    link(dve.bn_stats(ST[:, t], X[:, t]))
                dve.memset(HOLD[:], 0.0)
                for t in range(NT):
                    dve.bn_aggr(MV[:, t], ST[:, t]).then_inc(stats_ready, 1)
                dve.wait_ge(stats_ready, b * NT + NT)
                dve.tensor_scalar(VE[:], MV[:, :, 1], LN_EPS, None, ALU.add).then_inc(var_ready, 1)
                dve.wait_ge(rstd_ready, b + 1)
                for t in range(NT):
                    dve.tensor_scalar(XN[:, t], X[:, t], MV[:, t, 0:1], RS[:, t:t + 1], ALU.subtract,
                                      ALU.mult).then_inc(xn_ready, 1)
                dve.wait_ge(router_psum, b + 1)
                link(dve.tensor_copy(LG[:, :, 0:NE0], pQ[:, 0, 0:NT * NE0].rearrange("p (t e) -> p t e", t=NT)))
                dve.memset(HOLD[:], 0.0)
                for t in range(NT):
                    dve.max(TOP[:, t], LG[:, t]).then_inc(top_ready, 1)
                dve.wait_ge(top_ready, b * 2 * NT + NT)
                dve.tensor_scalar(NM[:], TOP[:, :, 6], -1.0, None, ALU.mult).then_inc(shift_ready, 1)
                for t in range(NT):
                    dve.match_replace(LR[:, t], TOP[:, t], LG[:, t], -BIG).then_inc(top_ready, 1)
                dve.wait_ge(top_ready, b * 2 * NT + 2 * NT)
                link(dve.tensor_tensor(EM[:], LR[:, :, 0:NE0], LG[:, :, 0:NE0], ALU.not_equal))
                dve.wait_ge(gates_exp, b + 1)
                link(dve.tensor_tensor(EM[:], EM[:], EG[:], ALU.mult))
                link(dve.tensor_reduce(CS[:], EM[:], AX_X, ALU.add))
                link(dve.reciprocal(CR[:], CS[:]))
                link(dve.tensor_scalar(CR[:], CR[:], 2.0, None, ALU.mult))
                for t in range(NT):
                    dve.tensor_scalar(CB[:, t], EM[:, t], CR[:, t:t + 1], None, ALU.mult).then_inc(comb_ready, 1)
                dve.wait_ge(comb_psum, b + 1)
                dve.tensor_copy(CT[:], pT[0:NE0, 0]).then_inc(comb_copied, 1)
                dve.wait_ge(spread_psum, b + 1)
                dve.wait_ge(lora_copied, b + 1)
                dve.tensor_tensor(HT[:], pT[:, 1], HT[:], ALU.mult).then_inc(lora_ready, 1)
                for h in range(H0):
                    dve.wait_ge(relu_ready, b * H0 + h + 1)
                    dve.tensor_scalar(NEG[:, h % 2], pQ[:, 0], BQ[:, h:h + 1], 0.0, ALU.add,
                                      ALU.min).then_inc(neg_ready, 1)
                    dve.wait_ge(exp_ready, b * H0 + h + 1)
                    dve.tensor_tensor(SG[:, h % 2], RL[:, h % 2], EX[:, h % 2], ALU.add).then_inc(sig_ready, 1)
                    dve.wait_ge(den_psum, b * H0 + h + 1)
                    dve.tensor_scalar(DN[:, h % 2], pQ[:, 1], 1e-6, None, ALU.add).then_inc(sign_ready, 1)
                    dve.wait_ge(sign_ready, (b * H0 + h) * 3 + 1)
                    dve.reciprocal(DN[:, h % 2], DN[:, h % 2]).then_inc(sign_ready, 1)
                    dve.wait_ge(sign_ready, (b * H0 + h) * 3 + 2)
                    dve.wait_ge(sig_ready, b * H0 + h + 1)
                    dve.tensor_tensor(SN[:, h % 2], SG[:, h % 2], DN[:, h % 2], ALU.mult).then_inc(sign_ready, 1)
                for t in range(NT):
                    dve.wait_ge(out_psum, b * NT + t + 1)
                    dve.wait_ge(xb_ready, b * NT + t + 1)
                    dve.tensor_tensor(X[:, t], X[:, t], pO[:, t], ALU.add).then_inc(y_ready, 1)
                link.end()

        @block.tensor
        def _(pe):
            pe.wait_ge(w_in, 11 * 16)
            for h in range(H0):
                pe.wait_ge(wo_in[h % 2], 16 * (h // 2 + 1))
                if h >= 2:
                    pe.wait_ge(mw_copied, h - 1)
                for g in range(G0):
                    ins = pe.matmul(pO[:, 2 + h % 2], MT[:, h], WO[:, h % 2, g], start=(g == 0), stop=(g == G0 - 1))
                ins.then_inc(mw_done, 1)
                pe.wait_ge(mw_done, h + 1)
                pe.sem_inc(wo_used, 1)
            pe.wait_ge(mw_copied, H0)
            pe.wait_ge(zb_ready, H0)
            with pe.Fori(0, NB) as b:
                for c in range(KC):
                    if c >= 2:
                        pe.wait_ge(xt_ready, b * KC + c - 1)
                    for t in range(NT):
                        if c == 0:
                            pe.wait_ge(xn_ready, b * NT + t + 1)
                        ins = pe.transpose(pT[:, c % 2, t * P:(t + 1) * P], XN[:, t, c * P:(c + 1) * P], ident[:])
                    ins.then_inc(xt_psum, 1)
                pe.wait_ge(xt_ready, b * KC + KC)
                for t in range(NT):
                    for c in range(KC):
                        ins = pe.matmul(pQ[:, 0, t * NE0:(t + 1) * NE0], XT[:, c, t * P:(t + 1) * P], WR[:, c],
                                        start=(c == 0), stop=(c == KC - 1))
                ins.then_inc(router_psum, 1)
                for c in range(KC):
                    ins = pe.matmul(pQ[:, 1], LA[:, c], XT[:, c], start=(c == 0), stop=(c == KC - 1))
                ins.then_inc(lora_psum, 1)
                for t in range(NT):
                    for c in range(KC):
                        pe.matmul(pO[:, t], XT[:, c, t * P:(t + 1) * P], WB[:, c], start=(c == 0), stop=False)
                pe.wait_ge(comb_ready, b * NT + NT)
                for t in range(NT):
                    ins = pe.transpose(pT[0:NE0, 0, t * P:(t + 1) * P], CB[:, t], ident[:])
                ins.then_inc(comb_psum, 1)
                pe.wait_ge(comb_copied, b + 1)
                pe.matmul(pT[:, 1], SEL[:], CT[:], start=True, stop=True).then_inc(spread_psum, 1)
                pe.wait_ge(lora_ready, b + 1)
                for t in range(NT):
                    pe.matmul(pO[:, t], HT[:, t * P:(t + 1) * P], LB[:], start=False, stop=False)

                def out_products(h):
                    pe.wait_ge(sign_ready, (b * H0 + h + 1) * 3)
                    for t in range(NT):
                        ins = pe.matmul(pO[:, t], SN[:, h % 2, t * P:(t + 1) * P], MW[:, h], start=False,
                                        stop=(h == H0 - 1))
                        if h == H0 - 1:
                            ins.then_inc(out_psum, 1)

                for h in range(H0):
                    if h >= 1:
                        pe.wait_ge(neg_ready, b * H0 + h)
                    for c in range(KC):
                        ins = pe.matmul(pQ[:, 0], WQ[:, c, h * P:(h + 1) * P], XT[:, c], start=(c == 0),
                                        stop=(c == KC - 1))
                    ins.then_inc(q_psum, 1)
                    if h >= 1:
                        out_products(h - 1)
                    pe.wait_ge(sig_ready, b * H0 + h + 1)
                    pe.matmul(pQ[:, 1], ZB[:, h], SG[:, h % 2], start=True, stop=True).then_inc(den_psum, 1)
                out_products(H0 - 1)
                pe.wait_ge(y_ready, b * NT + NT)

TOP_LAGS = 6
LAGP = S + 2


def layer1(nc, x_in, x_out, dft, cor, inv, w1, b1, a1, bl1, cf, ident_d):
    with ExitStack() as ctx:
        def sb(name, shape, dt=F32):
            return ctx.enter_context(nc.sbuf_tensor("b_" + name, shape, dt))

        def ps(name, shape, dt=F32):
            return ctx.enter_context(nc.psum_tensor("b_" + name, shape, dt))

        sem = Semaphores(ctx, nc, "b_")

        x_v = x_in.rearrange("b (t p) d -> b p t d", p=P)
        y_v = x_out.rearrange("b (t p) d -> b p t d", p=P)

        ident = sb("ident", [P, P])
        DFT = sb("DFT", [P, KC, D])
        COR = sb("COR", [P, KC, D])
        INV = sb("INV", [P, KC, D])
        W = sb("W", [P, KC, D])
        A1 = sb("A1", [P, D])
        BL = sb("BL", [P, D])
        CF = sb("CF", [P, 1])
        BB = sb("BB", [P, D])
        FX = sb("FX", [P, KC, S])
        SQ = sb("SQ", [P, KC, S])
        CO = sb("CO", [P, 2, LAGP])
        RP = sb("RP", [P, 2, LAGP])
        TOP = sb("TOP", [P, NT, 8])
        NM = sb("NM", [P, NT])
        EX = sb("EX", [P, 2, D])
        MK = sb("MK", [P, 2, D])
        WS = sb("WS", [P, NT])
        WR = sb("WR", [P, NT])
        WL = sb("WL", [P, NT, D])
        WT = sb("WT", [P, KC, S])
        FW = sb("FW", [P, KC, S])
        FA = sb("FA", [P, S])
        TM = sb("TM", [P, 2, 4, S])

        pT = ps("pT", [P, 2, S])
        pF = ps("pF", [P, 2, S])
        pO = ps("pO", [P, NT, S])
        nm = Normed(ctx, nc, "b_", ident, pT, sem)
        X = nm.x
        OH = nm.xn

        w_in = sem("w_in")
        lora_scaled = sem("lora_scaled")
        lora_psum = sem("lora_psum")
        w_ready = sem("w_ready")
        pads_set = sem("pads_set")
        fx_psum = sem("fx_psum")
        fx_ready = sem("fx_ready")
        sq_ready = sem("sq_ready")
        cor_psum = sem("cor_psum")
        cor_ready = sem("cor_ready")
        top_ready = sem("top_ready")
        shift_ready = sem("shift_ready")
        exp_ready = sem("exp_ready")
        lag_step = sem("lag_step")
        weight_ready = sem("weight_ready")
        wt_psum = sem("wt_psum")
        wt_ready = sem("wt_ready")
        fw_psum = sem("fw_psum")
        fw_ready = sem("fw_ready")
        term_ready = sem("term_ready")
        prod_ready = sem("prod_ready")
        out_psum = sem("out_psum")
        xb_ready = sem("xb_ready")
        y_ready = sem("y_ready")
        y_stored = sem("y_stored")
        LAG_STEPS = 4
        block = ctx.enter_context(nc.Block())

        @block.sync
        def _(sp):
            sp.dma_start(ident[:], ident_d).then_inc(w_in, 16)
            sp.dma_start(A1[:], a1).then_inc(w_in, 16)
            sp.dma_start(BL[:], bl1).then_inc(w_in, 16)
            sp.dma_start(CF[:], cf).then_inc(w_in, 16)
            sp.dma_start(W[:], w1).then_inc(w_in, 16)
            sp.dma_start(DFT[:], dft).then_inc(w_in, 16)
            sp.dma_start(COR[:], cor).then_inc(w_in, 16)
            sp.dma_start(INV[:], inv).then_inc(w_in, 16)
            sp.dma_start(BB[:], b1.partition_broadcast(P)).then_inc(w_in, 16)
            with sp.Fori(0, NB) as b:
                sp.wait_ge(y_stored, b * 16 + 16)
                sp.dma_start(X[:], x_v[bass.ds(b, 1)].rearrange("b p t d -> (b p) t d")).then_inc(nm.x_loaded, 16)
                sp.wait_ge(y_ready, b * NT + NT)
                sp.dma_start(y_v[bass.ds(b, 1)].rearrange("b p t d -> (b p) t d"), X[:]).then_inc(y_stored, 16)
            sp.wait_ge(y_stored, 16 * NB + 16)

        @block.scalar
        def _(act):
            with act.Fori(0, NB) as b:
                nm.scalar_part(act, b)
                for c in range(KC):
                    act.wait_ge(fx_psum, b * KC + c + 1)
                    act.activation(SQ[:, c], pF[:, c % 2], ACT.Square).then_inc(sq_ready, 1)
                    act.activation(FX[:, c], pF[:, c % 2], ACT.Copy).then_inc(fx_ready, 1)
                for t in range(NT):
                    act.wait_ge(cor_psum, b * NT + t + 1)
                    if t >= 2:
                        act.wait_ge(weight_ready, b * NT + t - 1)
                    act.activation(CO[:, t % 2, 0:D], pF[:, t % 2], ACT.Copy).then_inc(cor_ready, 1)
                    act.wait_ge(cor_ready, b * NT + t + 1)
                    act.wait_ge(shift_ready, b * NT + t + 1)
                    act.activation(EX[:, t % 2], CO[:, t % 2, 0:D], ACT.Exp, bias=NM[:, t:t + 1]).then_inc(exp_ready, 1)
                for c in range(KC):
                    act.wait_ge(wt_psum, b * KC + c + 1)
                    act.activation(WT[:, c], pT[:, c % 2], ACT.Copy).then_inc(wt_ready, 1)
                for c in range(KC):
                    act.wait_ge(fw_psum, b * KC + c + 1)
                    if c == 0:
                        act.activation(FA[:], pF[:, 0], ACT.Copy).then_inc(fw_ready, 1)
                    act.activation(FW[:, c], pF[:, c % 2], ACT.Copy).then_inc(fw_ready, 1)
                    if c == 2:
                        act.wait_ge(fw_ready, b * 7 + 4)
                        act.activation(FA[0:1, :], FW[0:1, 2], ACT.Copy).then_inc(fw_ready, 1)
                        act.wait_ge(fw_ready, b * 7 + 5)
                        act.activation(FW[0:1, 2], FW[0:1, 2], ACT.Copy, scale=0.0).then_inc(fw_ready, 1)

        @block.gpsimd
        def _(pool):
            pool.wait_ge(w_in, 9 * 16)
            pool.memset(CO[:, :, D:LAGP], BIG).then_inc(pads_set, 1)
            nm.pool_setup(pool)
            pool.sem_inc(y_stored, 16)
            with pool.Fori(0, NB) as b:
                nm.pool_part(pool, b)
                for t in range(NT):
                    pool.wait_ge(nm.xn_ready, b * NT + t + 1)
                    pool.tensor_tensor(X[:, t], X[:, t], BB[:], ALU.add).then_inc(xb_ready, 1)
                for k in range(2):
                    pool.wait_ge(term_ready, b * 8 + 4 * k + 4)
                    pool.tensor_tensor(OH[:, k], TM[:, k, 0], TM[:, k, 1], ALU.add).then_inc(prod_ready, 1)
                    pool.tensor_tensor(OH[:, k + 2], TM[:, k, 2], TM[:, k, 3], ALU.subtract).then_inc(prod_ready, 1)

        @block.vector
        def _(dve):
            dve.wait_ge(w_in, 9 * 16)
            dve.tensor_scalar(BL[:], BL[:], CF[:], 2.0, ALU.mult, ALU.mult).then_inc(lora_scaled, 1)
            for c in range(KC):
                dve.wait_ge(lora_psum, c + 1)
                dve.tensor_tensor(W[:, c], W[:, c], pO[:, c], ALU.add).then_inc(w_ready, 1)
            dve.wait_ge(pads_set, 1)
            with dve.Fori(0, NB) as b:
                nm.vector_part(dve, b)
                for t in range(NT):
                    i = t % 2
                    link = Chain(dve, lag_step, LAG_STEPS, b * NT + t)
                    dve.wait_ge(cor_ready, b * NT + t + 1)
                    dve.memset(nm.hold[:], 0.0)
                    dve.max(TOP[:, t], CO[:, i]).then_inc(top_ready, 1)
                    dve.wait_ge(top_ready, b * NT + t + 1)
                    dve.tensor_scalar(NM[:, t:t + 1], TOP[:, t, 2:3], -1.0, None, ALU.mult).then_inc(shift_ready, 1)
                    link(dve.match_replace(RP[:, i], TOP[:, t], CO[:, i], -BIG))
                    link(dve.tensor_tensor(MK[:, i], RP[:, i, 0:D], CO[:, i, 0:D], ALU.not_equal))
                    dve.wait_ge(exp_ready, b * NT + t + 1)
                    link(dve.tensor_tensor_reduce(WL[:, t], EX[:, i], MK[:, i], 1.0, 0.0, ALU.mult, ALU.add,
                                                  WS[:, t:t + 1]))
                    link(dve.reciprocal(WR[:, t:t + 1], WS[:, t:t + 1]))
                    dve.tensor_scalar(WL[:, t], WL[:, t], WR[:, t:t + 1], None, ALU.mult).then_inc(weight_ready, 1)
                    link.end()
                for k in range(2):
                    dve.wait_ge(fw_ready, b * 7 + 6 + k)
                    re, im = FW[:, k], FW[:, k + 2]
                    alt = FA[:] if k == 0 else FW[:, 1]
                    dve.tensor_tensor(TM[:, k, 0], re, FX[:, k], ALU.mult).then_inc(term_ready, 1)
                    dve.tensor_tensor(TM[:, k, 1], im, FX[:, k + 2], ALU.mult).then_inc(term_ready, 1)
                    dve.tensor_tensor(TM[:, k, 2], alt, FX[:, k + 2], ALU.mult).then_inc(term_ready, 1)
                    dve.tensor_tensor(TM[:, k, 3], im, FX[:, k], ALU.mult).then_inc(term_ready, 1)
                for t in range(NT):
                    dve.wait_ge(out_psum, b * NT + t + 1)
                    dve.wait_ge(xb_ready, b * NT + t + 1)
                    dve.tensor_tensor(X[:, t], X[:, t], pO[:, t], ALU.add).then_inc(y_ready, 1)

        @block.tensor
        def _(pe):
            pe.wait_ge(w_in, 9 * 16)
            pe.wait_ge(lora_scaled, 1)
            for c in range(KC):
                pe.matmul(pO[:, c], A1[:, c * P:(c + 1) * P], BL[:], start=True, stop=True).then_inc(lora_psum, 1)
            pe.wait_ge(w_ready, KC)
            with pe.Fori(0, NB) as b:
                nm.tensor_part(pe, b)
                pe.wait_ge(nm.xt_ready, b * KC + KC)
                for m in range(KC):
                    if m >= 2:
                        pe.wait_ge(fx_ready, b * KC + m - 1)
                    for c in range(KC):
                        ins = pe.matmul(pF[:, m % 2], DFT[:, c, m * P:(m + 1) * P], nm.xt[:, c], start=(c == 0),
                                        stop=(c == KC - 1))
                    ins.then_inc(fx_psum, 1)
                pe.wait_ge(fx_ready, b * KC + KC)
                for t in range(NT):
                    if t >= 2:
                        pe.wait_ge(cor_ready, b * NT + t - 1)
                    for c in range(KC):
                        ins = pe.matmul(pF[:, t % 2], SQ[:, c, t * P:(t + 1) * P], COR[:, c], start=(c == 0),
                                        stop=(c == KC - 1))
                    ins.then_inc(cor_psum, 1)
                    for c in range(KC):
                        pe.matmul(pO[:, t], nm.xt[:, c, t * P:(t + 1) * P], W[:, c], start=(c == 0), stop=False)
                for c in range(KC):
                    if c >= 2:
                        pe.wait_ge(wt_ready, b * KC + c - 1)
                    for t in range(NT):
                        if c == 0:
                            pe.wait_ge(weight_ready, b * NT + t + 1)
                        ins = pe.transpose(pT[:, c % 2, t * P:(t + 1) * P], WL[:, t, c * P:(c + 1) * P], ident[:])
                    ins.then_inc(wt_psum, 1)
                pe.wait_ge(wt_ready, b * KC + KC)
                for m in range(KC):
                    if m >= 2:
                        pe.wait_ge(fw_ready, b * 7 + m)
                    for c in range(KC):
                        ins = pe.matmul(pF[:, m % 2], DFT[:, c, m * P:(m + 1) * P], WT[:, c], start=(c == 0),
                                        stop=(c == KC - 1))
                    ins.then_inc(fw_psum, 1)
                pe.wait_ge(prod_ready, b * KC + KC)
                for t in range(NT):
                    for c in range(KC):
                        ins = pe.matmul(pO[:, t], OH[:, c, t * P:(t + 1) * P], INV[:, c], start=False,
                                        stop=(c == KC - 1))
                    ins.then_inc(out_psum, 1)
                pe.wait_ge(y_ready, b * NT + NT)

HD = 16
GH = 4
NG = 8
GW = GH * HD
VW = HD + 1
SW = 4 * HD
SM = 96 + 2 * GH
NCL = 64


def project(nc, tag, nk, x_in, scratch, wqkv, cos_d, sin_d, ident_d, gate=None):
    xt_d, q_d, k_d, v_d = scratch
    kw = NG * nk * HD
    kc = kw // P
    parts = [(0, D), (D, kw), (D + kw, kw)] if nk == GH else [(0, D), (D, 2 * kw)]
    with ExitStack() as ctx:
        def sb(name, shape, dt=F32):
            return ctx.enter_context(nc.sbuf_tensor(tag + name, shape, dt))

        def ps(name, shape, dt=F32):
            return ctx.enter_context(nc.psum_tensor(tag + name, shape, dt))

        sem = Semaphores(ctx, nc, tag)

        x_v = x_in.rearrange("b (t p) d -> b p t d", p=P)
        ident = sb("ident", [P, P])
        W = sb("W", [P, KC, D + 2 * kw])
        COS = sb("COS", [P, NT, HD // 2])
        SIN = sb("SIN", [P, NT, HD // 2])
        ROT = sb("ROT", [P, 2, 2, 2, D])
        QR = sb("QR", [P, NT, D + kw])
        HI = sb("HI", [P, KC + kc, S], F32R)
        LO = sb("LO", [P, KC + kc, S], F32R)
        V = sb("V", [P, NG, NT, nk, VW])
        pT = ps("pT", [P, 2, S])
        pA = ps("pA", [P, 2, 3, S])
        nm = Normed(ctx, nc, tag, ident, pT, sem)

        w_in = sem("w_in")
        ones_set = sem("ones_set")
        qkv_psum = sem("qkv_psum")
        turned = sem("turned")
        rotated = sem("rotated")
        v_ready = sem("v_ready")
        turn_psum = sem("turn_psum")
        hi_ready = sem("hi_ready")
        lo_ready = sem("lo_ready")
        stored = sem("stored")
        NST = 2 + 2 * 2 + 2 * (P // (nk * HD))
        if gate:
            cent, asg, cidx, sel_d = gate
            CE = sb("CE", [P, KC, NCL])
            CM = sb("CM", [P, NT])
            CN = sb("CN", [P, NT])
            CX = sb("CX", [P, NT, NCL])
            CS = sb("CS", [P, NT])
            CR = sb("CR", [P, NT])
            CP = sb("CP", [P, NCL])
            CT = sb("CT", [NCL, 2])
            AI = sb("AI", [NCL, D], I32)
            AF = sb("AF", [NCL, D])
            CI = sb("CI", [NCL, 1])
            SR = sb("SR", [1, D])
            logit_psum = sem("logit_psum")
            cmax_ready = sem("cmax_ready")
            cshift_ready = sem("cshift_ready")
            cexp_ready = sem("cexp_ready")
            crec_ready = sem("crec_ready")
            chit_ready = sem("chit_ready")
            best_psum = sem("best_psum")
            hit_ready = sem("hit_ready")
            asg_ready = sem("asg_ready")
            sel_psum = sem("sel_psum")
            sel_ready = sem("sel_ready")
            sel_stored = sem("sel_stored")
        NW = 4 + (3 if gate else 0)
        block = ctx.enter_context(nc.Block())

        @block.sync
        def _(sp):
            sp.dma_start(ident[:], ident_d).then_inc(w_in, 16)
            sp.dma_start(COS[:], cos_d).then_inc(w_in, 16)
            sp.dma_start(SIN[:], sin_d).then_inc(w_in, 16)
            sp.dma_start(W[:], wqkv).then_inc(w_in, 16)
            if gate:
                sp.dma_start(CE[:], cent).then_inc(w_in, 16)
                sp.dma_start(AI[:], asg.partition_broadcast(NCL)).then_inc(w_in, 16)
                sp.dma_start(CI[:], cidx).then_inc(w_in, 16)
            sp.sem_inc(stored, 16)
            with sp.Fori(0, NB) as b:
                one = bass.ds(b, 1)
                sp.wait_ge(stored, b * 16 * NST + 16)
                sp.dma_start(nm.x[:], x_v[one].rearrange("b p t d -> (b p) t d")).then_inc(nm.x_loaded, 16)
                sp.wait_ge(nm.xt_ready, b * KC + KC)
                sp.dma_start(xt_d[one].rearrange("b p c n -> (b p) c n"), nm.xt[:]).then_inc(stored, 16)
                sp.wait_ge(v_ready, b * NT + NT)
                sp.dma_start(v_d[one].rearrange("b g p m -> (b p) g m"),
                             V[:].rearrange("p g t j d -> p g (t j d)")).then_inc(stored, 16)
                sp.wait_ge(lo_ready, b * (KC + kc) + KC)
                for half in range(2):
                    rows = slice(half * GW, (half + 1) * GW)
                    for part, buf in ((0, HI), (1, LO)):
                        sp.dma_start(q_d[one, :, half, part].rearrange("b c f n -> (b f) c n"),
                                     buf[rows, 0:KC].bitcast(F32)).then_inc(stored, 16)
                sp.wait_ge(lo_ready, b * (KC + kc) + KC + kc)
                for g in range(P // (nk * HD)):
                    rows = slice(g * nk * HD, (g + 1) * nk * HD)
                    for part, buf in ((0, HI), (1, LO)):
                        sp.dma_start(k_d[one, :, g, part].rearrange("b c f n -> (b f) c n"),
                                     buf[rows, KC:KC + kc].bitcast(F32)).then_inc(stored, 16)
            sp.wait_ge(stored, 16 * NST * NB + 16)
            if gate:
                sp.wait_ge(sel_ready, 1)
                sp.dma_start(sel_d.rearrange("(a d) -> a d", a=1), SR[:]).then_inc(sel_stored, 16)
                sp.wait_ge(sel_stored, 16)

        @block.scalar
        def _(act):
            act.wait_ge(ones_set, 1)
            with act.Fori(0, NB) as b:
                nm.scalar_part(act, b)
                for t in range(NT):
                    act.wait_ge(turned, (b * NT + t) * 4 + 4)
                    act.wait_ge(qkv_psum, (b * NT + t + 1) * len(parts))
                    src = pA[:, t % 2, 2, 0:kw] if nk == GH else pA[:, t % 2, 1, kw:2 * kw]
                    act.activation(V[:, :, t, :, 0:HD], src.rearrange("p (g j d) -> p g j d", g=NG, j=nk),
                                   ACT.Copy).then_inc(v_ready, 1)
                    if gate:
                        act.wait_ge(cshift_ready, b * NT + t + 1)
                        act.activation(CX[:, t], pA[:, t % 2, 2, 0:NCL], ACT.Exp, bias=CN[:, t:t + 1], scale=10.0,
                                       accum_out=CS[:, t:t + 1]).then_inc(cexp_ready, 1)
                for c in range(KC + kc):
                    act.wait_ge(turn_psum, b * (KC + kc) + c + 1)
                    act.activation(HI[:, c], pT[:, c % 2], ACT.Copy).then_inc(hi_ready, 1)

        @block.gpsimd
        def _(pool):
            pool.wait_ge(w_in, NW * 16)
            pool.memset(V[:], 1.0).then_inc(ones_set, 1)
            nm.pool_setup(pool)
            with pool.Fori(0, NB) as b:
                nm.pool_part(pool, b)
                for t in range(NT):
                    for u, (at, width) in enumerate(((0, D), (D, kw))):
                        pool.wait_ge(turned, (b * NT + t) * 4 + 2 * u + 2)
                        h = width // NG // 2
                        c_, s_ = (ROT[:, t % 2, u, w, 0:width].rearrange("p (g a m) -> p g a m", g=NG, a=2)
                                  for w in (0, 1))
                        o_ = QR[:, t, at:at + width].rearrange("p (g a m) -> p g a m", g=NG, a=2)
                        pool.tensor_tensor(o_[:, :, 0], c_[:, :, 0], s_[:, :, 1], ALU.subtract).then_inc(rotated, 1)
                        pool.tensor_tensor(o_[:, :, 1], c_[:, :, 1], s_[:, :, 0], ALU.add).then_inc(rotated, 1)

        @block.vector
        def _(dve):
            dve.wait_ge(w_in, NW * 16)
            if gate:
                dve.memset(CP[:], 0.0).then_inc(chit_ready, 1)
            with dve.Fori(0, NB) as b:
                nm.vector_part(dve, b)
                for t in range(NT):
                    for u, width in enumerate((D, kw)):
                        dve.wait_ge(qkv_psum, (b * NT + t) * len(parts) + u + 1)
                        if t >= 2:
                            dve.wait_ge(rotated, (b * NT + t - 2) * 4 + 2 * u + 2)
                        src = pA[:, t % 2, u, 0:width].rearrange("p (m i j) -> p m i j", m=2 * NG, i=HD // 2)
                        for w, table in enumerate((COS, SIN)):
                            tab = table[:, t].unsqueeze(1).unsqueeze(3).to_broadcast(list(src.shape))
                            dve.tensor_tensor(
                                ROT[:, t % 2, u, w, 0:width].rearrange("p (m i j) -> p m i j", m=2 * NG, i=HD // 2),
                                src, tab, ALU.mult).then_inc(turned, 1)
                    if gate:
                        dve.wait_ge(logit_psum, b * NT + t + 1)
                        dve.tensor_reduce(CM[:, t:t + 1], pA[:, t % 2, 2, 0:NCL], AX_X, ALU.max).then_inc(cmax_ready, 1)
                        dve.wait_ge(cmax_ready, b * NT + t + 1)
                        dve.tensor_scalar(CN[:, t:t + 1], CM[:, t:t + 1], -10.0, None,
                                          ALU.mult).then_inc(cshift_ready, 1)
                if gate:
                    dve.wait_ge(cexp_ready, b * NT + NT)
                    dve.reciprocal(CR[:], CS[:]).then_inc(crec_ready, 1)
                    dve.wait_ge(crec_ready, b + 1)
                    for t in range(NT):
                        dve.wait_ge(chit_ready, b * NT + t + 1)
                        dve.scalar_tensor_tensor(CP[:], CX[:, t], CR[:, t:t + 1], CP[:], ALU.mult,
                                                 ALU.max).then_inc(chit_ready, 1)
                for c in range(KC + kc):
                    dve.wait_ge(hi_ready, b * (KC + kc) + c + 1)
                    dve.tensor_tensor(LO[:, c], pT[:, c % 2], HI[:, c].bitcast(F32), ALU.subtract).then_inc(lo_ready, 1)
            if gate:
                dve.wait_ge(best_psum, 1)
                dve.tensor_reduce(CT[:, 0:1], pT[0:NCL, 0, 0:P], AX_X, ALU.max).then_inc(hit_ready, 1)
                dve.wait_ge(hit_ready, 1)
                dve.tensor_scalar(CT[:, 1:2], CT[:, 0:1], 0.01, None, ALU.is_gt).then_inc(hit_ready, 1)
                dve.tensor_copy(AF[:], AI[:]).then_inc(asg_ready, 1)
                dve.wait_ge(asg_ready, 1)
                dve.tensor_scalar(AF[:], AF[:], CI[:], None, ALU.is_equal).then_inc(asg_ready, 1)
                dve.wait_ge(sel_psum, 1)
                dve.tensor_copy(SR[:], pT[0:1, 1]).then_inc(sel_ready, 1)

        @block.tensor
        def _(pe):
            pe.wait_ge(w_in, NW * 16)
            with pe.Fori(0, NB) as b:
                nm.tensor_part(pe, b)
                pe.wait_ge(nm.xt_ready, b * KC + KC)
                for t in range(NT):
                    if t >= 2:
                        pe.wait_ge(v_ready, b * NT + t - 1)
                        if gate:
                            pe.wait_ge(cexp_ready, b * NT + t - 1)
                    for n, (at, width) in enumerate(parts):
                        for c in range(KC):
                            ins = pe.matmul(pA[:, t % 2, n, 0:width], nm.xt[:, c, t * P:(t + 1) * P],
                                            W[:, c, at:at + width], start=(c == 0), stop=(c == KC - 1))
                        ins.then_inc(qkv_psum, 1)
                    if gate:
                        for c in range(KC):
                            ins = pe.matmul(pA[:, t % 2, 2, 0:NCL], nm.xt[:, c, t * P:(t + 1) * P], CE[:, c],
                                            start=(c == 0), stop=(c == KC - 1))
                        ins.then_inc(logit_psum, 1)
                for c in range(KC + kc):
                    if c >= 2:
                        pe.wait_ge(lo_ready, b * (KC + kc) + c - 1)
                    for t in range(NT):
                        if c == 0:
                            pe.wait_ge(rotated, (b * NT + t) * 4 + 4)
                        ins = pe.transpose(pT[:, c % 2, t * P:(t + 1) * P], QR[:, t, c * P:(c + 1) * P], ident[:])
                    ins.then_inc(turn_psum, 1)
                pe.wait_ge(lo_ready, (b + 1) * (KC + kc))
                if gate:
                    pe.wait_ge(cexp_ready, b * NT + NT)
            if gate:
                pe.wait_ge(chit_ready, 1 + NB * NT)
                pe.transpose(pT[0:NCL, 0, 0:P], CP[:], ident[:]).then_inc(best_psum, 1)
                pe.wait_ge(hit_ready, 2)
                pe.wait_ge(asg_ready, 2)
                pe.matmul(pT[0:1, 1], CT[:, 1:2], AF[:], start=True, stop=True).then_inc(sel_psum, 1)


def attend(nc, tag, nk, scratch, o_d, mask_q, mask_k, pick_d, ident_d):
    _, q_d, k_d, v_d = scratch
    NGR = NB * NG
    NBUF = 4
    OFF = [0, S, 2 * S - P, 3 * S - 3 * P]
    PTW = 4 * S - 6 * P
    with ExitStack() as ctx:
        def sb(name, shape, dt=F32):
            return ctx.enter_context(nc.sbuf_tensor(tag + name, shape, dt))

        def ps(name, shape, dt=F32):
            return ctx.enter_context(nc.psum_tensor(tag + name, shape, dt))

        sem = Semaphores(ctx, nc, tag)

        ident = sb("ident", [P, P])
        identb = sb("identb", [P, P], BF16)
        MF = sb("MF", [P, 2, P])
        MB = sb("MB", [P, 2, P], BF16)
        PICK = sb("PICK", [SM, GH * S])
        QS = [sb(f"QS{i}", [SM, GH, S], F32R) for i in range(NBUF)]
        KS = [sb(f"KS{i}", [SM, GH, S], F32R) for i in range(NBUF)]
        V = [sb(f"V{i}", [P, NT, nk, VW]) for i in range(2)]
        PT = [sb(f"PT{i}", [P, GH, PTW]) for i in range(2)]
        MX = sb("MX", [P, NT, GH])
        MN = sb("MN", [P, NT, 2 * GH], F32R)
        MR = [sb(f"MR{i}", [2 * GH, S], F32R) for i in range(2)]
        OV = sb("OV", [P, S])
        RC = sb("RC", [P, NT * GH])
        AO = [sb(f"AO{i}", [P, NT, GH, HD]) for i in range(2)]
        pS = ps("pS", [P, 2, 2, S])
        pX = ps("pX", [P, 2, S])
        pM = ps("pM", [P, S])
        pV = ps("pV", [P, S])

        c_in = sem("c_in")
        cast = sem("cast")
        ones_set = sem("ones_set")
        loaded = [sem(f"loaded{i}") for i in range(NBUF)]
        v_loaded = [sem("v_loaded_even"), sem("v_loaded_odd")]
        m_loaded = [sem("m_loaded_even"), sem("m_loaded_odd")]
        top_psum = sem("top_psum")
        top_ready = sem("top_ready")
        m_high = sem("m_high")
        m_split = sem("m_split")
        m_psum = sem("m_psum")
        m_ready = sem("m_ready")
        score_psum = sem("score_psum")
        exp_ready = sem("exp_ready")
        pv_done = sem("pv_done")
        ov_ready = sem("ov_ready")
        o_psum = sem("o_psum")
        rec_ready = sem("rec_ready")
        out_ready = sem("out_ready")
        o_stored = [sem("o_stored_even"), sem("o_stored_odd")]
        UNITS = 2 * NT
        TOPS = NT * GH
        AHEAD = GH
        NL = 6
        SCALE = HD ** -0.5

        block = ctx.enter_context(nc.Block())
        q_g = q_d.rearrange("b c h s (r j) n -> (b c h) (s r) (j n)", j=GH)
        k_g = k_d.rearrange("b c h s (r j) n -> (b c h) s r j n", j=nk)
        v_g = v_d.rearrange("b g p m -> (b g) p m")
        o_g = o_d.rearrange("b p t g m -> b g p t m")

        def pick(view, index):
            return view[bass.ds(index, 1)].rearrange("g p n -> (g p) n")

        def load_stacks(sp, i, G):
            for dup in range(2):
                sp.dma_start(QS[i][dup * 2 * HD:(dup + 1) * 2 * HD].bitcast(F32).rearrange("p j n -> p (j n)"),
                             pick(q_g, G)).then_inc(loaded[i], 16)
            for s in range(2):
                for dup in range(2):
                    at = (2 * s + dup) * HD
                    src = k_g[bass.ds(G, 1), s].rearrange("g r j n -> (g r) j n")
                    sp.dma_start(KS[i][at:at + HD].bitcast(F32),
                                 src.to_broadcast([HD, GH, S])).then_inc(loaded[i], 16)

        def load_v(sp, i, G):
            sp.dma_start(V[i][:].rearrange("p t j d -> p (t j d)"), pick(v_g, G)).then_inc(v_loaded[i], 16)

        def top_place(u):
            return NT - 1 - u // GH, u % GH


        @block.sync
        def _(sp):
            sp.dma_start(ident[:], ident_d).then_inc(c_in, 16)
            sp.dma_start(MF[:, 0], mask_q).then_inc(c_in, 16)
            sp.dma_start(MF[:, 1], mask_k).then_inc(c_in, 16)
            sp.dma_start(PICK[SW:SM], pick_d).then_inc(c_in, 16)
            for i in range(NBUF):
                load_stacks(sp, i, i)
            for i in range(2):
                load_v(sp, i, i)
                sp.sem_inc(o_stored[i], 16)
            with sp.Fori(0, NGR // NBUF) as r:
                n0 = NBUF * r
                next_s = [sp.snap((n0 + i + NBUF) % NGR) for i in range(NBUF)]
                next_v = [sp.snap((n0 + i + 2) % NGR) for i in range(NBUF)]
                place = [(sp.snap((n0 + i) // NG), sp.snap((n0 + i) % NG)) for i in range(NBUF)]
                for i in range(NBUF):
                    n = n0 + i
                    sp.wait_ge(score_psum, (n + 1) * UNITS)
                    load_stacks(sp, i, next_s[i])
                    sp.wait_ge(pv_done, n + 3)
                    load_v(sp, i % 2, next_v[i])
                    sp.wait_ge(out_ready, n + 2)
                    sp.dma_start(o_g[bass.ds(place[i][0], 1), bass.ds(place[i][1], 1)].rearrange("b g p t m -> (b g p) t m"),
                                 AO[i % 2][:].rearrange("p t j d -> p t (j d)")).then_inc(o_stored[i % 2], 16)
            for i in range(NBUF):
                sp.wait_ge(loaded[i], 16 * NL * (NGR // NBUF + 1))
            for i in range(2):
                sp.wait_ge(o_stored[i], 16 * (NGR // 2 + 1))
                sp.wait_ge(v_loaded[i], 16 * (NGR // 2 + 1))

        @block.scalar
        def _(act):
            act.sem_inc(exp_ready, 2)

            def maxima(i, n):
                act.wait_ge(m_psum, n + 1)
                act.activation(MR[i % 2][:], pM[0:2 * GH], ACT.Copy).then_inc(m_ready, 1)
                act.wait_ge(m_ready, n + 1)
                act.dma_start(QS[i][SM - 2 * GH:SM].bitcast(F32),
                              MR[i % 2][:].bitcast(F32).unsqueeze(1).to_broadcast([2 * GH, GH, S])
                              ).then_inc(m_loaded[i % 2], 16)

            maxima(0, 0)
            with act.Fori(0, NGR // NBUF) as r:
                for i in range(NBUF):
                    n = NBUF * r + i
                    act.wait_ge(pv_done, n + 1)
                    for u in range(UNITS):
                        j, hp = u // 2, u % 2
                        N = S - j * P
                        act.wait_ge(score_psum, n * UNITS + u + 1)
                        act.activation(PT[i % 2][:, 2 * hp:2 * hp + 2, OFF[j]:OFF[j] + N], pS[:, u % 2, :, 0:N],
                                       ACT.Exp, scale=SCALE).then_inc(exp_ready, 1)
                    maxima((i + 1) % NBUF, n + 1)
                    act.wait_ge(pv_done, n + 3)
                    act.activation(OV[:], pV[:], ACT.Copy).then_inc(ov_ready, 1)
            act.wait_ge(m_loaded[0], 16 * (NGR // 2 + 1))
            act.wait_ge(m_loaded[1], 16 * (NGR // 2))

        @block.vector
        def _(dve):
            dve.memset(pV[:], 0.0).then_inc(ones_set, 1)
            dve.wait_ge(c_in, 64)
            dve.tensor_copy(identb[:], ident[:]).then_inc(cast, 1)
            dve.tensor_copy(MB[:], MF[:]).then_inc(cast, 1)
            for i in range(NBUF):
                dve.tensor_copy(QS[i][SW:SM - 2 * GH].rearrange("p j n -> p (j n)"),
                                PICK[SW:SM - 2 * GH]).then_inc(ones_set, 1)
                dve.tensor_copy(KS[i][SW:SM].rearrange("p j n -> p (j n)"), PICK[SW:SM]).then_inc(ones_set, 1)
            dve.sem_inc(top_ready, 2)
            dve.sem_inc(out_ready, 1)

            def maxima(n, units):
                for u in units:
                    t, h = top_place(u)
                    dve.wait_ge(top_psum, n * TOPS + u + 1)
                    dve.tensor_reduce(MX[:, t, h:h + 1], pX[:, u % 2, 0:(t + 1) * P], AX_X,
                                      ALU.max).then_inc(top_ready, 1)

            def split(n):
                dve.wait_ge(top_ready, (n + 1) * TOPS + 2)
                dve.tensor_scalar(MN[:, :, 0:GH], MX[:], -1.0, None, ALU.mult).then_inc(m_high, 1)
                dve.wait_ge(m_high, n + 1)
                dve.scalar_tensor_tensor(MN[:, :, GH:2 * GH], MX[:], -1.0, MN[:, :, 0:GH].bitcast(F32), ALU.mult,
                                         ALU.subtract).then_inc(m_split, 1)

            maxima(0, range(TOPS))
            split(0)
            maxima(1, range(AHEAD))
            with dve.Fori(0, NGR // NBUF) as r:
                for i in range(NBUF):
                    n = NBUF * r + i
                    maxima(n + 1, range(AHEAD, TOPS))
                    split(n + 1)
                    maxima(n + 2, range(AHEAD))
                    dve.wait_ge(o_psum, n + 1)
                    sums = pM[:].rearrange("p (m d) -> p m d", d=2 * HD)
                    dve.reciprocal(RC[:], sums[:, :, HD]).then_inc(rec_ready, 1)
                    dve.wait_ge(rec_ready, n + 1)
                    dve.wait_ge(o_stored[i % 2], 16 * (2 * r + i // 2 + 1))
                    dve.tensor_tensor(AO[i % 2][:].rearrange("p t j d -> p (t j) d"), sums[:, :, 0:HD],
                                      RC[:].unsqueeze(2).to_broadcast([P, NT * GH, HD]),
                                      ALU.mult).then_inc(out_ready, 1)

        @block.tensor
        def _(pe):
            pe.sem_inc(pv_done, 2)
            pe.wait_ge(cast, 2)
            pe.wait_ge(c_in, 64)
            pe.wait_ge(ones_set, 2 * NBUF + 1)

            def tops(i, n, units):
                for u in units:
                    t, h = top_place(u)
                    N = (t + 1) * P
                    pe.wait_ge(top_ready, n * TOPS + u + 1)
                    pe.matmul(pX[:, u % 2, 0:N], QS[i][0:SM - 2 * GH, h, t * P:N], KS[i][0:SM - 2 * GH, h, 0:N],
                              start=True, stop=False)
                    pe.matmul(pX[:, u % 2, t * P:N], identb[:], MB[:, 0], start=False, stop=True).then_inc(top_psum, 1)

            def score_unit(i, n, u):
                j, hp = u // 2, u % 2
                N = S - j * P
                pe.wait_ge(exp_ready, n * UNITS + u + 1)
                for e in range(2):
                    h = 2 * hp + e
                    pe.matmul(pS[:, u % 2, e, 0:N], KS[i][:, h, j * P:(j + 1) * P],
                              QS[i][:, h, j * P:S], start=True, stop=False)
                    ins = pe.matmul(pS[:, u % 2, e, 0:P], identb[:], MB[:, 1], start=False, stop=True)
                ins.then_inc(score_psum, 1)

            def turn_maxima(n):
                pe.wait_ge(m_split, n + 1)
                for t in range(NT):
                    ins = pe.transpose(pM[0:2 * GH, t * P:(t + 1) * P], MN[:, t].bitcast(F32), ident[:])
                ins.then_inc(m_psum, 1)

            def values(i, j):
                for h in range(GH):
                    at = 2 * HD * h
                    ins = pe.matmul(pV[at:at + VW, j * P:S], V[i % 2][:, j, h if nk == GH else 0],
                                    PT[i % 2][:, h, OFF[j]:OFF[j] + S - j * P], start=(j == 0), stop=(j == NT - 1))
                return ins

            pe.wait_ge(loaded[0], 16 * NL)
            tops(0, 0, range(TOPS))
            turn_maxima(0)
            pe.wait_ge(loaded[1], 16 * NL)
            tops(1, 1, range(AHEAD))
            with pe.Fori(0, NGR // NBUF) as r:
                for i in range(NBUF):
                    n = NBUF * r + i
                    i1, i2 = (i + 1) % NBUF, (i + 2) % NBUF
                    pe.wait_ge(m_loaded[i % 2], 16 * (2 * r + i // 2 + 1))
                    for u in range(UNITS):
                        score_unit(i, n, u)
                        tops(i1, n + 1, range(AHEAD + 2 * u, min(AHEAD + 2 * u + 2, TOPS)))
                    pe.wait_ge(v_loaded[i % 2], 16 * (2 * r + i // 2 + 1))
                    for j in range(2):
                        pe.wait_ge(exp_ready, n * UNITS + 2 * j + 4)
                        values(i, j)
                    pe.wait_ge(out_ready, n + 1)
                    turn_maxima(n + 1)
                    pe.wait_ge(exp_ready, (n + 1) * UNITS + 2)
                    values(i, 2)
                    values(i, 3).then_inc(pv_done, 1)
                    pe.wait_ge(loaded[i2], 16 * NL * (r + 1 + (i + 2) // NBUF))
                    tops(i2, n + 2, range(AHEAD))
                    pe.wait_ge(ov_ready, n + 1)
                    for t in range(NT):
                        ins = pe.transpose(pM[:, t * P:(t + 1) * P], OV[:, t * P:(t + 1) * P], ident[:])
                    ins.then_inc(o_psum, 1)


def finish2(nc, x_in, x_out, xt_d, o_d, sel_d, wo, w2, b2, ident_d):
    with ExitStack() as ctx:
        def sb(name, shape, dt=F32):
            return ctx.enter_context(nc.sbuf_tensor("e_" + name, shape, dt))

        def ps(name, shape, dt=F32):
            return ctx.enter_context(nc.psum_tensor("e_" + name, shape, dt))

        sem = Semaphores(ctx, nc, "e_")

        x_v = x_in.rearrange("b (t p) d -> b p t d", p=P)
        y_v = x_out.rearrange("b (t p) d -> b p t d", p=P)
        ident = sb("ident", [P, P])
        WO = sb("WO", [P, KC, D])
        W = sb("W", [P, KC, D])
        BB = sb("BB", [P, D])
        SB = sb("SB", [P, D])
        X = sb("X", [P, 2, NT, D])
        XT = [sb(f"XT{i}", [P, KC, S]) for i in range(2)]
        O = [sb(f"O{i}", [P, NT, D]) for i in range(2)]
        OT = sb("OT", [P, KC, S])
        pT = ps("pT", [P, 2, S])
        pO = ps("pO", [P, NT, S])
        w_in = sem("w_in")
        w_ready = sem("w_ready")
        loaded = [sem("loaded_even"), sem("loaded_odd")]
        ot_psum = sem("ot_psum")
        ot_ready = sem("ot_ready")
        out_psum = sem("out_psum")
        xb_ready = sem("xb_ready")
        y_ready = sem("y_ready")
        y_stored = [sem("y_stored_even"), sem("y_stored_odd")]
        block = ctx.enter_context(nc.Block())

        @block.sync
        def _(sp):
            sp.dma_start(ident[:], ident_d).then_inc(w_in, 16)
            sp.dma_start(BB[:], b2.partition_broadcast(P)).then_inc(w_in, 16)
            sp.dma_start(SB[:], sel_d.partition_broadcast(P)).then_inc(w_in, 16)
            sp.dma_start(W[:], w2).then_inc(w_in, 16)
            sp.dma_start(WO[:], wo).then_inc(w_in, 16)
            for i in range(2):
                sp.sem_inc(y_stored[i], 16)
            with sp.Fori(0, NB // 2) as r:
                for i in range(2):
                    one = bass.ds(2 * r + i, 1)
                    sp.wait_ge(y_stored[i], 16 * (r + 1))
                    sp.dma_start(O[i][:], o_d[one].rearrange("b p t g m -> (b p) t (g m)")).then_inc(loaded[i], 16)
                    sp.dma_start(XT[i][:], xt_d[one].rearrange("b p c n -> (b p) c n")).then_inc(loaded[i], 16)
                    sp.dma_start(X[:, i], x_v[one].rearrange("b p t d -> (b p) t d")).then_inc(loaded[i], 16)

        @block.scalar
        def _(act):
            with act.Fori(0, NB // 2) as r:
                for i in range(2):
                    n = 2 * r + i
                    for c in range(KC):
                        act.wait_ge(ot_psum, n * KC + c + 1)
                        act.activation(OT[:, c], pT[:, c % 2], ACT.Copy).then_inc(ot_ready, 1)
                    act.wait_ge(y_ready, n * NT + NT)
                    act.dma_start(y_v[bass.ds(n, 1)].rearrange("b p t d -> (b p) t d"),
                                  X[:, i]).then_inc(y_stored[i], 16)
            for i in range(2):
                act.wait_ge(y_stored[i], 16 * (NB // 2 + 1))

        @block.gpsimd
        def _(pool):
            pool.wait_ge(w_ready, KC + 1)
            with pool.Fori(0, NB // 2) as r:
                for i in range(2):
                    pool.wait_ge(loaded[i], 48 * (r + 1))
                    for t in range(NT):
                        pool.tensor_tensor(X[:, i, t], X[:, i, t], BB[:], ALU.add).then_inc(xb_ready, 1)

        @block.vector
        def _(dve):
            dve.wait_ge(w_in, 80)
            for c in range(KC):
                dve.tensor_tensor(W[:, c], W[:, c], SB[:], ALU.mult).then_inc(w_ready, 1)
            dve.tensor_tensor(BB[:], BB[:], SB[:], ALU.mult).then_inc(w_ready, 1)
            with dve.Fori(0, NB // 2) as r:
                for i in range(2):
                    n = 2 * r + i
                    for t in range(NT):
                        dve.wait_ge(out_psum, n * NT + t + 1)
                        dve.wait_ge(xb_ready, n * NT + t + 1)
                        dve.tensor_tensor(X[:, i, t], X[:, i, t], pO[:, t], ALU.add).then_inc(y_ready, 1)

        @block.tensor
        def _(pe):
            pe.wait_ge(w_ready, KC + 1)
            pe.wait_ge(w_in, 80)
            with pe.Fori(0, NB // 2) as r:
                for i in range(2):
                    n = 2 * r + i
                    pe.wait_ge(loaded[i], 48 * (r + 1))
                    for c in range(KC):
                        if c >= 2:
                            pe.wait_ge(ot_ready, n * KC + c - 1)
                        for t in range(NT):
                            ins = pe.transpose(pT[:, c % 2, t * P:(t + 1) * P], O[i][:, t, c * P:(c + 1) * P], ident[:])
                        ins.then_inc(ot_psum, 1)
                    for t in range(NT):
                        for c in range(KC):
                            pe.matmul(pO[:, t], XT[i][:, c, t * P:(t + 1) * P], W[:, c], start=(c == 0), stop=False)
                    pe.wait_ge(ot_ready, n * KC + KC)
                    for t in range(NT):
                        for c in range(KC):
                            ins = pe.matmul(pO[:, t], OT[:, c, t * P:(t + 1) * P], WO[:, c], start=False,
                                            stop=(c == KC - 1))
                        ins.then_inc(out_psum, 1)
                    pe.wait_ge(y_ready, n * NT + NT)


def layer2(nc, x_in, x_out, wqkv, cos_d, sin_d, cent, asg, cidx, wo, w2, b2, mask_q, mask_k, pick_d, ident_d, nk=1):
    kw = NG * nk * HD
    xt_d = nc.dram_tensor("c_xt", (NB, P, KC, S), F32).ap()
    q_d = nc.dram_tensor("c_q", (NB, KC, 2, 2, GW, S), F32).ap()
    k_d = nc.dram_tensor("c_k", (NB, kw // P, P // (nk * HD), 2, nk * HD, S), F32).ap()
    v_d = nc.dram_tensor("c_v", (NB, NG, P, NT * nk * VW), F32).ap()
    o_d = nc.dram_tensor("c_o", (NB, P, NT, NG, GW), F32).ap()
    sel_d = nc.dram_tensor("c_sel", (D,), F32).ap()
    scratch = (xt_d, q_d, k_d, v_d)
    project(nc, "c_", nk, x_in, scratch, wqkv, cos_d, sin_d, ident_d, gate=(cent, asg, cidx, sel_d))
    attend(nc, "d_", nk, scratch, o_d, mask_q, mask_k, pick_d, ident_d)
    finish2(nc, x_in, x_out, xt_d, o_d, sel_d, wo, w2, b2, ident_d)

NE3 = 16
NX = NE3 + 2
NGE, EG3 = 4, 4
WE = 2 * D + D + 2


def moe(nc, x_in, x_out, xt_d, o_d, wo, wr, rb, rbias, we, eb3, ident_d):
    with ExitStack() as ctx:
        def sb(name, shape, dt=F32):
            return ctx.enter_context(nc.sbuf_tensor("h_" + name, shape, dt))

        def ps(name, shape, dt=F32):
            return ctx.enter_context(nc.psum_tensor("h_" + name, shape, dt))

        sem = Semaphores(ctx, nc, "h_")

        x_v = x_in.rearrange("b (t p) d -> b p t d", p=P)
        y_v = x_out.rearrange("b (t p) d -> b p t d", p=P)
        ident = sb("ident", [P, P])
        WO = sb("WO", [P, KC, D])
        WR = sb("WR", [P, KC, NE3])
        RB = sb("RB", [P, NE3])
        RBIAS = sb("RBIAS", [P, NE3])
        EB3 = sb("EB3", [NX, D])
        WX = [sb(f"WX{i}", [P, WE]) for i in range(2)]
        X = sb("X", [P, NT, D])
        XT = sb("XT", [P, KC, S])
        O = sb("O", [P, NT, D])
        OT = sb("OT", [P, KC, S])
        LG = sb("LG", [P, NT, NE3])
        MX = sb("MX", [P, NT])
        EX = sb("EX", [P, NT, NE3])
        SM3 = sb("SM3", [P, NT])
        RC = sb("RC", [P, NT])
        SC = sb("SC", [P, NT, NE3])
        GM = sb("GM", [P, NT, NGE + 6])
        GR = sb("GR", [P, NT, NGE + 6])
        TG = sb("TG", [P, NT, 8])
        PEN = sb("PEN", [P, NT, NGE])
        MS = sb("MS", [P, NT, NE3 + 6])
        MRP = sb("MRP", [P, NT, NE3 + 6])
        TE = sb("TE", [P, NT, 8])
        GT = sb("GT", [P, NT, NX])
        GTT = sb("GTT", [NX, S])
        A = sb("A", [P, 2, S])
        H = sb("H", [P, 2, S])
        HOLD = sb("HOLD", [P, 1])
        pH = ps("pH", [P, 2, 2, S])
        pY = ps("pY", [P, NT, S])

        w_in = sem("w_in")
        pads_set = sem("pads_set")
        we_loaded = [sem("we_loaded_even"), sem("we_loaded_odd")]
        x_loaded = sem("x_loaded")
        y_stored = sem("y_stored")
        logit_psum = sem("logit_psum")
        route_step = sem("route_step")
        shift_ready = sem("shift_ready")
        exp_ready = sem("exp_ready")
        gmax_ready = sem("gmax_ready")
        masked_ready = sem("masked_ready")
        gate_ready = sem("gate_ready")
        ot_psum = sem("ot_psum")
        ot_ready = sem("ot_ready")
        gt_psum = sem("gt_psum")
        gt_ready = sem("gt_ready")
        base_psum = sem("base_psum")
        h_psum = sem("h_psum")
        act_ready = sem("act_ready")
        h_ready = sem("h_ready")
        y_psum = sem("y_psum")
        y_added = sem("y_added")
        ROUTE = 10
        block = ctx.enter_context(nc.Block())

        @block.sync
        def _(sp):
            sp.dma_start(ident[:], ident_d).then_inc(w_in, 16)
            sp.dma_start(RB[:], rb.partition_broadcast(P)).then_inc(w_in, 16)
            sp.dma_start(RBIAS[:], rbias.partition_broadcast(P)).then_inc(w_in, 16)
            sp.dma_start(EB3[:], eb3).then_inc(w_in, 16)
            sp.dma_start(WR[:], wr).then_inc(w_in, 16)
            sp.dma_start(WO[:], wo).then_inc(w_in, 16)
            with sp.Fori(0, NB) as b:
                with sp.Fori(0, NX // 2) as r:
                    for i in range(2):
                        sp.wait_ge(y_psum, (b * NX + 2 * r + i + 1) * NT)
                        sp.dma_start(WX[i][:], we[bass.ds(2 * r + i, 1)].rearrange("e p m -> (e p) m")
                                     ).then_inc(we_loaded[i], 16)
            for i in range(2):
                sp.wait_ge(we_loaded[i], 16 * NB * NX // 2)

        @block.scalar
        def _(act):
            act.sem_inc(y_stored, 16)
            with act.Fori(0, NB) as b:
                one = bass.ds(b, 1)
                act.wait_ge(y_stored, b * 16 + 16)
                act.dma_start(X[:], x_v[one].rearrange("b p t d -> (b p) t d")).then_inc(x_loaded, 16)
                act.dma_start(XT[:], xt_d[one].rearrange("b p c n -> (b p) c n")).then_inc(x_loaded, 16)
                act.dma_start(O[:], o_d[one].rearrange("b p t g m -> (b p) t (g m)")).then_inc(x_loaded, 16)
                for t in range(NT):
                    act.wait_ge(shift_ready, b + 1)
                    act.activation(EX[:, t], LG[:, t], ACT.Exp, bias=MX[:, t:t + 1],
                                   accum_out=SM3[:, t:t + 1]).then_inc(exp_ready, 1)
                for c in range(KC):
                    act.wait_ge(ot_psum, b * KC + c + 1)
                    act.activation(OT[:, c], pH[:, 1, c % 2], ACT.Copy).then_inc(ot_ready, 1)
                with act.Fori(0, NX // 2) as r:
                    for i in range(2):
                        n = b * NX + 2 * r + i
                        act.wait_ge(h_psum, n + 1)
                        act.activation(A[:, i], pH[:, i, 0], ACT.Silu, bias=WX[i][:, WE - 2:WE - 1]).then_inc(act_ready, 1)
                act.wait_ge(y_added, (b + 1) * (NX + 1) * NT)
                act.dma_start(y_v[one].rearrange("b p t d -> (b p) t d"), X[:]).then_inc(y_stored, 16)
            act.wait_ge(y_stored, 16 * NB + 16)

        @block.gpsimd
        def _(pool):
            pool.memset(GM[:, :, NGE:], BIG).then_inc(pads_set, 1)
            pool.memset(MS[:, :, NE3:], BIG).then_inc(pads_set, 1)
            pool.memset(GT[:, :, NE3:], 1.0).then_inc(pads_set, 1)

        @block.vector
        def _(dve):
            dve.wait_ge(pads_set, 3)
            dve.wait_ge(w_in, 96)
            with dve.Fori(0, NB) as b:
                link = Chain(dve, route_step, ROUTE, b)
                dve.wait_ge(logit_psum, b + 1)
                lg = pH[:, 0, 0, 0:NT * NE3].rearrange("p (t e) -> p t e", t=NT)
                link(dve.tensor_tensor(LG[:], lg, RB[:].unsqueeze(1).to_broadcast([P, NT, NE3]), ALU.add))
                link(dve.tensor_reduce(MX[:], LG[:], AX_X, ALU.max))
                dve.tensor_scalar(MX[:], MX[:], -1.0, None, ALU.mult).then_inc(shift_ready, 1)
                dve.wait_ge(exp_ready, b * NT + NT)
                link(dve.reciprocal(RC[:], SM3[:]))
                for t in range(NT):
                    link(dve.scalar_tensor_tensor(SC[:, t], EX[:, t], RC[:, t:t + 1], RBIAS[:], ALU.mult, ALU.add))
                link(dve.tensor_reduce(GM[:, :, 0:NGE], SC[:].rearrange("p t (g e) -> p t g e", g=NGE), AX_X,
                                       ALU.max))
                dve.memset(HOLD[:], 0.0)
                for t in range(NT):
                    dve.max(TG[:, t], GM[:, t]).then_inc(gmax_ready, 1)
                dve.wait_ge(gmax_ready, b * 2 * NT + NT)
                dve.memset(HOLD[:], 0.0)
                for t in range(NT):
                    dve.match_replace(GR[:, t], TG[:, t], GM[:, t], -BIG).then_inc(gmax_ready, 1)
                dve.wait_ge(gmax_ready, b * 2 * NT + 2 * NT)
                link(dve.tensor_tensor(PEN[:], GR[:, :, 0:NGE], GM[:, :, 0:NGE], ALU.not_equal))
                link(dve.tensor_scalar(PEN[:], PEN[:], BIG, -BIG, ALU.mult, ALU.add))
                for t in range(NT):
                    dve.tensor_tensor(MS[:, t, 0:NE3].rearrange("p (g e) -> p g e", g=NGE),
                                      SC[:, t].rearrange("p (g e) -> p g e", g=NGE),
                                      PEN[:, t].unsqueeze(2).to_broadcast([P, NGE, EG3]),
                                      ALU.add).then_inc(masked_ready, 1)
                dve.wait_ge(masked_ready, b * 3 * NT + NT)
                dve.memset(HOLD[:], 0.0)
                for t in range(NT):
                    dve.max(TE[:, t], MS[:, t]).then_inc(masked_ready, 1)
                dve.wait_ge(masked_ready, b * 3 * NT + 2 * NT)
                dve.memset(HOLD[:], 0.0)
                for t in range(NT):
                    dve.match_replace(MRP[:, t], TE[:, t], MS[:, t], -BIG).then_inc(masked_ready, 1)
                dve.wait_ge(masked_ready, b * 3 * NT + 3 * NT)
                dve.tensor_tensor(GT[:, :, 0:NE3], MRP[:, :, 0:NE3], MS[:, :, 0:NE3],
                                  ALU.not_equal).then_inc(gate_ready, 1)
                dve.wait_ge(gate_ready, 2 * b + 1)
                dve.tensor_tensor(GT[:, :, 0:NE3], GT[:, :, 0:NE3], SC[:], ALU.mult).then_inc(gate_ready, 1)
                dve.wait_ge(gt_psum, b + 1)
                dve.tensor_copy(GTT[:], pH[0:NX, 0, 1]).then_inc(gt_ready, 1)
                dve.wait_ge(x_loaded, 48 * (b + 1))
                for t in range(NT):
                    dve.wait_ge(base_psum, b * NT + t + 1)
                    dve.tensor_tensor(X[:, t], X[:, t], pY[:, t], ALU.add).then_inc(y_added, 1)
                with dve.Fori(0, NX // 2) as r:
                    for i in range(2):
                        n = b * NX + 2 * r + i
                        dve.wait_ge(act_ready, n + 1)
                        dve.scalar_tensor_tensor(H[:, i], pH[:, i, 1], WX[i][:, WE - 1:WE], A[:, i], ALU.add,
                                                 ALU.mult).then_inc(h_ready, 1)
                        for t in range(NT):
                            dve.wait_ge(y_psum, (n + 2) * NT + t + 1)
                            dve.wait_ge(y_added, (n + b) * NT + t + 1)
                            dve.scalar_tensor_tensor(X[:, t], pY[:, t], GT[:, t, bass.ds(2 * r + i, 1)], X[:, t],
                                                     ALU.mult, ALU.add).then_inc(y_added, 1)
                link.end()

        @block.tensor
        def _(pe):
            pe.sem_inc(y_psum, 2 * NT)
            pe.wait_ge(w_in, 96)
            with pe.Fori(0, NB) as b:
                pe.wait_ge(x_loaded, 48 * (b + 1))
                for t in range(NT):
                    for c in range(KC):
                        ins = pe.matmul(pH[:, 0, 0, t * NE3:(t + 1) * NE3], XT[:, c, t * P:(t + 1) * P], WR[:, c],
                                        start=(c == 0), stop=(c == KC - 1))
                ins.then_inc(logit_psum, 1)
                for c in range(KC):
                    if c >= 2:
                        pe.wait_ge(ot_ready, b * KC + c - 1)
                    for t in range(NT):
                        ins = pe.transpose(pH[:, 1, c % 2, t * P:(t + 1) * P], O[:, t, c * P:(c + 1) * P], ident[:])
                    ins.then_inc(ot_psum, 1)
                pe.wait_ge(ot_ready, b * KC + KC)
                for t in range(NT):
                    for c in range(KC):
                        pe.matmul(pY[:, t], OT[:, c, t * P:(t + 1) * P], WO[:, c], start=(c == 0), stop=False)
                pe.wait_ge(gate_ready, 2 * b + 2)
                for t in range(NT):
                    ins = pe.transpose(pH[0:NX, 0, 1, t * P:(t + 1) * P], GT[:, t], ident[:])
                ins.then_inc(gt_psum, 1)
                pe.wait_ge(gt_ready, b + 1)
                for t in range(NT):
                    pe.matmul(pY[:, t], GTT[:, t * P:(t + 1) * P], EB3[:], start=False,
                              stop=True).then_inc(base_psum, 1)

                def up(i, n):
                    for w in range(2):
                        for c in range(KC):
                            at = (w * KC + c) * P
                            ins = pe.matmul(pH[:, i, w], WX[i][:, at:at + P], XT[:, c], start=(c == 0),
                                            stop=(c == KC - 1))
                    ins.then_inc(h_psum, 1)

                with pe.Fori(0, NX // 2) as r:
                    n = b * NX + 2 * r
                    for i in range(2):
                        pe.wait_ge(we_loaded[i], 16 * (b * (NX // 2) + r + 1))
                        up(i, n + i)
                    for i in range(2):
                        pe.wait_ge(h_ready, n + i + 1)
                        for t in range(NT):
                            pe.wait_ge(y_added, (n + i + b) * NT + t + 1)
                            ins = pe.matmul(pY[:, t], H[:, i, t * P:(t + 1) * P], WX[i][:, 2 * D:3 * D], start=True,
                                            stop=True)
                            ins.then_inc(y_psum, 1)


def layer3(nc, x_in, x_out, wqkv, cos_d, sin_d, wo, wr, rb, rbias, we, eb3, mask_q, mask_k, pick_d, ident_d):
    nk = GH
    kw = NG * nk * HD
    xt_d = nc.dram_tensor("f_xt", (NB, P, KC, S), F32).ap()
    q_d = nc.dram_tensor("f_q", (NB, KC, 2, 2, GW, S), F32).ap()
    k_d = nc.dram_tensor("f_k", (NB, kw // P, P // (nk * HD), 2, nk * HD, S), F32).ap()
    v_d = nc.dram_tensor("f_v", (NB, NG, P, NT * nk * VW), F32).ap()
    o_d = nc.dram_tensor("f_o", (NB, P, NT, NG, GW), F32).ap()
    scratch = (xt_d, q_d, k_d, v_d)
    project(nc, "f_", nk, x_in, scratch, wqkv, cos_d, sin_d, ident_d)
    attend(nc, "g_", nk, scratch, o_d, mask_q, mask_k, pick_d, ident_d)
    moe(nc, x_in, x_out, xt_d, o_d, wo, wr, rb, rbias, we, eb3, ident_d)


def _chunks(w):
    k, n = w.shape
    return w.reshape(k // P, P, n).transpose(1, 0, 2)


def _layout0(i):
    wq = i["L0_attn_Wq"].reshape(H0, G0, P, D)[:, 0].reshape(H0 * P, D).T
    return {
        "wq": _chunks(wq),
        "bq": i["L0_attn_bq"].reshape(H0, G0, P)[:, 0].T,
        "zb": i["L0_attn_z"].T,
        "mt": i["L0_attn_M"].transpose(2, 0, 1),
        "wo": i["L0_attn_Wo"].T.reshape(H0, G0, P, D).transpose(2, 0, 1, 3),
        "wb": _chunks(i["L0_ffn_W_base"].T),
        "bb": i["L0_ffn_b_base"],
        "wr": _chunks(i["L0_ffn_W_router"].T),
        "la": _chunks(i["L0_ffn_A"].reshape(R0, D).T),
        "lb": i["L0_ffn_B"].transpose(0, 2, 1).reshape(R0, D),
        "sel": np.repeat(np.eye(NE0, dtype=np.float32), R0 // NE0, axis=1),
        "ident": np.eye(P, dtype=np.float32),
    }


def _fourier():
    n = np.arange(D)
    f = np.arange(D // 2)
    cos = np.cos(2 * np.pi * ((n[:, None] * f) % D) / D)
    sin = np.sin(2 * np.pi * ((n[:, None] * f) % D) / D)
    sin[:, 0] = np.cos(np.pi * n)
    fwd = np.concatenate([cos, sin], axis=1)
    lag = np.minimum(n, D - n)
    scale = np.full(D // 2, 2.0 / D)
    scale[0] = 1.0 / D
    power = scale[:, None] * np.cos(2 * np.pi * ((f[:, None] * lag) % D) / D)
    power_i = power.copy()
    power_i[0] = np.cos(np.pi * lag) / D
    inv = np.concatenate([scale, scale])[:, None] * fwd.T
    cor = np.concatenate([power, power_i])
    return [_chunks(a.astype(np.float32)) for a in (fwd, cor, inv)]


def _layout1(i):
    fwd, cor, inv = _fourier()
    return {
        "dft": fwd, "cor": cor, "inv": inv,
        "w1": _chunks(i["L1_ffn_W"].T),
        "b1": i["L1_ffn_bias"],
        "a1": i["L1_ffn_lora_A"].reshape(P, D),
        "bl1": i["L1_ffn_lora_B"].transpose(0, 2, 1).reshape(P, D),
        "cf": np.repeat(i["L1_ffn_lora_weights"], 16).reshape(P, 1),
        "ident": np.eye(P, dtype=np.float32),
    }


def _rotary():
    inv = np.float32(1.0) / np.float32(10000.0) ** (np.arange(0, HD, 2, dtype=np.float32) / np.float32(HD))
    ang = np.arange(S, dtype=np.float32)[:, None] * inv[None, :].astype(np.float32)
    return [np.ascontiguousarray(f(ang.astype(np.float64)).astype(np.float32).reshape(NT, P, HD // 2).transpose(1, 0, 2))
            for f in (np.cos, np.sin)]


def _masks():
    row = np.arange(P)
    late = np.where(row[None, :] > row[:, None], np.float32(-1e30), np.float32(0.0))
    return late, np.ascontiguousarray(late.T)


def _pick():
    own = np.broadcast_to(np.eye(GH, dtype=np.float32)[None, :, :, None], (2, GH, GH, S)).reshape(2 * GH, GH * S)
    return np.concatenate([np.zeros((SM - 2 * GH - SW, GH * S), np.float32), own])


def _group_columns(w, heads, pairs_first):
    w = w.reshape(D, NG, heads, *((HD // 2, 2) if pairs_first else (2, HD // 2)))
    return w.transpose(0, 1, *((4, 3) if pairs_first else (3, 4)), 2).reshape(D, NG * heads * HD)


def _layout2(i):
    w = i["L2_attn_w_qkv"]
    cos, sin = _rotary()
    mq, mk = _masks()
    return {
        "wqkv": _chunks(np.concatenate([_group_columns(w[:, :D], GH, True), _group_columns(w[:, D:D + P], 1, True),
                                        w[:, D + P:]], axis=1)),
        "cos": cos, "sin": sin,
        "cent": _chunks(i["L2_ffn_centroids"].T),
        "asg": i["L2_ffn_assignments"],
        "cidx": np.arange(NCL, dtype=np.float32).reshape(NCL, 1),
        "wo": _chunks(i["L2_attn_w_o"]),
        "w2": _chunks(i["L2_ffn_weight"].T),
        "b2": i["L2_ffn_bias"],
        "mq": mq, "mk": mk, "pick": _pick(),
        "ident": np.eye(P, dtype=np.float32),
    }


def _layout3(i):
    cos, sin = _rotary()
    mq, mk = _masks()
    halves = [slice(0, P), slice(P, 2 * P)]
    w1 = np.concatenate([i["L3_ffn_ew1"], np.stack([i["L3_ffn_sw1"][:, h] for h in halves])])
    w2 = np.concatenate([i["L3_ffn_ew2"], np.stack([i["L3_ffn_sw2"][:, h] for h in halves])])
    w3 = np.concatenate([i["L3_ffn_ew3"], np.stack([i["L3_ffn_sw3"][h] for h in halves])])
    b1 = np.concatenate([i["L3_ffn_eb1"], i["L3_ffn_sb1"].reshape(2, P)])
    b2 = np.concatenate([i["L3_ffn_eb2"], i["L3_ffn_sb2"].reshape(2, P)])
    up = [w.reshape(NX, KC, P, P).transpose(0, 2, 1, 3).reshape(NX, P, D) for w in (w1, w2)]
    return {
        "wqkv": _chunks(np.concatenate([_group_columns(i["L3_attn_wq"].T, GH, False),
                                        _group_columns(i["L3_attn_wk"].T, GH, False), i["L3_attn_wv"].T], axis=1)),
        "cos": cos, "sin": sin,
        "wo": _chunks(i["L3_attn_wo"].T),
        "wr": _chunks(i["L3_ffn_router_w"]),
        "rb": i["L3_ffn_router_b"],
        "rbias": i["L3_ffn_router_bias"],
        "we": np.concatenate([*up, w3, b1[:, :, None], b2[:, :, None]], axis=2),
        "eb3": np.concatenate([i["L3_ffn_eb3"], i["L3_ffn_sb3"][None], np.zeros((1, D), np.float32)]),
        "mq": mq, "mk": mk, "pick": _pick(),
        "ident": np.eye(P, dtype=np.float32),
    }


def build(nc, x, out, arrays):
    between = [nc.dram_tensor(f"x{n}", (NB, S, D), F32).ap() for n in (1, 2, 3)]
    for layer, x_in, x_out, ins in zip((layer0, layer1, layer2, layer3), (x, *between), (*between, out), arrays):
        layer(nc, x_in, x_out, *ins)


def kernel(**inputs):
    import concourse.bacc as _bacc
    from concourse.bass_utils import run_bass_kernel_spmd as _run

    inputs = {k: np.asarray(v) for k, v in inputs.items()}
    nc = _bacc.Bacc("TRN2", target_bir_lowering=False, num_devices=1)
    arrays = {}

    def given(name, a):
        arrays[name] = np.ascontiguousarray(a)
        return nc.dram_tensor(name, arrays[name].shape, mybir.dt.from_np(arrays[name].dtype),
                              kind="ExternalInput").ap()

    x = given("in_x", inputs["L0_attn_hidden_states"])
    layers = [[given(f"in_{n}_{name}", a) for name, a in layout(inputs).items()]
              for n, layout in enumerate((_layout0, _layout1, _layout2, _layout3))]
    out = nc.dram_tensor("out", (NB, S, D), F32, kind="ExternalOutput").ap()
    build(nc, x, out, layers)
    return _run(nc, [arrays], core_ids=[0]).results[0]["out"]
```

```python
from contextlib import ExitStack

import numpy as np
import concourse.bass as bass
from concourse import mybir

F32 = mybir.dt.float32
F32R = mybir.dt.float32r
BF16 = mybir.dt.bfloat16
I32 = mybir.dt.int32
ALU = mybir.AluOpType
ACT = mybir.ActivationFunctionType
AX_X = mybir.AxisListType.X

P = 128
D = 512
NB = 4
S = 512
NT = S // P
KC = D // P
LN_EPS = 1e-5
BIG = 3.0e38


class Semaphores:

    def __init__(self, ctx, nc, tag):
        self.nc, self.tag, self.held = nc, tag, []
        ctx.callback(self.give_back)

    def __call__(self, name):
        self.held.append(self.nc.alloc_semaphore(self.tag + name))
        return self.held[-1]

    def give_back(self):
        self.nc.clear_and_free_semaphores(self.held)
        self.nc.all_engine_barrier()


class Chain:

    def __init__(self, eng, sem, per=0, turn=0):
        self.eng, self.sem, self.base, self.n, self.per = eng, sem, turn * per, 0, per

    def __call__(self, ins):
        self.n += 1
        ins.then_inc(self.sem, 1)
        self.eng.wait_ge(self.sem, self.base + self.n)

    def end(self):
        assert self.n == self.per, (self.sem, self.n, self.per)


class Normed:

    def __init__(self, ctx, nc, tag, ident, banks, sem):
        def sb(name, shape, dt=F32):
            return ctx.enter_context(nc.sbuf_tensor(tag + name, shape, dt))

        self.ident, self.banks = ident, banks
        self.x = sb("X", [P, NT, D])
        self.xn = sb("XN", [P, NT, D])
        self.xt = sb("XT", [P, KC, S])
        self.moments = sb("ST", [P, NT, 6])
        self.mv = sb("MV", [P, NT, 2])
        self.ve = sb("VE", [P, NT])
        self.half = sb("HALF", [P, NT])
        self.rs = sb("RS", [P, NT])
        self.hold = sb("HOLD", [P, 1])
        self.half_set = sem("half_set")
        self.x_loaded = sem("x_loaded")
        self.moments_ready = sem("moments_ready")
        self.stats_ready = sem("stats_ready")
        self.var_ready = sem("var_ready")
        self.rstd_ready = sem("rstd_ready")
        self.xn_ready = sem("xn_ready")
        self.xt_psum = sem("xt_psum")
        self.xt_ready = sem("xt_ready")

    def vector_part(self, dve, b):
        dve.wait_ge(self.x_loaded, b * 16 + 16)
        for t in range(NT):
            dve.bn_stats(self.moments[:, t], self.x[:, t]).then_inc(self.moments_ready, 1)
        dve.wait_ge(self.moments_ready, b * NT + NT)
        dve.memset(self.hold[:], 0.0)
        for t in range(NT):
            dve.bn_aggr(self.mv[:, t], self.moments[:, t]).then_inc(self.stats_ready, 1)
        dve.wait_ge(self.stats_ready, b * NT + NT)
        dve.tensor_scalar(self.ve[:], self.mv[:, :, 1], LN_EPS, None, ALU.add).then_inc(self.var_ready, 1)
        dve.wait_ge(self.rstd_ready, b + 1)
        for t in range(NT):
            dve.tensor_scalar(self.xn[:, t], self.x[:, t], self.mv[:, t, 0:1], self.rs[:, t:t + 1], ALU.subtract,
                              ALU.mult).then_inc(self.xn_ready, 1)

    def pool_setup(self, pool):
        pool.memset(self.half[:], -0.5).then_inc(self.half_set, 1)
        pool.wait_ge(self.half_set, 1)

    def pool_part(self, pool, b):
        pool.wait_ge(self.var_ready, b + 1)
        pool.tensor_tensor(self.rs[:], self.ve[:], self.half[:], ALU.pow).then_inc(self.rstd_ready, 1)

    def tensor_part(self, pe, b):
        for c in range(KC):
            if c >= 2:
                pe.wait_ge(self.xt_ready, b * KC + c - 1)
            for t in range(NT):
                if c == 0:
                    pe.wait_ge(self.xn_ready, b * NT + t + 1)
                ins = pe.transpose(self.banks[:, c % 2, t * P:(t + 1) * P], self.xn[:, t, c * P:(c + 1) * P],
                                   self.ident[:])
            ins.then_inc(self.xt_psum, 1)

    def scalar_part(self, act, b):
        for c in range(KC):
            act.wait_ge(self.xt_psum, b * KC + c + 1)
            act.activation(self.xt[:, c], self.banks[:, c % 2], ACT.Copy).then_inc(self.xt_ready, 1)

H0, R0 = 8, P
G0 = 4
NE0 = 8
TOPB = 14


def layer0(nc, x_in, x_out, wq, bq, zb, mt, wo, wb, bb, wr, la, lb, sel, ident_d):
    with ExitStack() as ctx:
        def sb(name, shape, dt=F32):
            return ctx.enter_context(nc.sbuf_tensor("a_" + name, shape, dt))

        def ps(name, shape, dt=F32):
            return ctx.enter_context(nc.psum_tensor("a_" + name, shape, dt))

        sem = Semaphores(ctx, nc, "a_")

        x_v = x_in.rearrange("b (t p) d -> b p t d", p=P)
        y_v = x_out.rearrange("b (t p) d -> b p t d", p=P)

        WQ = sb("WQ", [P, KC, H0 * P])
        WB = sb("WB", [P, KC, D])
        MW = sb("MW", [P, H0, D])
        MT = sb("MT", [P, H0, P])
        WO = sb("WO", [P, 2, G0, D])
        ZB = sb("ZB", [P, H0, P])
        ZC = sb("ZC", [P, H0])
        BQ = sb("BQ", [P, H0])
        WR = sb("WR", [P, KC, NE0])
        LA = sb("LA", [P, KC, R0])
        LB = sb("LB", [P, D])
        SEL = sb("SEL", [NE0, R0])
        BB = sb("BB", [P, D])
        ident = sb("ident", [P, P])
        X = sb("X", [P, NT, D])
        XN = sb("XN", [P, NT, D])
        XT = sb("XT", [P, KC, S])
        HT = sb("HT", [P, S])
        ST = sb("ST", [P, NT, 6])
        MV = sb("MV", [P, NT, 2])
        VE = sb("VE", [P, NT])
        HALF = sb("HALF", [P, NT])
        RS = sb("RS", [P, NT])
        LG = sb("LG", [P, NT, TOPB])
        LR = sb("LR", [P, NT, TOPB])
        TOP = sb("TOP", [P, NT, 8])
        NM = sb("NM", [P, NT])
        EG = sb("EG", [P, NT, NE0])
        EM = sb("EM", [P, NT, NE0])
        CS = sb("CS", [P, NT])
        CR = sb("CR", [P, NT])
        CB = sb("CB", [P, NT, NE0])
        CT = sb("CT", [NE0, S])
        NEG = sb("NEG", [P, 2, S])
        EX = sb("EX", [P, 2, S])
        RL = sb("RL", [P, 2, S])
        SG = sb("SG", [P, 2, S])
        DN = sb("DN", [P, 2, S])
        SN = sb("SN", [P, 2, S])

        HOLD = sb("HOLD", [P, 1])

        pT = ps("pT", [P, 2, S])
        pQ = ps("pQ", [P, 2, S])
        pO = ps("pO", [P, NT, S])

        w_in = sem("w_in")
        wo_in = [sem("wo_in_even"), sem("wo_in_odd")]
        wo_used = sem("wo_used")
        mw_done = sem("mw_done")
        mw_copied = sem("mw_copied")
        x_loaded = sem("x_loaded")
        stats_ready = sem("stats_ready")
        var_ready = sem("var_ready")
        rstd_ready = sem("rstd_ready")
        xn_ready = sem("xn_ready")
        xt_psum = sem("xt_psum")
        xt_ready = sem("xt_ready")
        router_psum = sem("router_psum")
        top_ready = sem("top_ready")
        shift_ready = sem("shift_ready")
        gates_exp = sem("gates_exp")
        comb_ready = sem("comb_ready")
        comb_psum = sem("comb_psum")
        comb_copied = sem("comb_copied")
        lora_psum = sem("lora_psum")
        lora_copied = sem("lora_copied")
        spread_psum = sem("spread_psum")
        lora_ready = sem("lora_ready")
        q_psum = sem("q_psum")
        neg_ready = sem("neg_ready")
        exp_ready = sem("exp_ready")
        relu_ready = sem("relu_ready")
        sig_ready = sem("sig_ready")
        den_psum = sem("den_psum")
        sign_ready = sem("sign_ready")
        out_psum = sem("out_psum")
        y_ready = sem("y_ready")
        xb_ready = sem("xb_ready")
        y_stored = sem("y_stored")
        dve_step = sem("dve_step")
        pool_step = sem("pool_step")
        pads_set = sem("pads_set")
        ones_set = sem("ones_set")
        zb_ready = sem("zb_ready")

        DVE_PER = NT + 6
        block = ctx.enter_context(nc.Block())

        @block.sync
        def _(sp):
            sp.dma_start(ident[:], ident_d).then_inc(w_in, 16)
            sp.dma_start(MT[:], mt).then_inc(w_in, 16)
            sp.dma_start(WB[:], wb).then_inc(w_in, 16)
            sp.dma_start(WR[:], wr).then_inc(w_in, 16)
            sp.dma_start(LA[:], la).then_inc(w_in, 16)
            sp.dma_start(LB[:], lb).then_inc(w_in, 16)
            sp.dma_start(SEL[:], sel).then_inc(w_in, 16)
            sp.dma_start(ZC[:], zb).then_inc(w_in, 16)
            sp.dma_start(BQ[:], bq).then_inc(w_in, 16)
            sp.dma_start(WQ[:], wq).then_inc(w_in, 16)
            sp.dma_start(BB[:], bb.partition_broadcast(P)).then_inc(w_in, 16)
            with sp.Fori(0, NB) as b:
                sp.wait_ge(y_stored, b * 16 + 16)
                sp.dma_start(X[:], x_v[bass.ds(b, 1)].rearrange("b p t d -> (b p) t d")).then_inc(x_loaded, 16)
                sp.wait_ge(y_ready, b * NT + NT)
                sp.dma_start(y_v[bass.ds(b, 1)].rearrange("b p t d -> (b p) t d"), X[:]).then_inc(y_stored, 16)
            sp.wait_ge(y_stored, 16 * NB + 16)

        @block.scalar
        def _(act):
            for h in range(H0):
                if h >= 2:
                    act.wait_ge(wo_used, h - 1)
                act.dma_start(WO[:, h % 2], wo[:, h]).then_inc(wo_in[h % 2], 16)
                if h >= 1:
                    act.wait_ge(mw_done, h)
                    act.activation(MW[:, h - 1], pO[:, 2 + (h - 1) % 2], ACT.Copy).then_inc(mw_copied, 1)
            act.wait_ge(mw_done, H0)
            act.activation(MW[:, H0 - 1], pO[:, 2 + (H0 - 1) % 2], ACT.Copy).then_inc(mw_copied, 1)
            with act.Fori(0, NB) as b:
                for c in range(KC):
                    act.wait_ge(xt_psum, b * KC + c + 1)
                    act.activation(XT[:, c], pT[:, c % 2], ACT.Copy).then_inc(xt_ready, 1)
                act.wait_ge(shift_ready, b + 1)
                for t in range(NT):
                    ins = act.activation(EG[:, t], LG[:, t, 0:NE0], ACT.Exp, bias=NM[:, t:t + 1])
                ins.then_inc(gates_exp, 1)
                act.wait_ge(lora_psum, b + 1)
                act.activation(HT[:], pQ[:, 1], ACT.Copy).then_inc(lora_copied, 1)
                for h in range(H0):
                    act.wait_ge(q_psum, b * H0 + h + 1)
                    act.activation(RL[:, h % 2], pQ[:, 0], ACT.Relu, bias=BQ[:, h:h + 1]).then_inc(relu_ready, 1)
                    act.wait_ge(neg_ready, b * H0 + h + 1)
                    act.activation(EX[:, h % 2], NEG[:, h % 2], ACT.Exp).then_inc(exp_ready, 1)

        @block.gpsimd
        def _(pool):
            pool.wait_ge(w_in, 11 * 16)
            pool.memset(HALF[:], -0.5).then_inc(pads_set, 1)
            pool.memset(LG[:, :, NE0:TOPB], BIG).then_inc(pads_set, 1)
            pool.wait_ge(pads_set, 2)
            pool.sem_inc(y_stored, 16)
            with pool.Fori(0, NB) as b:
                pool.wait_ge(var_ready, b + 1)
                pool.tensor_tensor(RS[:], VE[:], HALF[:], ALU.pow).then_inc(rstd_ready, 1)
                for t in range(NT):
                    pool.wait_ge(xn_ready, b * NT + t + 1)
                    pool.tensor_tensor(X[:, t], X[:, t], BB[:], ALU.add).then_inc(xb_ready, 1)

        @block.vector
        def _(dve):
            dve.memset(ZB[:], 1.0).then_inc(ones_set, 1)
            dve.wait_ge(ones_set, 1)
            dve.wait_ge(pads_set, 2)
            dve.wait_ge(w_in, 11 * 16)
            for h in range(H0):
                dve.tensor_scalar(ZB[:, h], ZB[:, h], ZC[:, h:h + 1], None, ALU.mult).then_inc(zb_ready, 1)
            with dve.Fori(0, NB) as b:
                link = Chain(dve, dve_step, DVE_PER, b)
                dve.wait_ge(x_loaded, b * 16 + 16)
                for t in range(NT):
                    link(dve.bn_stats(ST[:, t], X[:, t]))
                dve.memset(HOLD[:], 0.0)
                for t in range(NT):
                    dve.bn_aggr(MV[:, t], ST[:, t]).then_inc(stats_ready, 1)
                dve.wait_ge(stats_ready, b * NT + NT)
                dve.tensor_scalar(VE[:], MV[:, :, 1], LN_EPS, None, ALU.add).then_inc(var_ready, 1)
                dve.wait_ge(rstd_ready, b + 1)
                for t in range(NT):
                    dve.tensor_scalar(XN[:, t], X[:, t], MV[:, t, 0:1], RS[:, t:t + 1], ALU.subtract,
                                      ALU.mult).then_inc(xn_ready, 1)
                dve.wait_ge(router_psum, b + 1)
                link(dve.tensor_copy(LG[:, :, 0:NE0], pQ[:, 0, 0:NT * NE0].rearrange("p (t e) -> p t e", t=NT)))
                dve.memset(HOLD[:], 0.0)
                for t in range(NT):
                    dve.max(TOP[:, t], LG[:, t]).then_inc(top_ready, 1)
                dve.wait_ge(top_ready, b * 2 * NT + NT)
                dve.tensor_scalar(NM[:], TOP[:, :, 6], -1.0, None, ALU.mult).then_inc(shift_ready, 1)
                for t in range(NT):
                    dve.match_replace(LR[:, t], TOP[:, t], LG[:, t], -BIG).then_inc(top_ready, 1)
                dve.wait_ge(top_ready, b * 2 * NT + 2 * NT)
                link(dve.tensor_tensor(EM[:], LR[:, :, 0:NE0], LG[:, :, 0:NE0], ALU.not_equal))
                dve.wait_ge(gates_exp, b + 1)
                link(dve.tensor_tensor(EM[:], EM[:], EG[:], ALU.mult))
                link(dve.tensor_reduce(CS[:], EM[:], AX_X, ALU.add))
                link(dve.reciprocal(CR[:], CS[:]))
                link(dve.tensor_scalar(CR[:], CR[:], 2.0, None, ALU.mult))
                for t in range(NT):
                    dve.tensor_scalar(CB[:, t], EM[:, t], CR[:, t:t + 1], None, ALU.mult).then_inc(comb_ready, 1)
                dve.wait_ge(comb_psum, b + 1)
                dve.tensor_copy(CT[:], pT[0:NE0, 0]).then_inc(comb_copied, 1)
                dve.wait_ge(spread_psum, b + 1)
                dve.wait_ge(lora_copied, b + 1)
                dve.tensor_tensor(HT[:], pT[:, 1], HT[:], ALU.mult).then_inc(lora_ready, 1)
                for h in range(H0):
                    dve.wait_ge(relu_ready, b * H0 + h + 1)
                    dve.tensor_scalar(NEG[:, h % 2], pQ[:, 0], BQ[:, h:h + 1], 0.0, ALU.add,
                                      ALU.min).then_inc(neg_ready, 1)
                    dve.wait_ge(exp_ready, b * H0 + h + 1)
                    dve.tensor_tensor(SG[:, h % 2], RL[:, h % 2], EX[:, h % 2], ALU.add).then_inc(sig_ready, 1)
                    dve.wait_ge(den_psum, b * H0 + h + 1)
                    dve.tensor_scalar(DN[:, h % 2], pQ[:, 1], 1e-6, None, ALU.add).then_inc(sign_ready, 1)
                    dve.wait_ge(sign_ready, (b * H0 + h) * 3 + 1)
                    dve.reciprocal(DN[:, h % 2], DN[:, h % 2]).then_inc(sign_ready, 1)
                    dve.wait_ge(sign_ready, (b * H0 + h) * 3 + 2)
                    dve.wait_ge(sig_ready, b * H0 + h + 1)
                    dve.tensor_tensor(SN[:, h % 2], SG[:, h % 2], DN[:, h % 2], ALU.mult).then_inc(sign_ready, 1)
                for t in range(NT):
                    dve.wait_ge(out_psum, b * NT + t + 1)
                    dve.wait_ge(xb_ready, b * NT + t + 1)
                    dve.tensor_tensor(X[:, t], X[:, t], pO[:, t], ALU.add).then_inc(y_ready, 1)
                link.end()

        @block.tensor
        def _(pe):
            pe.wait_ge(w_in, 11 * 16)
            for h in range(H0):
                pe.wait_ge(wo_in[h % 2], 16 * (h // 2 + 1))
                if h >= 2:
                    pe.wait_ge(mw_copied, h - 1)
                for g in range(G0):
                    ins = pe.matmul(pO[:, 2 + h % 2], MT[:, h], WO[:, h % 2, g], start=(g == 0), stop=(g == G0 - 1))
                ins.then_inc(mw_done, 1)
                pe.wait_ge(mw_done, h + 1)
                pe.sem_inc(wo_used, 1)
            pe.wait_ge(mw_copied, H0)
            pe.wait_ge(zb_ready, H0)
            with pe.Fori(0, NB) as b:
                for c in range(KC):
                    if c >= 2:
                        pe.wait_ge(xt_ready, b * KC + c - 1)
                    for t in range(NT):
                        if c == 0:
                            pe.wait_ge(xn_ready, b * NT + t + 1)
                        ins = pe.transpose(pT[:, c % 2, t * P:(t + 1) * P], XN[:, t, c * P:(c + 1) * P], ident[:])
                    ins.then_inc(xt_psum, 1)
                pe.wait_ge(xt_ready, b * KC + KC)
                for t in range(NT):
                    for c in range(KC):
                        ins = pe.matmul(pQ[:, 0, t * NE0:(t + 1) * NE0], XT[:, c, t * P:(t + 1) * P], WR[:, c],
                                        start=(c == 0), stop=(c == KC - 1))
                ins.then_inc(router_psum, 1)
                for c in range(KC):
                    ins = pe.matmul(pQ[:, 1], LA[:, c], XT[:, c], start=(c == 0), stop=(c == KC - 1))
                ins.then_inc(lora_psum, 1)
                for t in range(NT):
                    for c in range(KC):
                        pe.matmul(pO[:, t], XT[:, c, t * P:(t + 1) * P], WB[:, c], start=(c == 0), stop=False)
                pe.wait_ge(comb_ready, b * NT + NT)
                for t in range(NT):
                    ins = pe.transpose(pT[0:NE0, 0, t * P:(t + 1) * P], CB[:, t], ident[:])
                ins.then_inc(comb_psum, 1)
                pe.wait_ge(comb_copied, b + 1)
                pe.matmul(pT[:, 1], SEL[:], CT[:], start=True, stop=True).then_inc(spread_psum, 1)
                pe.wait_ge(lora_ready, b + 1)
                for t in range(NT):
                    pe.matmul(pO[:, t], HT[:, t * P:(t + 1) * P], LB[:], start=False, stop=False)

                def out_products(h):
                    pe.wait_ge(sign_ready, (b * H0 + h + 1) * 3)
                    for t in range(NT):
                        ins = pe.matmul(pO[:, t], SN[:, h % 2, t * P:(t + 1) * P], MW[:, h], start=False,
                                        stop=(h == H0 - 1))
                        if h == H0 - 1:
                            ins.then_inc(out_psum, 1)

                for h in range(H0):
                    if h >= 1:
                        pe.wait_ge(neg_ready, b * H0 + h)
                    for c in range(KC):
                        ins = pe.matmul(pQ[:, 0], WQ[:, c, h * P:(h + 1) * P], XT[:, c], start=(c == 0),
                                        stop=(c == KC - 1))
                    ins.then_inc(q_psum, 1)
                    if h >= 1:
                        out_products(h - 1)
                    pe.wait_ge(sig_ready, b * H0 + h + 1)
                    pe.matmul(pQ[:, 1], ZB[:, h], SG[:, h % 2], start=True, stop=True).then_inc(den_psum, 1)
                out_products(H0 - 1)
                pe.wait_ge(y_ready, b * NT + NT)

TOP_LAGS = 6
LAGP = S + 2


def layer1(nc, x_in, x_out, dft, cor, inv, w1, b1, a1, bl1, cf, ident_d):
    with ExitStack() as ctx:
        def sb(name, shape, dt=F32):
            return ctx.enter_context(nc.sbuf_tensor("b_" + name, shape, dt))

        def ps(name, shape, dt=F32):
            return ctx.enter_context(nc.psum_tensor("b_" + name, shape, dt))

        sem = Semaphores(ctx, nc, "b_")

        x_v = x_in.rearrange("b (t p) d -> b p t d", p=P)
        y_v = x_out.rearrange("b (t p) d -> b p t d", p=P)

        ident = sb("ident", [P, P])
        DFT = sb("DFT", [P, KC, D])
        COR = sb("COR", [P, KC, D])
        INV = sb("INV", [P, KC, D])
        W = sb("W", [P, KC, D])
        A1 = sb("A1", [P, D])
        BL = sb("BL", [P, D])
        CF = sb("CF", [P, 1])
        BB = sb("BB", [P, D])
        FX = sb("FX", [P, KC, S])
        SQ = sb("SQ", [P, KC, S])
        CO = sb("CO", [P, 2, LAGP])
        RP = sb("RP", [P, 2, LAGP])
        TOP = sb("TOP", [P, NT, 8])
        NM = sb("NM", [P, NT])
        EX = sb("EX", [P, 2, D])
        MK = sb("MK", [P, 2, D])
        WS = sb("WS", [P, NT])
        WR = sb("WR", [P, NT])
        WL = sb("WL", [P, NT, D])
        WT = sb("WT", [P, KC, S])
        FW = sb("FW", [P, KC, S])
        FA = sb("FA", [P, S])
        TM = sb("TM", [P, 2, 4, S])

        pT = ps("pT", [P, 2, S])
        pF = ps("pF", [P, 2, S])
        pO = ps("pO", [P, NT, S])
        nm = Normed(ctx, nc, "b_", ident, pT, sem)
        X = nm.x
        OH = nm.xn

        w_in = sem("w_in")
        lora_scaled = sem("lora_scaled")
        lora_psum = sem("lora_psum")
        w_ready = sem("w_ready")
        pads_set = sem("pads_set")
        fx_psum = sem("fx_psum")
        fx_ready = sem("fx_ready")
        sq_ready = sem("sq_ready")
        cor_psum = sem("cor_psum")
        cor_ready = sem("cor_ready")
        top_ready = sem("top_ready")
        shift_ready = sem("shift_ready")
        exp_ready = sem("exp_ready")
        lag_step = sem("lag_step")
        weight_ready = sem("weight_ready")
        wt_psum = sem("wt_psum")
        wt_ready = sem("wt_ready")
        fw_psum = sem("fw_psum")
        fw_ready = sem("fw_ready")
        term_ready = sem("term_ready")
        prod_ready = sem("prod_ready")
        out_psum = sem("out_psum")
        xb_ready = sem("xb_ready")
        y_ready = sem("y_ready")
        y_stored = sem("y_stored")
        LAG_STEPS = 4
        block = ctx.enter_context(nc.Block())

        @block.sync
        def _(sp):
            sp.dma_start(ident[:], ident_d).then_inc(w_in, 16)
            sp.dma_start(A1[:], a1).then_inc(w_in, 16)
            sp.dma_start(BL[:], bl1).then_inc(w_in, 16)
            sp.dma_start(CF[:], cf).then_inc(w_in, 16)
            sp.dma_start(W[:], w1).then_inc(w_in, 16)
            sp.dma_start(DFT[:], dft).then_inc(w_in, 16)
            sp.dma_start(COR[:], cor).then_inc(w_in, 16)
            sp.dma_start(INV[:], inv).then_inc(w_in, 16)
            sp.dma_start(BB[:], b1.partition_broadcast(P)).then_inc(w_in, 16)
            with sp.Fori(0, NB) as b:
                sp.wait_ge(y_stored, b * 16 + 16)
                sp.dma_start(X[:], x_v[bass.ds(b, 1)].rearrange("b p t d -> (b p) t d")).then_inc(nm.x_loaded, 16)
                sp.wait_ge(y_ready, b * NT + NT)
                sp.dma_start(y_v[bass.ds(b, 1)].rearrange("b p t d -> (b p) t d"), X[:]).then_inc(y_stored, 16)
            sp.wait_ge(y_stored, 16 * NB + 16)

        @block.scalar
        def _(act):
            with act.Fori(0, NB) as b:
                nm.scalar_part(act, b)
                for c in range(KC):
                    act.wait_ge(fx_psum, b * KC + c + 1)
                    act.activation(SQ[:, c], pF[:, c % 2], ACT.Square).then_inc(sq_ready, 1)
                    act.activation(FX[:, c], pF[:, c % 2], ACT.Copy).then_inc(fx_ready, 1)
                for t in range(NT):
                    act.wait_ge(cor_psum, b * NT + t + 1)
                    if t >= 2:
                        act.wait_ge(weight_ready, b * NT + t - 1)
                    act.activation(CO[:, t % 2, 0:D], pF[:, t % 2], ACT.Copy).then_inc(cor_ready, 1)
                    act.wait_ge(cor_ready, b * NT + t + 1)
                    act.wait_ge(shift_ready, b * NT + t + 1)
                    act.activation(EX[:, t % 2], CO[:, t % 2, 0:D], ACT.Exp, bias=NM[:, t:t + 1]).then_inc(exp_ready, 1)
                for c in range(KC):
                    act.wait_ge(wt_psum, b * KC + c + 1)
                    act.activation(WT[:, c], pT[:, c % 2], ACT.Copy).then_inc(wt_ready, 1)
                for c in range(KC):
                    act.wait_ge(fw_psum, b * KC + c + 1)
                    if c == 0:
                        act.activation(FA[:], pF[:, 0], ACT.Copy).then_inc(fw_ready, 1)
                    act.activation(FW[:, c], pF[:, c % 2], ACT.Copy).then_inc(fw_ready, 1)
                    if c == 2:
                        act.wait_ge(fw_ready, b * 7 + 4)
                        act.activation(FA[0:1, :], FW[0:1, 2], ACT.Copy).then_inc(fw_ready, 1)
                        act.wait_ge(fw_ready, b * 7 + 5)
                        act.activation(FW[0:1, 2], FW[0:1, 2], ACT.Copy, scale=0.0).then_inc(fw_ready, 1)

        @block.gpsimd
        def _(pool):
            pool.wait_ge(w_in, 9 * 16)
            pool.memset(CO[:, :, D:LAGP], BIG).then_inc(pads_set, 1)
            nm.pool_setup(pool)
            pool.sem_inc(y_stored, 16)
            with pool.Fori(0, NB) as b:
                nm.pool_part(pool, b)
                for t in range(NT):
                    pool.wait_ge(nm.xn_ready, b * NT + t + 1)
                    pool.tensor_tensor(X[:, t], X[:, t], BB[:], ALU.add).then_inc(xb_ready, 1)
                for k in range(2):
                    pool.wait_ge(term_ready, b * 8 + 4 * k + 4)
                    pool.tensor_tensor(OH[:, k], TM[:, k, 0], TM[:, k, 1], ALU.add).then_inc(prod_ready, 1)
                    pool.tensor_tensor(OH[:, k + 2], TM[:, k, 2], TM[:, k, 3], ALU.subtract).then_inc(prod_ready, 1)

        @block.vector
        def _(dve):
            dve.wait_ge(w_in, 9 * 16)
            dve.tensor_scalar(BL[:], BL[:], CF[:], 2.0, ALU.mult, ALU.mult).then_inc(lora_scaled, 1)
            for c in range(KC):
                dve.wait_ge(lora_psum, c + 1)
                dve.tensor_tensor(W[:, c], W[:, c], pO[:, c], ALU.add).then_inc(w_ready, 1)
            dve.wait_ge(pads_set, 1)
            with dve.Fori(0, NB) as b:
                nm.vector_part(dve, b)
                for t in range(NT):
                    i = t % 2
                    link = Chain(dve, lag_step, LAG_STEPS, b * NT + t)
                    dve.wait_ge(cor_ready, b * NT + t + 1)
                    dve.memset(nm.hold[:], 0.0)
                    dve.max(TOP[:, t], CO[:, i]).then_inc(top_ready, 1)
                    dve.wait_ge(top_ready, b * NT + t + 1)
                    dve.tensor_scalar(NM[:, t:t + 1], TOP[:, t, 2:3], -1.0, None, ALU.mult).then_inc(shift_ready, 1)
                    link(dve.match_replace(RP[:, i], TOP[:, t], CO[:, i], -BIG))
                    link(dve.tensor_tensor(MK[:, i], RP[:, i, 0:D], CO[:, i, 0:D], ALU.not_equal))
                    dve.wait_ge(exp_ready, b * NT + t + 1)
                    link(dve.tensor_tensor_reduce(WL[:, t], EX[:, i], MK[:, i], 1.0, 0.0, ALU.mult, ALU.add,
                                                  WS[:, t:t + 1]))
                    link(dve.reciprocal(WR[:, t:t + 1], WS[:, t:t + 1]))
                    dve.tensor_scalar(WL[:, t], WL[:, t], WR[:, t:t + 1], None, ALU.mult).then_inc(weight_ready, 1)
                    link.end()
                for k in range(2):
                    dve.wait_ge(fw_ready, b * 7 + 6 + k)
                    re, im = FW[:, k], FW[:, k + 2]
                    alt = FA[:] if k == 0 else FW[:, 1]
                    dve.tensor_tensor(TM[:, k, 0], re, FX[:, k], ALU.mult).then_inc(term_ready, 1)
                    dve.tensor_tensor(TM[:, k, 1], im, FX[:, k + 2], ALU.mult).then_inc(term_ready, 1)
                    dve.tensor_tensor(TM[:, k, 2], alt, FX[:, k + 2], ALU.mult).then_inc(term_ready, 1)
                    dve.tensor_tensor(TM[:, k, 3], im, FX[:, k], ALU.mult).then_inc(term_ready, 1)
                for t in range(NT):
                    dve.wait_ge(out_psum, b * NT + t + 1)
                    dve.wait_ge(xb_ready, b * NT + t + 1)
                    dve.tensor_tensor(X[:, t], X[:, t], pO[:, t], ALU.add).then_inc(y_ready, 1)

        @block.tensor
        def _(pe):
            pe.wait_ge(w_in, 9 * 16)
            pe.wait_ge(lora_scaled, 1)
            for c in range(KC):
                pe.matmul(pO[:, c], A1[:, c * P:(c + 1) * P], BL[:], start=True, stop=True).then_inc(lora_psum, 1)
            pe.wait_ge(w_ready, KC)
            with pe.Fori(0, NB) as b:
                nm.tensor_part(pe, b)
                pe.wait_ge(nm.xt_ready, b * KC + KC)
                for m in range(KC):
                    if m >= 2:
                        pe.wait_ge(fx_ready, b * KC + m - 1)
                    for c in range(KC):
                        ins = pe.matmul(pF[:, m % 2], DFT[:, c, m * P:(m + 1) * P], nm.xt[:, c], start=(c == 0),
                                        stop=(c == KC - 1))
                    ins.then_inc(fx_psum, 1)
                pe.wait_ge(fx_ready, b * KC + KC)
                for t in range(NT):
                    if t >= 2:
                        pe.wait_ge(cor_ready, b * NT + t - 1)
                    for c in range(KC):
                        ins = pe.matmul(pF[:, t % 2], SQ[:, c, t * P:(t + 1) * P], COR[:, c], start=(c == 0),
                                        stop=(c == KC - 1))
                    ins.then_inc(cor_psum, 1)
                    for c in range(KC):
                        pe.matmul(pO[:, t], nm.xt[:, c, t * P:(t + 1) * P], W[:, c], start=(c == 0), stop=False)
                for c in range(KC):
                    if c >= 2:
                        pe.wait_ge(wt_ready, b * KC + c - 1)
                    for t in range(NT):
                        if c == 0:
                            pe.wait_ge(weight_ready, b * NT + t + 1)
                        ins = pe.transpose(pT[:, c % 2, t * P:(t + 1) * P], WL[:, t, c * P:(c + 1) * P], ident[:])
                    ins.then_inc(wt_psum, 1)
                pe.wait_ge(wt_ready, b * KC + KC)
                for m in range(KC):
                    if m >= 2:
                        pe.wait_ge(fw_ready, b * 7 + m)
                    for c in range(KC):
                        ins = pe.matmul(pF[:, m % 2], DFT[:, c, m * P:(m + 1) * P], WT[:, c], start=(c == 0),
                                        stop=(c == KC - 1))
                    ins.then_inc(fw_psum, 1)
                pe.wait_ge(prod_ready, b * KC + KC)
                for t in range(NT):
                    for c in range(KC):
                        ins = pe.matmul(pO[:, t], OH[:, c, t * P:(t + 1) * P], INV[:, c], start=False,
                                        stop=(c == KC - 1))
                    ins.then_inc(out_psum, 1)
                pe.wait_ge(y_ready, b * NT + NT)

HD = 16
GH = 4
NG = 8
GW = GH * HD
VW = HD + 1
SW = 4 * HD
SM = 96 + 2 * GH
NCL = 64


def project(nc, tag, nk, x_in, scratch, wqkv, cos_d, sin_d, ident_d, gate=None, xn_d=None):
    xt_d, q_d, k_d, v_d = scratch
    kw = NG * nk * HD
    kc = kw // P
    parts = [(0, D), (D, kw), (D + kw, kw)] if nk == GH else [(0, D), (D, 2 * kw)]
    with ExitStack() as ctx:
        def sb(name, shape, dt=F32):
            return ctx.enter_context(nc.sbuf_tensor(tag + name, shape, dt))

        def ps(name, shape, dt=F32):
            return ctx.enter_context(nc.psum_tensor(tag + name, shape, dt))

        sem = Semaphores(ctx, nc, tag)

        x_v = x_in.rearrange("b (t p) d -> b p t d", p=P)
        ident = sb("ident", [P, P])
        W = sb("W", [P, KC, D + 2 * kw])
        COS = sb("COS", [P, NT, HD // 2])
        SIN = sb("SIN", [P, NT, HD // 2])
        ROT = sb("ROT", [P, 2, 2, 2, D])
        QR = sb("QR", [P, NT, D + kw])
        HI = sb("HI", [P, KC + kc, S], F32R)
        LO = sb("LO", [P, KC + kc, S], F32R)
        V = sb("V", [P, NG, NT, nk, VW])
        pT = ps("pT", [P, 2, S])
        pA = ps("pA", [P, 2, 3, S])
        nm = Normed(ctx, nc, tag, ident, pT, sem)

        w_in = sem("w_in")
        ones_set = sem("ones_set")
        qkv_psum = sem("qkv_psum")
        turned = sem("turned")
        rotated = sem("rotated")
        v_ready = sem("v_ready")
        turn_psum = sem("turn_psum")
        hi_ready = sem("hi_ready")
        lo_ready = sem("lo_ready")
        stored = sem("stored")
        NST = 2 + 2 * 2 + 2 * (P // (nk * HD)) + (xn_d is not None)
        if gate:
            cent, asg, cidx, sel_d = gate
            CE = sb("CE", [P, KC, NCL])
            CM = sb("CM", [P, NT])
            CN = sb("CN", [P, NT])
            CX = sb("CX", [P, NT, NCL])
            CS = sb("CS", [P, NT])
            CR = sb("CR", [P, NT])
            CP = sb("CP", [P, NCL])
            CT = sb("CT", [NCL, 2])
            AI = sb("AI", [NCL, D], I32)
            AF = sb("AF", [NCL, D])
            CI = sb("CI", [NCL, 1])
            SR = sb("SR", [1, D])
            logit_psum = sem("logit_psum")
            cmax_ready = sem("cmax_ready")
            cshift_ready = sem("cshift_ready")
            cexp_ready = sem("cexp_ready")
            crec_ready = sem("crec_ready")
            chit_ready = sem("chit_ready")
            best_psum = sem("best_psum")
            hit_ready = sem("hit_ready")
            asg_ready = sem("asg_ready")
            sel_psum = sem("sel_psum")
            sel_ready = sem("sel_ready")
            sel_stored = sem("sel_stored")
        NW = 4 + (3 if gate else 0)
        block = ctx.enter_context(nc.Block())

        @block.sync
        def _(sp):
            sp.dma_start(ident[:], ident_d).then_inc(w_in, 16)
            sp.dma_start(COS[:], cos_d).then_inc(w_in, 16)
            sp.dma_start(SIN[:], sin_d).then_inc(w_in, 16)
            sp.dma_start(W[:], wqkv).then_inc(w_in, 16)
            if gate:
                sp.dma_start(CE[:], cent).then_inc(w_in, 16)
                sp.dma_start(AI[:], asg.partition_broadcast(NCL)).then_inc(w_in, 16)
                sp.dma_start(CI[:], cidx).then_inc(w_in, 16)
            sp.sem_inc(stored, 16)
            with sp.Fori(0, NB) as b:
                one = bass.ds(b, 1)
                sp.wait_ge(stored, b * 16 * NST + 16)
                sp.dma_start(nm.x[:], x_v[one].rearrange("b p t d -> (b p) t d")).then_inc(nm.x_loaded, 16)
                sp.wait_ge(nm.xt_ready, b * KC + KC)
                sp.dma_start(xt_d[one].rearrange("b p c n -> (b p) c n"), nm.xt[:]).then_inc(stored, 16)
                if xn_d is not None:
                    sp.wait_ge(nm.xn_ready, b * NT + NT)
                    sp.dma_start(xn_d.rearrange("(b t p) d -> b p t d", b=NB, p=P)[one].rearrange(
                        "b p t d -> (b p) t d"), nm.xn[:]).then_inc(stored, 16)
                sp.wait_ge(v_ready, b * NT + NT)
                sp.dma_start(v_d[one].rearrange("b g p m -> (b p) g m"),
                             V[:].rearrange("p g t j d -> p g (t j d)")).then_inc(stored, 16)
                sp.wait_ge(lo_ready, b * (KC + kc) + KC)
                for half in range(2):
                    rows = slice(half * GW, (half + 1) * GW)
                    for part, buf in ((0, HI), (1, LO)):
                        sp.dma_start(q_d[one, :, half, part].rearrange("b c f n -> (b f) c n"),
                                     buf[rows, 0:KC].bitcast(F32)).then_inc(stored, 16)
                sp.wait_ge(lo_ready, b * (KC + kc) + KC + kc)
                for g in range(P // (nk * HD)):
                    rows = slice(g * nk * HD, (g + 1) * nk * HD)
                    for part, buf in ((0, HI), (1, LO)):
                        sp.dma_start(k_d[one, :, g, part].rearrange("b c f n -> (b f) c n"),
                                     buf[rows, KC:KC + kc].bitcast(F32)).then_inc(stored, 16)
            sp.wait_ge(stored, 16 * NST * NB + 16)
            if gate:
                sp.wait_ge(sel_ready, 1)
                sp.dma_start(sel_d.rearrange("(a d) -> a d", a=1), SR[:]).then_inc(sel_stored, 16)
                sp.wait_ge(sel_stored, 16)

        @block.scalar
        def _(act):
            act.wait_ge(ones_set, 1)
            with act.Fori(0, NB) as b:
                nm.scalar_part(act, b)
                for t in range(NT):
                    act.wait_ge(turned, (b * NT + t) * 4 + 4)
                    act.wait_ge(qkv_psum, (b * NT + t + 1) * len(parts))
                    src = pA[:, t % 2, 2, 0:kw] if nk == GH else pA[:, t % 2, 1, kw:2 * kw]
                    act.activation(V[:, :, t, :, 0:HD], src.rearrange("p (g j d) -> p g j d", g=NG, j=nk),
                                   ACT.Copy).then_inc(v_ready, 1)
                    if gate:
                        act.wait_ge(cshift_ready, b * NT + t + 1)
                        act.activation(CX[:, t], pA[:, t % 2, 2, 0:NCL], ACT.Exp, bias=CN[:, t:t + 1], scale=10.0,
                                       accum_out=CS[:, t:t + 1]).then_inc(cexp_ready, 1)
                for c in range(KC + kc):
                    act.wait_ge(turn_psum, b * (KC + kc) + c + 1)
                    act.activation(HI[:, c], pT[:, c % 2], ACT.Copy).then_inc(hi_ready, 1)

        @block.gpsimd
        def _(pool):
            pool.wait_ge(w_in, NW * 16)
            pool.memset(V[:], 1.0).then_inc(ones_set, 1)
            nm.pool_setup(pool)
            with pool.Fori(0, NB) as b:
                nm.pool_part(pool, b)
                for t in range(NT):
                    for u, (at, width) in enumerate(((0, D), (D, kw))):
                        pool.wait_ge(turned, (b * NT + t) * 4 + 2 * u + 2)
                        h = width // NG // 2
                        c_, s_ = (ROT[:, t % 2, u, w, 0:width].rearrange("p (g a m) -> p g a m", g=NG, a=2)
                                  for w in (0, 1))
                        o_ = QR[:, t, at:at + width].rearrange("p (g a m) -> p g a m", g=NG, a=2)
                        pool.tensor_tensor(o_[:, :, 0], c_[:, :, 0], s_[:, :, 1], ALU.subtract).then_inc(rotated, 1)
                        pool.tensor_tensor(o_[:, :, 1], c_[:, :, 1], s_[:, :, 0], ALU.add).then_inc(rotated, 1)

        @block.vector
        def _(dve):
            dve.wait_ge(w_in, NW * 16)
            if gate:
                dve.memset(CP[:], 0.0).then_inc(chit_ready, 1)
            with dve.Fori(0, NB) as b:
                nm.vector_part(dve, b)
                for t in range(NT):
                    for u, width in enumerate((D, kw)):
                        dve.wait_ge(qkv_psum, (b * NT + t) * len(parts) + u + 1)
                        if t >= 2:
                            dve.wait_ge(rotated, (b * NT + t - 2) * 4 + 2 * u + 2)
                        src = pA[:, t % 2, u, 0:width].rearrange("p (m i j) -> p m i j", m=2 * NG, i=HD // 2)
                        for w, table in enumerate((COS, SIN)):
                            tab = table[:, t].unsqueeze(1).unsqueeze(3).to_broadcast(list(src.shape))
                            dve.tensor_tensor(
                                ROT[:, t % 2, u, w, 0:width].rearrange("p (m i j) -> p m i j", m=2 * NG, i=HD // 2),
                                src, tab, ALU.mult).then_inc(turned, 1)
                    if gate:
                        dve.wait_ge(logit_psum, b * NT + t + 1)
                        dve.tensor_reduce(CM[:, t:t + 1], pA[:, t % 2, 2, 0:NCL], AX_X, ALU.max).then_inc(cmax_ready, 1)
                        dve.wait_ge(cmax_ready, b * NT + t + 1)
                        dve.tensor_scalar(CN[:, t:t + 1], CM[:, t:t + 1], -10.0, None,
                                          ALU.mult).then_inc(cshift_ready, 1)
                if gate:
                    dve.wait_ge(cexp_ready, b * NT + NT)
                    dve.reciprocal(CR[:], CS[:]).then_inc(crec_ready, 1)
                    dve.wait_ge(crec_ready, b + 1)
                    for t in range(NT):
                        dve.wait_ge(chit_ready, b * NT + t + 1)
                        dve.scalar_tensor_tensor(CP[:], CX[:, t], CR[:, t:t + 1], CP[:], ALU.mult,
                                                 ALU.max).then_inc(chit_ready, 1)
                for c in range(KC + kc):
                    dve.wait_ge(hi_ready, b * (KC + kc) + c + 1)
                    dve.tensor_tensor(LO[:, c], pT[:, c % 2], HI[:, c].bitcast(F32), ALU.subtract).then_inc(lo_ready, 1)
            if gate:
                dve.wait_ge(best_psum, 1)
                dve.tensor_reduce(CT[:, 0:1], pT[0:NCL, 0, 0:P], AX_X, ALU.max).then_inc(hit_ready, 1)
                dve.wait_ge(hit_ready, 1)
                dve.tensor_scalar(CT[:, 1:2], CT[:, 0:1], 0.01, None, ALU.is_gt).then_inc(hit_ready, 1)
                dve.tensor_copy(AF[:], AI[:]).then_inc(asg_ready, 1)
                dve.wait_ge(asg_ready, 1)
                dve.tensor_scalar(AF[:], AF[:], CI[:], None, ALU.is_equal).then_inc(asg_ready, 1)
                dve.wait_ge(sel_psum, 1)
                dve.tensor_copy(SR[:], pT[0:1, 1]).then_inc(sel_ready, 1)

        @block.tensor
        def _(pe):
            pe.wait_ge(w_in, NW * 16)
            with pe.Fori(0, NB) as b:
                nm.tensor_part(pe, b)
                pe.wait_ge(nm.xt_ready, b * KC + KC)
                for t in range(NT):
                    if t >= 2:
                        pe.wait_ge(v_ready, b * NT + t - 1)
                        if gate:
                            pe.wait_ge(cexp_ready, b * NT + t - 1)
                    for n, (at, width) in enumerate(parts):
                        for c in range(KC):
                            ins = pe.matmul(pA[:, t % 2, n, 0:width], nm.xt[:, c, t * P:(t + 1) * P],
                                            W[:, c, at:at + width], start=(c == 0), stop=(c == KC - 1))
                        ins.then_inc(qkv_psum, 1)
                    if gate:
                        for c in range(KC):
                            ins = pe.matmul(pA[:, t % 2, 2, 0:NCL], nm.xt[:, c, t * P:(t + 1) * P], CE[:, c],
                                            start=(c == 0), stop=(c == KC - 1))
                        ins.then_inc(logit_psum, 1)
                for c in range(KC + kc):
                    if c >= 2:
                        pe.wait_ge(lo_ready, b * (KC + kc) + c - 1)
                    for t in range(NT):
                        if c == 0:
                            pe.wait_ge(rotated, (b * NT + t) * 4 + 4)
                        ins = pe.transpose(pT[:, c % 2, t * P:(t + 1) * P], QR[:, t, c * P:(c + 1) * P], ident[:])
                    ins.then_inc(turn_psum, 1)
                pe.wait_ge(lo_ready, (b + 1) * (KC + kc))
                if gate:
                    pe.wait_ge(cexp_ready, b * NT + NT)
            if gate:
                pe.wait_ge(chit_ready, 1 + NB * NT)
                pe.transpose(pT[0:NCL, 0, 0:P], CP[:], ident[:]).then_inc(best_psum, 1)
                pe.wait_ge(hit_ready, 2)
                pe.wait_ge(asg_ready, 2)
                pe.matmul(pT[0:1, 1], CT[:, 1:2], AF[:], start=True, stop=True).then_inc(sel_psum, 1)


def attend(nc, tag, nk, scratch, o_d, mask_q, mask_k, pick_d, ident_d):
    _, q_d, k_d, v_d = scratch
    NGR = NB * NG
    NBUF = 4
    OFF = [0, S, 2 * S - P, 3 * S - 3 * P]
    PTW = 4 * S - 6 * P
    with ExitStack() as ctx:
        def sb(name, shape, dt=F32):
            return ctx.enter_context(nc.sbuf_tensor(tag + name, shape, dt))

        def ps(name, shape, dt=F32):
            return ctx.enter_context(nc.psum_tensor(tag + name, shape, dt))

        sem = Semaphores(ctx, nc, tag)

        ident = sb("ident", [P, P])
        identb = sb("identb", [P, P], BF16)
        MF = sb("MF", [P, 2, P])
        MB = sb("MB", [P, 2, P], BF16)
        PICK = sb("PICK", [SM, GH * S])
        QS = [sb(f"QS{i}", [SM, GH, S], F32R) for i in range(NBUF)]
        KS = [sb(f"KS{i}", [SM, GH, S], F32R) for i in range(NBUF)]
        V = [sb(f"V{i}", [P, NT, nk, VW]) for i in range(2)]
        PT = [sb(f"PT{i}", [P, GH, PTW]) for i in range(2)]
        MX = sb("MX", [P, NT, GH])
        MN = sb("MN", [P, NT, 2 * GH], F32R)
        MR = [sb(f"MR{i}", [2 * GH, S], F32R) for i in range(2)]
        OV = sb("OV", [P, S])
        RC = sb("RC", [P, NT * GH])
        AO = [sb(f"AO{i}", [P, NT, GH, HD]) for i in range(2)]
        pS = ps("pS", [P, 2, 2, S])
        pX = ps("pX", [P, 2, S])
        pM = ps("pM", [P, S])
        pV = ps("pV", [P, S])

        c_in = sem("c_in")
        cast = sem("cast")
        ones_set = sem("ones_set")
        loaded = [sem(f"loaded{i}") for i in range(NBUF)]
        v_loaded = [sem("v_loaded_even"), sem("v_loaded_odd")]
        m_loaded = [sem("m_loaded_even"), sem("m_loaded_odd")]
        top_psum = sem("top_psum")
        top_ready = sem("top_ready")
        m_high = sem("m_high")
        m_split = sem("m_split")
        m_psum = sem("m_psum")
        m_ready = sem("m_ready")
        score_psum = sem("score_psum")
        exp_ready = sem("exp_ready")
        pv_done = sem("pv_done")
        ov_ready = sem("ov_ready")
        o_psum = sem("o_psum")
        rec_ready = sem("rec_ready")
        out_ready = sem("out_ready")
        o_stored = [sem("o_stored_even"), sem("o_stored_odd")]
        UNITS = 2 * NT
        TOPS = NT * GH
        AHEAD = GH
        NL = 6
        SCALE = HD ** -0.5

        block = ctx.enter_context(nc.Block())
        q_g = q_d.rearrange("b c h s (r j) n -> (b c h) (s r) (j n)", j=GH)
        k_g = k_d.rearrange("b c h s (r j) n -> (b c h) s r j n", j=nk)
        v_g = v_d.rearrange("b g p m -> (b g) p m")
        o_g = o_d.rearrange("b p t g m -> b g p t m")

        def pick(view, index):
            return view[bass.ds(index, 1)].rearrange("g p n -> (g p) n")

        def load_stacks(sp, i, G):
            for dup in range(2):
                sp.dma_start(QS[i][dup * 2 * HD:(dup + 1) * 2 * HD].bitcast(F32).rearrange("p j n -> p (j n)"),
                             pick(q_g, G)).then_inc(loaded[i], 16)
            for s in range(2):
                for dup in range(2):
                    at = (2 * s + dup) * HD
                    src = k_g[bass.ds(G, 1), s].rearrange("g r j n -> (g r) j n")
                    sp.dma_start(KS[i][at:at + HD].bitcast(F32),
                                 src.to_broadcast([HD, GH, S])).then_inc(loaded[i], 16)

        def load_v(sp, i, G):
            sp.dma_start(V[i][:].rearrange("p t j d -> p (t j d)"), pick(v_g, G)).then_inc(v_loaded[i], 16)

        def top_place(u):
            return NT - 1 - u // GH, u % GH


        @block.sync
        def _(sp):
            sp.dma_start(ident[:], ident_d).then_inc(c_in, 16)
            sp.dma_start(MF[:, 0], mask_q).then_inc(c_in, 16)
            sp.dma_start(MF[:, 1], mask_k).then_inc(c_in, 16)
            sp.dma_start(PICK[SW:SM], pick_d).then_inc(c_in, 16)
            for i in range(NBUF):
                load_stacks(sp, i, i)
            for i in range(2):
                load_v(sp, i, i)
                sp.sem_inc(o_stored[i], 16)
            with sp.Fori(0, NGR // NBUF) as r:
                n0 = NBUF * r
                next_s = [sp.snap((n0 + i + NBUF) % NGR) for i in range(NBUF)]
                next_v = [sp.snap((n0 + i + 2) % NGR) for i in range(NBUF)]
                place = [(sp.snap((n0 + i) // NG), sp.snap((n0 + i) % NG)) for i in range(NBUF)]
                for i in range(NBUF):
                    n = n0 + i
                    sp.wait_ge(score_psum, (n + 1) * UNITS)
                    load_stacks(sp, i, next_s[i])
                    sp.wait_ge(pv_done, n + 3)
                    load_v(sp, i % 2, next_v[i])
                    sp.wait_ge(out_ready, n + 2)
                    sp.dma_start(o_g[bass.ds(place[i][0], 1), bass.ds(place[i][1], 1)].rearrange("b g p t m -> (b g p) t m"),
                                 AO[i % 2][:].rearrange("p t j d -> p t (j d)")).then_inc(o_stored[i % 2], 16)
            for i in range(NBUF):
                sp.wait_ge(loaded[i], 16 * NL * (NGR // NBUF + 1))
            for i in range(2):
                sp.wait_ge(o_stored[i], 16 * (NGR // 2 + 1))
                sp.wait_ge(v_loaded[i], 16 * (NGR // 2 + 1))

        @block.scalar
        def _(act):
            act.sem_inc(exp_ready, 2)

            def maxima(i, n):
                act.wait_ge(m_psum, n + 1)
                act.activation(MR[i % 2][:], pM[0:2 * GH], ACT.Copy).then_inc(m_ready, 1)
                act.wait_ge(m_ready, n + 1)
                act.dma_start(QS[i][SM - 2 * GH:SM].bitcast(F32),
                              MR[i % 2][:].bitcast(F32).unsqueeze(1).to_broadcast([2 * GH, GH, S])
                              ).then_inc(m_loaded[i % 2], 16)

            maxima(0, 0)
            with act.Fori(0, NGR // NBUF) as r:
                for i in range(NBUF):
                    n = NBUF * r + i
                    act.wait_ge(pv_done, n + 1)
                    for u in range(UNITS):
                        j, hp = u // 2, u % 2
                        N = S - j * P
                        act.wait_ge(score_psum, n * UNITS + u + 1)
                        act.activation(PT[i % 2][:, 2 * hp:2 * hp + 2, OFF[j]:OFF[j] + N], pS[:, u % 2, :, 0:N],
                                       ACT.Exp, scale=SCALE).then_inc(exp_ready, 1)
                    maxima((i + 1) % NBUF, n + 1)
                    act.wait_ge(pv_done, n + 3)
                    act.activation(OV[:], pV[:], ACT.Copy).then_inc(ov_ready, 1)
            act.wait_ge(m_loaded[0], 16 * (NGR // 2 + 1))
            act.wait_ge(m_loaded[1], 16 * (NGR // 2))

        @block.vector
        def _(dve):
            dve.memset(pV[:], 0.0).then_inc(ones_set, 1)
            dve.wait_ge(c_in, 64)
            dve.tensor_copy(identb[:], ident[:]).then_inc(cast, 1)
            dve.tensor_copy(MB[:], MF[:]).then_inc(cast, 1)
            for i in range(NBUF):
                dve.tensor_copy(QS[i][SW:SM - 2 * GH].rearrange("p j n -> p (j n)"),
                                PICK[SW:SM - 2 * GH]).then_inc(ones_set, 1)
                dve.tensor_copy(KS[i][SW:SM].rearrange("p j n -> p (j n)"), PICK[SW:SM]).then_inc(ones_set, 1)
            dve.sem_inc(top_ready, 2)
            dve.sem_inc(out_ready, 1)

            def maxima(n, units):
                for u in units:
                    t, h = top_place(u)
                    dve.wait_ge(top_psum, n * TOPS + u + 1)
                    dve.tensor_reduce(MX[:, t, h:h + 1], pX[:, u % 2, 0:(t + 1) * P], AX_X,
                                      ALU.max).then_inc(top_ready, 1)

            def split(n):
                dve.wait_ge(top_ready, (n + 1) * TOPS + 2)
                dve.tensor_scalar(MN[:, :, 0:GH], MX[:], -1.0, None, ALU.mult).then_inc(m_high, 1)
                dve.wait_ge(m_high, n + 1)
                dve.scalar_tensor_tensor(MN[:, :, GH:2 * GH], MX[:], -1.0, MN[:, :, 0:GH].bitcast(F32), ALU.mult,
                                         ALU.subtract).then_inc(m_split, 1)

            maxima(0, range(TOPS))
            split(0)
            maxima(1, range(AHEAD))
            with dve.Fori(0, NGR // NBUF) as r:
                for i in range(NBUF):
                    n = NBUF * r + i
                    maxima(n + 1, range(AHEAD, TOPS))
                    split(n + 1)
                    maxima(n + 2, range(AHEAD))
                    dve.wait_ge(o_psum, n + 1)
                    sums = pM[:].rearrange("p (m d) -> p m d", d=2 * HD)
                    dve.reciprocal(RC[:], sums[:, :, HD]).then_inc(rec_ready, 1)
                    dve.wait_ge(rec_ready, n + 1)
                    dve.wait_ge(o_stored[i % 2], 16 * (2 * r + i // 2 + 1))
                    dve.tensor_tensor(AO[i % 2][:].rearrange("p t j d -> p (t j) d"), sums[:, :, 0:HD],
                                      RC[:].unsqueeze(2).to_broadcast([P, NT * GH, HD]),
                                      ALU.mult).then_inc(out_ready, 1)

        @block.tensor
        def _(pe):
            pe.sem_inc(pv_done, 2)
            pe.wait_ge(cast, 2)
            pe.wait_ge(c_in, 64)
            pe.wait_ge(ones_set, 2 * NBUF + 1)

            def tops(i, n, units):
                for u in units:
                    t, h = top_place(u)
                    N = (t + 1) * P
                    pe.wait_ge(top_ready, n * TOPS + u + 1)
                    pe.matmul(pX[:, u % 2, 0:N], QS[i][0:SM - 2 * GH, h, t * P:N], KS[i][0:SM - 2 * GH, h, 0:N],
                              start=True, stop=False)
                    pe.matmul(pX[:, u % 2, t * P:N], identb[:], MB[:, 0], start=False, stop=True).then_inc(top_psum, 1)

            def score_unit(i, n, u):
                j, hp = u // 2, u % 2
                N = S - j * P
                pe.wait_ge(exp_ready, n * UNITS + u + 1)
                for e in range(2):
                    h = 2 * hp + e
                    pe.matmul(pS[:, u % 2, e, 0:N], KS[i][:, h, j * P:(j + 1) * P],
                              QS[i][:, h, j * P:S], start=True, stop=False)
                    ins = pe.matmul(pS[:, u % 2, e, 0:P], identb[:], MB[:, 1], start=False, stop=True)
                ins.then_inc(score_psum, 1)

            def turn_maxima(n):
                pe.wait_ge(m_split, n + 1)
                for t in range(NT):
                    ins = pe.transpose(pM[0:2 * GH, t * P:(t + 1) * P], MN[:, t].bitcast(F32), ident[:])
                ins.then_inc(m_psum, 1)

            def values(i, j):
                for h in range(GH):
                    at = 2 * HD * h
                    ins = pe.matmul(pV[at:at + VW, j * P:S], V[i % 2][:, j, h if nk == GH else 0],
                                    PT[i % 2][:, h, OFF[j]:OFF[j] + S - j * P], start=(j == 0), stop=(j == NT - 1))
                return ins

            pe.wait_ge(loaded[0], 16 * NL)
            tops(0, 0, range(TOPS))
            turn_maxima(0)
            pe.wait_ge(loaded[1], 16 * NL)
            tops(1, 1, range(AHEAD))
            with pe.Fori(0, NGR // NBUF) as r:
                for i in range(NBUF):
                    n = NBUF * r + i
                    i1, i2 = (i + 1) % NBUF, (i + 2) % NBUF
                    pe.wait_ge(m_loaded[i % 2], 16 * (2 * r + i // 2 + 1))
                    for u in range(UNITS):
                        score_unit(i, n, u)
                        tops(i1, n + 1, range(AHEAD + 2 * u, min(AHEAD + 2 * u + 2, TOPS)))
                    pe.wait_ge(v_loaded[i % 2], 16 * (2 * r + i // 2 + 1))
                    for j in range(2):
                        pe.wait_ge(exp_ready, n * UNITS + 2 * j + 4)
                        values(i, j)
                    pe.wait_ge(out_ready, n + 1)
                    turn_maxima(n + 1)
                    pe.wait_ge(exp_ready, (n + 1) * UNITS + 2)
                    values(i, 2)
                    values(i, 3).then_inc(pv_done, 1)
                    pe.wait_ge(loaded[i2], 16 * NL * (r + 1 + (i + 2) // NBUF))
                    tops(i2, n + 2, range(AHEAD))
                    pe.wait_ge(ov_ready, n + 1)
                    for t in range(NT):
                        ins = pe.transpose(pM[:, t * P:(t + 1) * P], OV[:, t * P:(t + 1) * P], ident[:])
                    ins.then_inc(o_psum, 1)


def finish2(nc, x_in, x_out, xt_d, o_d, sel_d, wo, w2, b2, ident_d):
    with ExitStack() as ctx:
        def sb(name, shape, dt=F32):
            return ctx.enter_context(nc.sbuf_tensor("e_" + name, shape, dt))

        def ps(name, shape, dt=F32):
            return ctx.enter_context(nc.psum_tensor("e_" + name, shape, dt))

        sem = Semaphores(ctx, nc, "e_")

        x_v = x_in.rearrange("b (t p) d -> b p t d", p=P)
        y_v = x_out.rearrange("b (t p) d -> b p t d", p=P)
        ident = sb("ident", [P, P])
        WO = sb("WO", [P, KC, D])
        W = sb("W", [P, KC, D])
        BB = sb("BB", [P, D])
        SB = sb("SB", [P, D])
        X = sb("X", [P, 2, NT, D])
        XT = [sb(f"XT{i}", [P, KC, S]) for i in range(2)]
        O = [sb(f"O{i}", [P, NT, D]) for i in range(2)]
        OT = sb("OT", [P, KC, S])
        pT = ps("pT", [P, 2, S])
        pO = ps("pO", [P, NT, S])
        w_in = sem("w_in")
        w_ready = sem("w_ready")
        loaded = [sem("loaded_even"), sem("loaded_odd")]
        ot_psum = sem("ot_psum")
        ot_ready = sem("ot_ready")
        out_psum = sem("out_psum")
        xb_ready = sem("xb_ready")
        y_ready = sem("y_ready")
        y_stored = [sem("y_stored_even"), sem("y_stored_odd")]
        block = ctx.enter_context(nc.Block())

        @block.sync
        def _(sp):
            sp.dma_start(ident[:], ident_d).then_inc(w_in, 16)
            sp.dma_start(BB[:], b2.partition_broadcast(P)).then_inc(w_in, 16)
            sp.dma_start(SB[:], sel_d.partition_broadcast(P)).then_inc(w_in, 16)
            sp.dma_start(W[:], w2).then_inc(w_in, 16)
            sp.dma_start(WO[:], wo).then_inc(w_in, 16)
            for i in range(2):
                sp.sem_inc(y_stored[i], 16)
            with sp.Fori(0, NB // 2) as r:
                for i in range(2):
                    one = bass.ds(2 * r + i, 1)
                    sp.wait_ge(y_stored[i], 16 * (r + 1))
                    sp.dma_start(O[i][:], o_d[one].rearrange("b p t g m -> (b p) t (g m)")).then_inc(loaded[i], 16)
                    sp.dma_start(XT[i][:], xt_d[one].rearrange("b p c n -> (b p) c n")).then_inc(loaded[i], 16)
                    sp.dma_start(X[:, i], x_v[one].rearrange("b p t d -> (b p) t d")).then_inc(loaded[i], 16)

        @block.scalar
        def _(act):
            with act.Fori(0, NB // 2) as r:
                for i in range(2):
                    n = 2 * r + i
                    for c in range(KC):
                        act.wait_ge(ot_psum, n * KC + c + 1)
                        act.activation(OT[:, c], pT[:, c % 2], ACT.Copy).then_inc(ot_ready, 1)
                    act.wait_ge(y_ready, n * NT + NT)
                    act.dma_start(y_v[bass.ds(n, 1)].rearrange("b p t d -> (b p) t d"),
                                  X[:, i]).then_inc(y_stored[i], 16)
            for i in range(2):
                act.wait_ge(y_stored[i], 16 * (NB // 2 + 1))

        @block.gpsimd
        def _(pool):
            pool.wait_ge(w_ready, KC + 1)
            with pool.Fori(0, NB // 2) as r:
                for i in range(2):
                    pool.wait_ge(loaded[i], 48 * (r + 1))
                    for t in range(NT):
                        pool.tensor_tensor(X[:, i, t], X[:, i, t], BB[:], ALU.add).then_inc(xb_ready, 1)

        @block.vector
        def _(dve):
            dve.wait_ge(w_in, 80)
            for c in range(KC):
                dve.tensor_tensor(W[:, c], W[:, c], SB[:], ALU.mult).then_inc(w_ready, 1)
            dve.tensor_tensor(BB[:], BB[:], SB[:], ALU.mult).then_inc(w_ready, 1)
            with dve.Fori(0, NB // 2) as r:
                for i in range(2):
                    n = 2 * r + i
                    for t in range(NT):
                        dve.wait_ge(out_psum, n * NT + t + 1)
                        dve.wait_ge(xb_ready, n * NT + t + 1)
                        dve.tensor_tensor(X[:, i, t], X[:, i, t], pO[:, t], ALU.add).then_inc(y_ready, 1)

        @block.tensor
        def _(pe):
            pe.wait_ge(w_ready, KC + 1)
            pe.wait_ge(w_in, 80)
            with pe.Fori(0, NB // 2) as r:
                for i in range(2):
                    n = 2 * r + i
                    pe.wait_ge(loaded[i], 48 * (r + 1))
                    for c in range(KC):
                        if c >= 2:
                            pe.wait_ge(ot_ready, n * KC + c - 1)
                        for t in range(NT):
                            ins = pe.transpose(pT[:, c % 2, t * P:(t + 1) * P], O[i][:, t, c * P:(c + 1) * P], ident[:])
                        ins.then_inc(ot_psum, 1)
                    for t in range(NT):
                        for c in range(KC):
                            pe.matmul(pO[:, t], XT[i][:, c, t * P:(t + 1) * P], W[:, c], start=(c == 0), stop=False)
                    pe.wait_ge(ot_ready, n * KC + KC)
                    for t in range(NT):
                        for c in range(KC):
                            ins = pe.matmul(pO[:, t], OT[:, c, t * P:(t + 1) * P], WO[:, c], start=False,
                                            stop=(c == KC - 1))
                        ins.then_inc(out_psum, 1)
                    pe.wait_ge(y_ready, n * NT + NT)


def layer2(nc, x_in, x_out, wqkv, cos_d, sin_d, cent, asg, cidx, wo, w2, b2, mask_q, mask_k, pick_d, ident_d, nk=1):
    kw = NG * nk * HD
    xt_d = nc.dram_tensor("c_xt", (NB, P, KC, S), F32).ap()
    q_d = nc.dram_tensor("c_q", (NB, KC, 2, 2, GW, S), F32).ap()
    k_d = nc.dram_tensor("c_k", (NB, kw // P, P // (nk * HD), 2, nk * HD, S), F32).ap()
    v_d = nc.dram_tensor("c_v", (NB, NG, P, NT * nk * VW), F32).ap()
    o_d = nc.dram_tensor("c_o", (NB, P, NT, NG, GW), F32).ap()
    sel_d = nc.dram_tensor("c_sel", (D,), F32).ap()
    scratch = (xt_d, q_d, k_d, v_d)
    project(nc, "c_", nk, x_in, scratch, wqkv, cos_d, sin_d, ident_d, gate=(cent, asg, cidx, sel_d))
    attend(nc, "d_", nk, scratch, o_d, mask_q, mask_k, pick_d, ident_d)
    finish2(nc, x_in, x_out, xt_d, o_d, sel_d, wo, w2, b2, ident_d)

NE3 = 16
NX = NE3 + 2
GC = 96
NGE, EG3 = 4, 4
WE = 2 * D + D + 2
TT = NB * NT
TOPK = 2
NBLK = (TOPK * NB * S + NE3 * (P - 1)) // P + 1
NBX = NBLK + 2
FAR = 65536.0


def route(nc, keep, x_in, xt_d, o_d, base_d, tab_d, wo, wr, rb, rbias, ws, eb3, w12, w3, b12, ident_d):
    W12, W3, B12, GATES, CHOSEN = keep
    with ExitStack() as ctx:
        def sb(name, shape, dt=F32):
            return ctx.enter_context(nc.sbuf_tensor("h_" + name, shape, dt))

        def ps(name, shape, dt=F32):
            return ctx.enter_context(nc.psum_tensor("h_" + name, shape, dt))

        sem = Semaphores(ctx, nc, "h_")

        x_v = x_in.rearrange("b (t p) d -> b p t d", p=P)
        base_v = base_d.rearrange("(b t p) d -> b p t d", p=P, t=NT)
        ident = sb("ident", [P, P])
        WO = sb("WO", [P, KC, D])
        WR = sb("WR", [P, KC, NE3])
        RB = sb("RB", [P, NE3])
        RBIAS = sb("RBIAS", [P, NE3])
        EB3 = sb("EB3", [GC, D])
        WS = sb("WS", [P, 2, WE])
        X = sb("X", [P, NT, D])
        XT = sb("XT", [P, KC, S])
        O = sb("O", [P, NT, D])
        OT = sb("OT", [P, KC, S])
        ZERO = sb("ZERO", [NBX, P])
        LG = sb("LG", [P, NT, NE3])
        MX = sb("MX", [P, NT])
        EX = sb("EX", [P, NT, NE3])
        SM3 = sb("SM3", [P, NT])
        RC = sb("RC", [P, NT])
        SC = sb("SC", [P, NT, NE3])
        GM = sb("GM", [P, NT, NGE + 6])
        GR = sb("GR", [P, NT, NGE + 6])
        TG = sb("TG", [P, NT, 8])
        PEN = sb("PEN", [P, NT, NGE])
        MS = sb("MS", [P, NT, NE3 + 6])
        MRP = sb("MRP", [P, NT, NE3 + 6])
        TE = sb("TE", [P, NT, 8])
        GT = sb("GT", [P, NT, GC])
        GTT = sb("GTT", [GC, S])
        A = sb("A", [P, S])
        H = sb("H", [P, 2, S])
        HOLD = sb("HOLD", [P, 1])
        pH = ps("pH", [P, 2, S])
        pT = ps("pT", [P, 2, S])
        pY = ps("pY", [P, NT, S])

        w_in = sem("w_in")
        experts_in = sem("experts_in")
        pads_set = sem("pads_set")
        zero_stored = sem("zero_stored")
        x_loaded = sem("x_loaded")
        xt_loaded = sem("xt_loaded")
        o_loaded = sem("o_loaded")
        y_stored = sem("y_stored")
        logit_psum = sem("logit_psum")
        route_step = sem("route_step")
        shift_ready = sem("shift_ready")
        exp_ready = sem("exp_ready")
        gmax_ready = sem("gmax_ready")
        masked_ready = sem("masked_ready")
        gate_ready = sem("gate_ready")
        ot_psum = sem("ot_psum")
        ot_ready = sem("ot_ready")
        gt_psum = sem("gt_psum")
        gt_ready = sem("gt_ready")
        h_psum = sem("h_psum")
        act_ready = sem("act_ready")
        h_ready = sem("h_ready")
        y_psum = sem("y_psum")
        y_ready = sem("y_ready")
        ROUTE = 11
        block = ctx.enter_context(nc.Block())

        @block.sync
        def _(sp):
            sp.dma_start(ident[:], ident_d).then_inc(w_in, 16)
            sp.dma_start(RB[:], rb.partition_broadcast(P)).then_inc(w_in, 16)
            sp.dma_start(RBIAS[:], rbias.partition_broadcast(P)).then_inc(w_in, 16)
            sp.dma_start(EB3[:], eb3).then_inc(w_in, 16)
            sp.dma_start(WR[:], wr).then_inc(w_in, 16)
            sp.dma_start(WS[:], ws).then_inc(w_in, 16)
            sp.dma_start(WO[:], wo).then_inc(w_in, 16)
            with sp.Fori(0, NB) as b:
                one = bass.ds(b, 1)
                sp.wait_ge(y_stored, b * 16 + 16)
                sp.dma_start(X[:], x_v[one].rearrange("b p t d -> (b p) t d")).then_inc(x_loaded, 16)
                sp.wait_ge(y_ready, b * NT + NT)
                sp.dma_start(base_v[one].rearrange("b p t d -> (b p) t d"), X[:]).then_inc(y_stored, 16)
            sp.wait_ge(y_stored, 16 * NB + 16)

        @block.scalar
        def _(act):
            act.sem_inc(y_stored, 16)
            act.sem_inc(h_psum, 2)
            act.sem_inc(ot_psum, KC)
            with act.Fori(0, NB) as b:
                one = bass.ds(b, 1)
                act.wait_ge(h_psum, b * 2 + 2)
                act.dma_start(XT[:], xt_d[one].rearrange("b p c n -> (b p) c n")).then_inc(xt_loaded, 16)
                act.wait_ge(ot_psum, b * KC + KC)
                act.dma_start(O[:], o_d[one].rearrange("b p t g m -> (b p) t (g m)")).then_inc(o_loaded, 16)
                for t in range(NT):
                    act.wait_ge(shift_ready, b + 1)
                    act.activation(EX[:, t], LG[:, t], ACT.Exp, bias=MX[:, t:t + 1],
                                   accum_out=SM3[:, t:t + 1]).then_inc(exp_ready, 1)
                for s in range(2):
                    act.wait_ge(h_psum, b * 2 + s + 3)
                    act.activation(A[:], pH[:, 0], ACT.Silu, bias=WS[:, s, WE - 2:WE - 1]).then_inc(act_ready, 1)
                    if s == 0:
                        for c in range(KC):
                            act.wait_ge(ot_psum, b * KC + KC + c + 1)
                            act.activation(OT[:, c], pT[:, (c + 1) % 2], ACT.Copy).then_inc(ot_ready, 1)
                            if c == 1:
                                act.wait_ge(h_ready, b * 2 + 1)

        @block.gpsimd
        def _(pool):
            pool.dma_start(W12[:], w12).then_inc(experts_in, 16)
            pool.dma_start(W3[:], w3).then_inc(experts_in, 16)
            pool.dma_start(B12[:], b12.partition_broadcast(P)).then_inc(experts_in, 16)
            pool.memset(GM[:, :, NGE:], BIG).then_inc(pads_set, 1)
            pool.memset(MS[:, :, NE3:], BIG).then_inc(pads_set, 1)
            pool.memset(GT[:, :, NE3:NX], 1.0).then_inc(pads_set, 1)
            pool.memset(GT[:, :, NX:], 0.0).then_inc(pads_set, 1)
            pool.memset(ZERO[:], 0.0).then_inc(pads_set, 1)
            pool.wait_ge(pads_set, 5)
            pool.dma_start(tab_d.rearrange("(k p) a -> k (p a)", p=P), ZERO[:]).then_inc(zero_stored, 16)
            pool.wait_ge(zero_stored, 16)
            pool.wait_ge(experts_in, 48)

        @block.vector
        def _(dve):
            dve.wait_ge(pads_set, 5)
            dve.wait_ge(w_in, 112)
            with dve.Fori(0, NB) as b:
                one = bass.ds(b, 1)
                link = Chain(dve, route_step, ROUTE, b)

                def gated(s):
                    dve.wait_ge(act_ready, b * 2 + s + 1)
                    dve.scalar_tensor_tensor(H[:, s], pH[:, 1], WS[:, s, WE - 1:WE], A[:], ALU.add,
                                             ALU.mult).then_inc(h_ready, 1)

                dve.wait_ge(logit_psum, b + 1)
                lg = pT[:, 0, 0:NT * NE3].rearrange("p (t e) -> p t e", t=NT)
                link(dve.tensor_tensor(LG[:], lg, RB[:].unsqueeze(1).to_broadcast([P, NT, NE3]), ALU.add))
                link(dve.tensor_reduce(MX[:], LG[:], AX_X, ALU.max))
                dve.tensor_scalar(MX[:], MX[:], -1.0, None, ALU.mult).then_inc(shift_ready, 1)
                dve.wait_ge(exp_ready, b * NT + NT)
                link(dve.reciprocal(RC[:], SM3[:]))
                for t in range(NT):
                    link(dve.scalar_tensor_tensor(SC[:, t], EX[:, t], RC[:, t:t + 1], RBIAS[:], ALU.mult, ALU.add))
                link(dve.tensor_reduce(GM[:, :, 0:NGE], SC[:].rearrange("p t (g e) -> p t g e", g=NGE), AX_X,
                                       ALU.max))
                gated(0)
                dve.memset(HOLD[:], 0.0)
                for t in range(NT):
                    dve.max(TG[:, t], GM[:, t]).then_inc(gmax_ready, 1)
                dve.wait_ge(gmax_ready, b * 2 * NT + NT)
                dve.memset(HOLD[:], 0.0)
                for t in range(NT):
                    dve.match_replace(GR[:, t], TG[:, t], GM[:, t], -BIG).then_inc(gmax_ready, 1)
                dve.wait_ge(gmax_ready, b * 2 * NT + 2 * NT)
                link(dve.tensor_tensor(PEN[:], GR[:, :, 0:NGE], GM[:, :, 0:NGE], ALU.not_equal))
                link(dve.tensor_scalar(PEN[:], PEN[:], BIG, -BIG, ALU.mult, ALU.add))
                for t in range(NT):
                    dve.tensor_tensor(MS[:, t, 0:NE3].rearrange("p (g e) -> p g e", g=NGE),
                                      SC[:, t].rearrange("p (g e) -> p g e", g=NGE),
                                      PEN[:, t].unsqueeze(2).to_broadcast([P, NGE, EG3]),
                                      ALU.add).then_inc(masked_ready, 1)
                dve.wait_ge(masked_ready, b * 3 * NT + NT)
                dve.memset(HOLD[:], 0.0)
                for t in range(NT):
                    dve.max(TE[:, t], MS[:, t]).then_inc(masked_ready, 1)
                dve.wait_ge(masked_ready, b * 3 * NT + 2 * NT)
                dve.memset(HOLD[:], 0.0)
                for t in range(NT):
                    dve.match_replace(MRP[:, t], TE[:, t], MS[:, t], -BIG).then_inc(masked_ready, 1)
                dve.wait_ge(masked_ready, b * 3 * NT + 3 * NT)
                chosen = CHOSEN[:, one].rearrange("p b t e -> p (b t) e")
                gates = GATES[:, one].rearrange("p b t e -> p (b t) e")
                link(dve.tensor_tensor(chosen, MRP[:, :, 0:NE3], MS[:, :, 0:NE3], ALU.not_equal))
                dve.tensor_tensor(GT[:, :, 0:NE3], chosen, SC[:], ALU.mult).then_inc(gate_ready, 1)
                dve.tensor_tensor(gates, chosen, SC[:], ALU.mult).then_inc(gate_ready, 1)
                gated(1)
                dve.wait_ge(gt_psum, b + 1)
                dve.tensor_copy(GTT[:], pT[0:GC, 0]).then_inc(gt_ready, 1)
                dve.wait_ge(x_loaded, 16 * (b + 1))
                for t in range(NT):
                    dve.wait_ge(y_psum, b * NT + t + 1)
                    dve.tensor_tensor(X[:, t], X[:, t], pY[:, t], ALU.add).then_inc(y_ready, 1)
                link.end()

        @block.tensor
        def _(pe):
            pe.wait_ge(w_in, 112)
            with pe.Fori(0, NB) as b:
                def up(s):
                    for w in range(2):
                        for c in range(KC):
                            at = (w * KC + c) * P
                            ins = pe.matmul(pH[:, w], WS[:, s, at:at + P], XT[:, c], start=(c == 0),
                                            stop=(c == KC - 1))
                    ins.then_inc(h_psum, 1)

                pe.wait_ge(xt_loaded, 16 * (b + 1))
                for t in range(NT):
                    for c in range(KC):
                        ins = pe.matmul(pT[:, 0, t * NE3:(t + 1) * NE3], XT[:, c, t * P:(t + 1) * P], WR[:, c],
                                        start=(c == 0), stop=(c == KC - 1))
                ins.then_inc(logit_psum, 1)
                up(0)
                pe.wait_ge(o_loaded, 16 * (b + 1))
                for c in range(KC):
                    if c == 1:
                        pe.wait_ge(route_step, b * ROUTE + 1)
                    if c >= 2:
                        pe.wait_ge(ot_ready, b * KC + c - 1)
                    for t in range(NT):
                        ins = pe.transpose(pT[:, (c + 1) % 2, t * P:(t + 1) * P], O[:, t, c * P:(c + 1) * P], ident[:])
                    ins.then_inc(ot_psum, 1)
                pe.wait_ge(h_ready, b * 2 + 1)
                up(1)
                pe.wait_ge(ot_ready, b * KC + KC)
                for t in range(NT):
                    for c in range(KC):
                        pe.matmul(pY[:, t], OT[:, c, t * P:(t + 1) * P], WO[:, c], start=(c == 0), stop=False)
                pe.wait_ge(gate_ready, 2 * b + 2)
                for t in range(NT):
                    ins = pe.transpose(pT[0:GC, 0, t * P:(t + 1) * P], GT[:, t], ident[:])
                ins.then_inc(gt_psum, 1)
                pe.wait_ge(h_ready, b * 2 + 2)
                for t in range(NT):
                    for s in range(2):
                        pe.matmul(pY[:, t], H[:, s, t * P:(t + 1) * P], WS[:, s, 2 * D:3 * D], start=False, stop=False)
                pe.wait_ge(gt_ready, b + 1)
                for t in range(NT):
                    pe.matmul(pY[:, t], GTT[:, t * P:(t + 1) * P], EB3[:], start=False,
                              stop=True).then_inc(y_psum, 1)
                pe.wait_ge(y_ready, b * NT + NT)


def place(nc, keep, places, tab_d, tri, le, kx, tid, ident_d):
    GATES, CHOSEN = keep
    SLOT, GATE, TOKEN, EXPERT = places
    with ExitStack() as ctx:
        def sb(name, shape, dt=F32):
            return ctx.enter_context(nc.sbuf_tensor("i_" + name, shape, dt))

        def ps(name, shape, dt=F32):
            return ctx.enter_context(nc.psum_tensor("i_" + name, shape, dt))

        sem = Semaphores(ctx, nc, "i_")

        EE = NE3 * NE3
        ident = sb("ident", [P, P])
        TRI = sb("TRI", [P, P])
        ONES = sb("ONES", [P, P])
        LE = sb("LE", [P, NE3, NE3])
        KX = sb("KX", [P, NBX])
        TID = sb("TID", [P, TT])
        COUNT = sb("COUNT", [P, NE3])
        FULL = sb("FULL", [P, NE3])
        CMP = sb("CMP", [P, NE3, NE3])
        BLOCKS = sb("BLOCKS", [P, NE3])
        CUM = sb("CUM", [P, NE3, NE3])
        END = sb("END", [P, NE3])
        FIRST = sb("FIRST", [P, NE3])
        ALL = sb("ALL", [P, TT, NE3])
        OWN = sb("OWN", [P, TT, NE3])
        EQ = sb("EQ", [P, TT, NE3])
        SF = sb("SF", [P, TOPK, TT])
        PAST = sb("PAST", [1, NBX, NE3])
        EF = sb("EF", [1, NBX])
        TAB = sb("TAB", [NBX, P])
        pR = ps("pR", [P, S])
        pC = ps("pC", [P, S])
        pTab = ps("pTab", [P, S])
        w_in = sem("w_in")
        ones_set = sem("ones_set")
        rank_psum = sem("rank_psum")
        step = sem("step")
        slot_ready = sem("slot_ready")
        expert_ready = sem("expert_ready")
        scattered = sem("scattered")
        tab_loaded = sem("tab_loaded")
        tab_psum = sem("tab_psum")
        token_ready = sem("token_ready")
        block = ctx.enter_context(nc.Block())
        chosen = CHOSEN[:].rearrange("p b t e -> p (b t) e")
        gates = GATES[:].rearrange("p b t e -> p (b t) e")

        @block.sync
        def _(sp):
            for buf, src in ((ident, ident_d), (TRI, tri), (LE, le), (KX, kx), (TID, tid)):
                sp.dma_start(buf[:], src).then_inc(w_in, 16)
            sp.wait_ge(scattered, 16 * TOPK * TT)
            sp.dma_start(TAB[:], tab_d.rearrange("(k p) a -> k (p a)", p=P)).then_inc(tab_loaded, 16)

        @block.gpsimd
        def _(pool):
            pool.memset(ONES[:], 1.0).then_inc(ones_set, 1)
            pool.wait_ge(w_in, 80)
            pool.wait_ge(slot_ready, 1)
            for k in range(TOPK):
                for t in range(TT):
                    pool.indirect_dma_start(tab_d, bass.IndirectOffsetOnAxis(ap=SLOT[:, k, t:t + 1], axis=0),
                                            TID[:, t:t + 1], None).then_inc(scattered, 16)

        @block.tensor
        def _(pe):
            pe.wait_ge(w_in, 80)
            pe.wait_ge(ones_set, 1)
            pe.matmul(pR[:, 0:TT * NE3], TRI[:], chosen, start=True, stop=False)
            for t in range(TT - 1):
                later = TT - 1 - t
                pe.matmul(pR[:, (t + 1) * NE3:TT * NE3], ONES[:],
                          chosen[:, t].unsqueeze(1).to_broadcast([P, later, NE3]), start=False, stop=(t == TT - 2))
            pe.matmul(pC[:, 0:TT * NE3], ONES[:], chosen, start=True, stop=True).then_inc(rank_psum, 1)
            pe.wait_ge(tab_loaded, 16)
            pe.transpose(pTab[:, 0:NBX], TAB[:], ident[0:NBX, 0:NBX]).then_inc(tab_psum, 1)

        @block.vector
        def _(dve):
            link = Chain(dve, step)
            dve.wait_ge(w_in, 80)
            dve.wait_ge(rank_psum, 1)
            link(dve.tensor_reduce(COUNT[:], pC[:, 0:TT * NE3].rearrange("p (t e) -> p e t", t=TT), AX_X, ALU.add))
            link(dve.tensor_scalar(FULL[:], KX[:, 0:NE3], float(P), None, ALU.mult))
            link(dve.tensor_tensor(CMP[:], COUNT[:].unsqueeze(2).to_broadcast([P, NE3, NE3]),
                                   FULL[:].unsqueeze(1).to_broadcast([P, NE3, NE3]), ALU.is_gt))
            link(dve.tensor_reduce(BLOCKS[:], CMP[:], AX_X, ALU.add))
            link(dve.tensor_tensor(CUM[:], LE[:], BLOCKS[:].unsqueeze(1).to_broadcast([P, NE3, NE3]), ALU.mult))
            link(dve.tensor_reduce(END[:], CUM[:], AX_X, ALU.add))
            link(dve.tensor_tensor(FIRST[:], END[:], BLOCKS[:], ALU.subtract))
            link(dve.tensor_scalar(FIRST[:], FIRST[:], float(P), None, ALU.mult))
            link(dve.tensor_tensor(ALL[:], pR[:, 0:TT * NE3].rearrange("p (t e) -> p t e", t=TT),
                                   FIRST[:].unsqueeze(1).to_broadcast([P, TT, NE3]), ALU.add))
            link(dve.scalar_tensor_tensor(OWN[:], chosen, -FAR, ALL[:], ALU.mult, ALU.add))
            link(dve.tensor_reduce(SF[:, 0], OWN[:], AX_X, ALU.min))
            link(dve.tensor_scalar(SF[:, 0], SF[:, 0], FAR, None, ALU.add))
            link(dve.tensor_tensor(OWN[:], chosen, ALL[:], ALU.mult))
            link(dve.tensor_reduce(SF[:, 1], OWN[:], AX_X, ALU.max))
            dve.tensor_copy(SLOT[:], SF[:]).then_inc(slot_ready, 1)
            link(dve.tensor_tensor(PAST[:], END[0:1].unsqueeze(1).to_broadcast([1, NBX, NE3]),
                                   KX[0:1].unsqueeze(2).to_broadcast([1, NBX, NE3]), ALU.is_le))
            link(dve.tensor_reduce(EF[:], PAST[:], AX_X, ALU.add))
            link(dve.tensor_scalar(EF[:], EF[:], float(NE3 - 1), None, ALU.min))
            dve.tensor_copy(EXPERT[:], EF[:]).then_inc(expert_ready, 1)
            for k in range(TOPK):
                link(dve.tensor_tensor(EQ[:], ALL[:], SF[:, k].unsqueeze(2).to_broadcast([P, TT, NE3]), ALU.is_equal))
                link(dve.tensor_tensor(EQ[:], EQ[:], gates, ALU.mult))
                link(dve.tensor_reduce(GATE[:, k], EQ[:], AX_X, ALU.add))
            dve.wait_ge(tab_psum, 1)
            dve.tensor_copy(TOKEN[:], pTab[:, 0:NBX]).then_inc(token_ready, 1)


def carry_wait(pool, hold, at):
    pool.tensor_tensor(hold[:, at:at + 1], hold[:, 0:1], hold[:, 0:1], ALU.add)


def experts(nc, keep, places, xn_d, ys_d, ident_d):
    W12, W3, B12 = keep
    TOKEN, EXPERT = places
    UN = 4
    with ExitStack() as ctx:
        def sb(name, shape, dt=F32):
            return ctx.enter_context(nc.sbuf_tensor("j_" + name, shape, dt))

        def ps(name, shape, dt=F32):
            return ctx.enter_context(nc.psum_tensor("j_" + name, shape, dt))

        sem = Semaphores(ctx, nc, "j_")

        ident = sb("ident", [P, P])
        X = [sb(f"X{i}", [P, D]) for i in range(UN)]
        IX = [sb(f"IX{i}", [P, 1], I32) for i in range(UN)]
        HOLD = sb("HOLD", [1, 3])
        XT = [sb(f"XT{i}", [P, KC, P]) for i in range(2)]
        U = sb("U", [P, 2, 2, P])
        A = sb("A", [P, 2, P])
        H = sb("H", [P, 2, P])
        HT = sb("HT", [P, 2, P])
        Y = [sb(f"Y{i}", [P, D]) for i in range(2)]
        pT = ps("pT", [P, 2, S])
        pU = ps("pU", [P, 2, S])
        pHT = ps("pHT", [P, 2, S])
        pY = ps("pY", [P, 2, S])
        w_in = sem("w_in")
        gathered = [sem(f"gathered{i}") for i in range(UN)]
        ix_ready = sem("ix_ready")
        xt_psum = sem("xt_psum")
        xt_ready = sem("xt_ready")
        u_psum = sem("u_psum")
        u_ready = sem("u_ready")
        a_ready = sem("a_ready")
        h_ready = sem("h_ready")
        ht_psum = sem("ht_psum")
        ht_ready = sem("ht_ready")
        y_psum = sem("y_psum")
        y_ready = sem("y_ready")
        stored = [sem("stored_even"), sem("stored_odd")]
        ys_v = ys_d.rearrange("(k p) d -> k p d", p=P)
        block = ctx.enter_context(nc.Block())

        @block.sync
        def _(sp):
            sp.dma_start(ident[:], ident_d).then_inc(w_in, 16)
            for i in range(2):
                sp.sem_inc(stored[i], 16)
            with sp.Fori(0, NBLK // UN) as r:
                for i in range(UN):
                    n = UN * r + i
                    sp.wait_ge(y_ready, n + 3)
                    sp.dma_start(ys_v[bass.ds(n, 1)].rearrange("k p d -> (k p) d"),
                                 Y[i % 2][:]).then_inc(stored[i % 2], 16)
            for i in range(2):
                sp.wait_ge(stored[i], 16 * (NBLK // 2 + 1))

        @block.gpsimd
        def _(pool):
            def gather(i, n):
                pool.tensor_copy(IX[i][:], TOKEN[:, bass.ds(n, 1)]).then_inc(ix_ready, 1)
                pool.wait_ge(ix_ready, n + 2)
                carry_wait(pool, HOLD, 2)
                pool.indirect_dma_start(X[i][:], None, xn_d, bass.IndirectOffsetOnAxis(ap=IX[i][:], axis=0)
                                        ).then_inc(gathered[i], 16)

            pool.memset(HOLD[:], 0.0).then_inc(ix_ready, 1)
            pool.wait_ge(ix_ready, 1)
            for i in range(2):
                gather(i, i)
            pool.sem_inc(xt_psum, 2)
            with pool.Fori(0, NBLK // UN) as r:
                for i in range(UN):
                    n = UN * r + i
                    pool.wait_ge(xt_psum, n + 1)
                    carry_wait(pool, HOLD, 1)
                    gather((i + 2) % UN, n + 2)
            for i in range(UN):
                pool.wait_ge(gathered[i], 16 * (NBLK // UN + (i < 2)))

        @block.scalar
        def _(act):
            def features(i, n):
                act.wait_ge(xt_psum, n + 3)
                act.activation(XT[i % 2][:].rearrange("p c n -> p (c n)"), pT[:, i % 2],
                               ACT.Copy).then_inc(xt_ready, 1)

            def gate(i, n):
                act.wait_ge(u_ready, n + 1)
                act.activation(A[:, i % 2], U[:, i % 2, 0], ACT.Silu).then_inc(a_ready, 1)

            features(0, 0)
            features(1, 1)
            gate(0, 0)
            with act.Fori(0, NBLK // UN) as r:
                for i in range(UN):
                    n = UN * r + i
                    act.wait_ge(ht_psum, n + 1)
                    act.activation(HT[:, i % 2], pHT[:, i % 2, 0:P], ACT.Copy).then_inc(ht_ready, 1)
                    features(i, n + 2)
                    gate(i + 1, n + 1)

        @block.vector
        def _(dve):
            dve.sem_inc(y_ready, 2)

            def biased(i, n):
                e = dve.value_load(EXPERT[0:1, bass.ds(n, 1)], min_val=0, max_val=NE3 - 1)
                dve.wait_ge(u_psum, n + 1)
                dve.tensor_tensor(U[:, i % 2].rearrange("p w m -> p (w m)"), pU[:, i % 2, 0:2 * P],
                                  B12[:, bass.ds(e, 1)].rearrange("p e m -> p (e m)"), ALU.add).then_inc(u_ready, 1)

            def gated(i, n):
                dve.wait_ge(a_ready, n + 1)
                dve.tensor_tensor(H[:, i % 2], U[:, i % 2, 1], A[:, i % 2], ALU.mult).then_inc(h_ready, 1)

            biased(0, 0)
            gated(0, 0)
            with dve.Fori(0, NBLK // UN) as r:
                for i in range(UN):
                    n = UN * r + i
                    biased(i + 1, n + 1)
                    dve.wait_ge(stored[i % 2], 16 * (2 * r + i // 2 + 1))
                    dve.wait_ge(y_psum, n + 1)
                    dve.tensor_copy(Y[i % 2][:], pY[:, i % 2]).then_inc(y_ready, 1)
                    gated(i + 1, n + 1)

        @block.tensor
        def _(pe):
            pe.wait_ge(w_in, 16)

            def turn(i, n, passes):
                pe.wait_ge(gathered[i], 16 * passes)
                for c in range(KC):
                    ins = pe.transpose(pT[:, i % 2, c * P:(c + 1) * P], X[i][:, c * P:(c + 1) * P], ident[:])
                ins.then_inc(xt_psum, 1)

            def up(i, n):
                e = pe.value_load(EXPERT[0:1, bass.ds(n, 1)], min_val=0, max_val=NE3 - 1)
                pe.wait_ge(xt_ready, n + 1)
                for c in range(KC):
                    ins = pe.matmul(pU[:, i % 2, 0:2 * P], XT[i % 2][:, c],
                                    W12[:, bass.ds(e, 1), c].rearrange("p e m -> p (e m)"), start=(c == 0),
                                    stop=(c == KC - 1))
                ins.then_inc(u_psum, 1)
                return e

            turn(0, 0, 1)
            turn(1, 1, 1)
            up(0, 0)
            with pe.Fori(0, NBLK // UN) as r:
                for i in range(UN):
                    n = UN * r + i
                    up(i + 1, n + 1)
                    pe.wait_ge(h_ready, n + 1)
                    pe.transpose(pHT[:, i % 2, 0:P], H[:, i % 2], ident[:]).then_inc(ht_psum, 1)
                    turn((i + 2) % UN, n + 2, r + 1 + (i + 2) // UN)
                    e = pe.value_load(EXPERT[0:1, bass.ds(n, 1)], min_val=0, max_val=NE3 - 1)
                    pe.wait_ge(ht_ready, n + 1)
                    pe.wait_ge(y_ready, n + 1)
                    pe.matmul(pY[:, i % 2], HT[:, i % 2], W3[:, bass.ds(e, 1)].rearrange("p e m -> p (e m)"),
                              start=True, stop=True).then_inc(y_psum, 1)


def combine(nc, places, base_d, ys_d, x_out):
    SLOT, GATE = places
    UN = 4
    with ExitStack() as ctx:
        sem = Semaphores(ctx, nc, "k_")

        B = [ctx.enter_context(nc.sbuf_tensor(f"k_B{i}", [P, D], F32)) for i in range(UN)]
        Y = [ctx.enter_context(nc.sbuf_tensor(f"k_Y{i}", [P, TOPK, D], F32)) for i in range(UN)]
        IX = [ctx.enter_context(nc.sbuf_tensor(f"k_IX{i}", [P, TOPK], I32)) for i in range(UN)]
        HOLD = ctx.enter_context(nc.sbuf_tensor("k_HOLD", [1, 3], F32))
        ix_ready = sem("ix_ready")
        base_loaded = [sem(f"base_loaded{i}") for i in range(UN)]
        gathered = [sem(f"gathered{i}") for i in range(UN)]
        added = sem("added")
        stored = [sem(f"stored{i}") for i in range(UN)]
        base_v = base_d.rearrange("(t p) d -> t p d", p=P)
        out_v = x_out.rearrange("b (t p) d -> (b t) p d", p=P)
        block = ctx.enter_context(nc.Block())

        @block.sync
        def _(sp):
            for i in range(UN):
                sp.sem_inc(stored[i], 16)
            with sp.Fori(0, TT // UN) as r:
                for i in range(UN):
                    sp.wait_ge(stored[i], 16 * (r + 1))
                    sp.dma_start(B[i][:], base_v[bass.ds(UN * r + i, 1)].rearrange("t p d -> (t p) d")
                                 ).then_inc(base_loaded[i], 16)

        @block.gpsimd
        def _(pool):
            pool.memset(HOLD[:], 0.0).then_inc(ix_ready, 1)
            pool.wait_ge(ix_ready, 1)
            pool.sem_inc(added, TOPK * UN)
            with pool.Fori(0, TT // UN) as r:
                for i in range(UN):
                    n = UN * r + i
                    pool.wait_ge(added, TOPK * (n + 1))
                    carry_wait(pool, HOLD, 1)
                    pool.tensor_copy(IX[i][:], SLOT[:, :, bass.ds(n, 1)].rearrange("p k a -> p (k a)")).then_inc(ix_ready, 1)
                    pool.wait_ge(ix_ready, n + 2)
                    carry_wait(pool, HOLD, 2)
                    for k in range(TOPK):
                        pool.indirect_dma_start(Y[i][:, k], None, ys_d,
                                                bass.IndirectOffsetOnAxis(ap=IX[i][:, k:k + 1], axis=0)
                                                ).then_inc(gathered[i], 16)

        @block.vector
        def _(dve):
            with dve.Fori(0, TT // UN) as r:
                for i in range(UN):
                    n = UN * r + i
                    dve.wait_ge(base_loaded[i], 16 * (r + 1))
                    dve.wait_ge(gathered[i], 16 * TOPK * (r + 1))
                    for k in range(TOPK):
                        dve.scalar_tensor_tensor(B[i][:], Y[i][:, k], GATE[:, k, bass.ds(n, 1)], B[i][:], ALU.mult,
                                                 ALU.add).then_inc(added, 1)
                        dve.wait_ge(added, TOPK * (n + UN) + k + 1)

        @block.scalar
        def _(act):
            with act.Fori(0, TT // UN) as r:
                for i in range(UN):
                    n = UN * r + i
                    act.wait_ge(added, TOPK * (n + UN + 1))
                    act.dma_start(out_v[bass.ds(n, 1)].rearrange("t p d -> (t p) d"), B[i][:]).then_inc(stored[i], 16)
            for i in range(UN):
                act.wait_ge(stored[i], 16 * (TT // UN + 1))


def layer3(nc, x_in, x_out, wqkv, cos_d, sin_d, wo, wr, rb, rbias, ws, eb3, w12, w3, b12, tri, le, kx, tid, mask_q,
           mask_k, pick_d, ident_d):
    nk = GH
    kw = NG * nk * HD
    xt_d = nc.dram_tensor("f_xt", (NB, P, KC, S), F32).ap()
    xn_d = nc.dram_tensor("f_xn", (NB * S, D), F32).ap()
    q_d = nc.dram_tensor("f_q", (NB, KC, 2, 2, GW, S), F32).ap()
    k_d = nc.dram_tensor("f_k", (NB, kw // P, P // (nk * HD), 2, nk * HD, S), F32).ap()
    v_d = nc.dram_tensor("f_v", (NB, NG, P, NT * nk * VW), F32).ap()
    o_d = nc.dram_tensor("f_o", (NB, P, NT, NG, GW), F32).ap()
    base_d = nc.dram_tensor("h_base", (NB * S, D), F32).ap()
    tab_d = nc.dram_tensor("h_tab", (NBX * P, 1), F32).ap()
    ys_d = nc.dram_tensor("j_ys", (NBLK * P, D), F32).ap()
    scratch = (xt_d, q_d, k_d, v_d)
    project(nc, "f_", nk, x_in, scratch, wqkv, cos_d, sin_d, ident_d, xn_d=xn_d)
    attend(nc, "g_", nk, scratch, o_d, mask_q, mask_k, pick_d, ident_d)
    with ExitStack() as ctx:
        def sb(name, shape, dt=F32):
            return ctx.enter_context(nc.sbuf_tensor("m_" + name, shape, dt))

        W12 = sb("W12", [P, NE3, KC, 2 * P])
        W3 = sb("W3", [P, NE3, D])
        B12 = sb("B12", [P, NE3, 2 * P])
        GATES = sb("GATES", [P, NB, NT, NE3])
        CHOSEN = sb("CHOSEN", [P, NB, NT, NE3])
        SLOT = sb("SLOT", [P, TOPK, TT], I32)
        GATE = sb("GATE", [P, TOPK, TT])
        TOKEN = sb("TOKEN", [P, NBX], I32)
        EXPERT = sb("EXPERT", [1, NBX], I32)
        route(nc, (W12, W3, B12, GATES, CHOSEN), x_in, xt_d, o_d, base_d, tab_d, wo, wr, rb, rbias, ws, eb3, w12, w3,
              b12, ident_d)
        place(nc, (GATES, CHOSEN), (SLOT, GATE, TOKEN, EXPERT), tab_d, tri, le, kx, tid, ident_d)
        experts(nc, (W12, W3, B12), (TOKEN, EXPERT), xn_d, ys_d, ident_d)
        combine(nc, (SLOT, GATE), base_d, ys_d, x_out)


def _chunks(w):
    k, n = w.shape
    return w.reshape(k // P, P, n).transpose(1, 0, 2)


def _layout0(i):
    wq = i["L0_attn_Wq"].reshape(H0, G0, P, D)[:, 0].reshape(H0 * P, D).T
    return {
        "wq": _chunks(wq),
        "bq": i["L0_attn_bq"].reshape(H0, G0, P)[:, 0].T,
        "zb": i["L0_attn_z"].T,
        "mt": i["L0_attn_M"].transpose(2, 0, 1),
        "wo": i["L0_attn_Wo"].T.reshape(H0, G0, P, D).transpose(2, 0, 1, 3),
        "wb": _chunks(i["L0_ffn_W_base"].T),
        "bb": i["L0_ffn_b_base"],
        "wr": _chunks(i["L0_ffn_W_router"].T),
        "la": _chunks(i["L0_ffn_A"].reshape(R0, D).T),
        "lb": i["L0_ffn_B"].transpose(0, 2, 1).reshape(R0, D),
        "sel": np.repeat(np.eye(NE0, dtype=np.float32), R0 // NE0, axis=1),
        "ident": np.eye(P, dtype=np.float32),
    }


def _fourier():
    n = np.arange(D)
    f = np.arange(D // 2)
    cos = np.cos(2 * np.pi * ((n[:, None] * f) % D) / D)
    sin = np.sin(2 * np.pi * ((n[:, None] * f) % D) / D)
    sin[:, 0] = np.cos(np.pi * n)
    fwd = np.concatenate([cos, sin], axis=1)
    lag = np.minimum(n, D - n)
    scale = np.full(D // 2, 2.0 / D)
    scale[0] = 1.0 / D
    power = scale[:, None] * np.cos(2 * np.pi * ((f[:, None] * lag) % D) / D)
    power_i = power.copy()
    power_i[0] = np.cos(np.pi * lag) / D
    inv = np.concatenate([scale, scale])[:, None] * fwd.T
    cor = np.concatenate([power, power_i])
    return [_chunks(a.astype(np.float32)) for a in (fwd, cor, inv)]


def _layout1(i):
    fwd, cor, inv = _fourier()
    return {
        "dft": fwd, "cor": cor, "inv": inv,
        "w1": _chunks(i["L1_ffn_W"].T),
        "b1": i["L1_ffn_bias"],
        "a1": i["L1_ffn_lora_A"].reshape(P, D),
        "bl1": i["L1_ffn_lora_B"].transpose(0, 2, 1).reshape(P, D),
        "cf": np.repeat(i["L1_ffn_lora_weights"], 16).reshape(P, 1),
        "ident": np.eye(P, dtype=np.float32),
    }


def _rotary():
    inv = np.float32(1.0) / np.float32(10000.0) ** (np.arange(0, HD, 2, dtype=np.float32) / np.float32(HD))
    ang = np.arange(S, dtype=np.float32)[:, None] * inv[None, :].astype(np.float32)
    return [np.ascontiguousarray(f(ang.astype(np.float64)).astype(np.float32).reshape(NT, P, HD // 2).transpose(1, 0, 2))
            for f in (np.cos, np.sin)]


def _masks():
    row = np.arange(P)
    late = np.where(row[None, :] > row[:, None], np.float32(-1e30), np.float32(0.0))
    return late, np.ascontiguousarray(late.T)


def _pick():
    own = np.broadcast_to(np.eye(GH, dtype=np.float32)[None, :, :, None], (2, GH, GH, S)).reshape(2 * GH, GH * S)
    return np.concatenate([np.zeros((SM - 2 * GH - SW, GH * S), np.float32), own])


def _group_columns(w, heads, pairs_first):
    w = w.reshape(D, NG, heads, *((HD // 2, 2) if pairs_first else (2, HD // 2)))
    return w.transpose(0, 1, *((4, 3) if pairs_first else (3, 4)), 2).reshape(D, NG * heads * HD)


def _layout2(i):
    w = i["L2_attn_w_qkv"]
    cos, sin = _rotary()
    mq, mk = _masks()
    return {
        "wqkv": _chunks(np.concatenate([_group_columns(w[:, :D], GH, True), _group_columns(w[:, D:D + P], 1, True),
                                        w[:, D + P:]], axis=1)),
        "cos": cos, "sin": sin,
        "cent": _chunks(i["L2_ffn_centroids"].T),
        "asg": i["L2_ffn_assignments"],
        "cidx": np.arange(NCL, dtype=np.float32).reshape(NCL, 1),
        "wo": _chunks(i["L2_attn_w_o"]),
        "w2": _chunks(i["L2_ffn_weight"].T),
        "b2": i["L2_ffn_bias"],
        "mq": mq, "mk": mk, "pick": _pick(),
        "ident": np.eye(P, dtype=np.float32),
    }


def _layout3(i):
    cos, sin = _rotary()
    mq, mk = _masks()
    halves = [slice(0, P), slice(P, 2 * P)]
    sw = [np.stack([i[name][:, h] for h in halves]) for name in ("L3_ffn_sw1", "L3_ffn_sw2")]
    up = [w.reshape(2, KC, P, P).transpose(0, 2, 1, 3).reshape(2, P, D) for w in sw]
    ws = np.concatenate([*up, i["L3_ffn_sw3"].reshape(2, P, D),
                         i["L3_ffn_sb1"].reshape(2, P, 1), i["L3_ffn_sb2"].reshape(2, P, 1)], axis=2)
    w12 = np.concatenate([i["L3_ffn_ew1"], i["L3_ffn_ew2"]], axis=2)
    row = np.arange(P)
    expert = np.arange(NE3)
    return {
        "wqkv": _chunks(np.concatenate([_group_columns(i["L3_attn_wq"].T, GH, False),
                                        _group_columns(i["L3_attn_wk"].T, GH, False), i["L3_attn_wv"].T], axis=1)),
        "cos": cos, "sin": sin,
        "wo": _chunks(i["L3_attn_wo"].T),
        "wr": _chunks(i["L3_ffn_router_w"]),
        "rb": i["L3_ffn_router_b"],
        "rbias": i["L3_ffn_router_bias"],
        "ws": ws.transpose(1, 0, 2),
        "eb3": np.concatenate([i["L3_ffn_eb3"], i["L3_ffn_sb3"][None], np.zeros((GC - NE3 - 1, D), np.float32)]),
        "w12": w12.reshape(NE3, KC, P, 2 * P).transpose(2, 0, 1, 3),
        "w3": i["L3_ffn_ew3"].transpose(1, 0, 2),
        "b12": np.concatenate([i["L3_ffn_eb1"], i["L3_ffn_eb2"]], axis=1),
        "tri": (row[:, None] < row[None, :]).astype(np.float32),
        "le": np.broadcast_to((expert[None, :] <= expert[:, None]).astype(np.float32), (P, NE3, NE3)),
        "kx": np.broadcast_to(np.arange(NBX, dtype=np.float32), (P, NBX)),
        "tid": np.arange(TT * P, dtype=np.float32).reshape(TT, P).T,
        "mq": mq, "mk": mk, "pick": _pick(),
        "ident": np.eye(P, dtype=np.float32),
    }


def build(nc, x, out, arrays):
    between = [nc.dram_tensor(f"x{n}", (NB, S, D), F32).ap() for n in (1, 2, 3)]
    for layer, x_in, x_out, ins in zip((layer0, layer1, layer2, layer3), (x, *between), (*between, out), arrays):
        layer(nc, x_in, x_out, *ins)


def kernel(**inputs):
    import concourse.bacc as _bacc
    from concourse.bass_utils import run_bass_kernel_spmd as _run

    inputs = {k: np.asarray(v) for k, v in inputs.items()}
    nc = _bacc.Bacc("TRN2", target_bir_lowering=False, num_devices=1)
    arrays = {}

    def given(name, a):
        arrays[name] = np.ascontiguousarray(a)
        return nc.dram_tensor(name, arrays[name].shape, mybir.dt.from_np(arrays[name].dtype),
                              kind="ExternalInput").ap()

    x = given("in_x", inputs["L0_attn_hidden_states"])
    layers = [[given(f"in_{n}_{name}", a) for name, a in layout(inputs).items()]
              for n, layout in enumerate((_layout0, _layout1, _layout2, _layout3))]
    out = nc.dram_tensor("out", (NB, S, D), F32, kind="ExternalOutput").ap()
    build(nc, x, out, layers)
    return _run(nc, [arrays], core_ids=[0]).results[0]["out"]
```

```python
from contextlib import ExitStack

import numpy as np
import concourse.bass as bass
from concourse import mybir

F32 = mybir.dt.float32
F32R = mybir.dt.float32r
BF16 = mybir.dt.bfloat16
I32 = mybir.dt.int32
ALU = mybir.AluOpType
ACT = mybir.ActivationFunctionType
AX_X = mybir.AxisListType.X

P = 128
D = 512
NB = 4
S = 512
NT = S // P
KC = D // P
LN_EPS = 1e-5
BIG = 3.0e38


class Semaphores:

    def __init__(self, ctx, nc, tag):
        self.nc, self.tag, self.held = nc, tag, []
        ctx.callback(self.give_back)

    def __call__(self, name):
        self.held.append(self.nc.alloc_semaphore(self.tag + name))
        return self.held[-1]

    def give_back(self):
        self.nc.clear_and_free_semaphores(self.held)
        self.nc.all_engine_barrier()


class Chain:

    def __init__(self, eng, sem, per=0, turn=0):
        self.eng, self.sem, self.base, self.n, self.per = eng, sem, turn * per, 0, per

    def __call__(self, ins):
        self.n += 1
        ins.then_inc(self.sem, 1)
        self.eng.wait_ge(self.sem, self.base + self.n)

    def end(self):
        assert self.n == self.per, (self.sem, self.n, self.per)


class Normed:

    def __init__(self, ctx, nc, tag, ident, banks, sem):
        def sb(name, shape, dt=F32):
            return ctx.enter_context(nc.sbuf_tensor(tag + name, shape, dt))

        self.ident, self.banks = ident, banks
        self.x = sb("X", [P, NT, D])
        self.xn = sb("XN", [P, NT, D])
        self.xt = sb("XT", [P, KC, S])
        self.moments = sb("ST", [P, NT, 6])
        self.mv = sb("MV", [P, NT, 2])
        self.ve = sb("VE", [P, NT])
        self.half = sb("HALF", [P, NT])
        self.rs = sb("RS", [P, NT])
        self.hold = sb("HOLD", [P, 1])
        self.half_set = sem("half_set")
        self.x_loaded = sem("x_loaded")
        self.moments_ready = sem("moments_ready")
        self.stats_ready = sem("stats_ready")
        self.var_ready = sem("var_ready")
        self.rstd_ready = sem("rstd_ready")
        self.xn_ready = sem("xn_ready")
        self.xt_psum = sem("xt_psum")
        self.xt_ready = sem("xt_ready")

    def load(self, sp, x_v, b):
        sp.dma_start(self.x[:], x_v[bass.ds(b, 1)].rearrange("b p t d -> (b p) t d")).then_inc(self.x_loaded, 16)

    def vector_moments(self, dve, b, tiles):
        dve.wait_ge(self.x_loaded, b * 16 + 16)
        for t in tiles:
            dve.bn_stats(self.moments[:, t], self.x[:, t]).then_inc(self.moments_ready, 1)

    def vector_variance(self, dve, b):
        dve.wait_ge(self.moments_ready, b * NT + NT)
        dve.memset(self.hold[:], 0.0)
        for t in range(NT):
            dve.bn_aggr(self.mv[:, t], self.moments[:, t]).then_inc(self.stats_ready, 1)
        dve.wait_ge(self.stats_ready, b * NT + NT)
        dve.tensor_scalar(self.ve[:], self.mv[:, :, 1], LN_EPS, None, ALU.add).then_inc(self.var_ready, 1)

    def vector_norm(self, dve, b, first=False, stored=None):
        if not first:
            dve.wait_ge(self.xt_psum, b * KC)
            if stored is not None:
                dve.wait_ge(stored, b * 16)
        dve.wait_ge(self.rstd_ready, b + 1)
        for t in range(NT):
            dve.tensor_scalar(self.xn[:, t], self.x[:, t], self.mv[:, t, 0:1], self.rs[:, t:t + 1], ALU.subtract,
                              ALU.mult).then_inc(self.xn_ready, 1)

    def vector_part(self, dve, b, first=False, stored=None):
        self.vector_moments(dve, b, range(NT))
        self.vector_variance(dve, b)
        self.vector_norm(dve, b, first, stored)

    def pool_setup(self, pool):
        pool.memset(self.half[:], -0.5).then_inc(self.half_set, 1)
        pool.wait_ge(self.half_set, 1)

    def pool_part(self, pool, b):
        pool.wait_ge(self.var_ready, b + 1)
        pool.tensor_tensor(self.rs[:], self.ve[:], self.half[:], ALU.pow).then_inc(self.rstd_ready, 1)

    def tensor_part(self, pe, b):
        for c in range(KC):
            if c >= 2:
                pe.wait_ge(self.xt_ready, b * KC + c - 1)
            for t in range(NT):
                if c == 0:
                    pe.wait_ge(self.xn_ready, b * NT + t + 1)
                ins = pe.transpose(self.banks[:, c % 2, t * P:(t + 1) * P], self.xn[:, t, c * P:(c + 1) * P],
                                   self.ident[:])
            ins.then_inc(self.xt_psum, 1)

    def scalar_part(self, act, b):
        for c in range(KC):
            act.wait_ge(self.xt_psum, b * KC + c + 1)
            act.activation(self.xt[:, c], self.banks[:, c % 2], ACT.Copy).then_inc(self.xt_ready, 1)

H0, R0 = 8, P
G0 = 4
NE0 = 8
TOPB = 14


def layer0(nc, x_in, x_out, wq, bq, zb, mt, wo, wb, bb, wr, la, lb, sel, ident_d):
    with ExitStack() as ctx:
        def sb(name, shape, dt=F32):
            return ctx.enter_context(nc.sbuf_tensor("a_" + name, shape, dt))

        def ps(name, shape, dt=F32):
            return ctx.enter_context(nc.psum_tensor("a_" + name, shape, dt))

        sem = Semaphores(ctx, nc, "a_")

        x_v = x_in.rearrange("b (t p) d -> b p t d", p=P)
        y_v = x_out.rearrange("b (t p) d -> b p t d", p=P)

        NWO = 4
        WQ = sb("WQ", [P, KC, H0 * P])
        WB = sb("WB", [P, KC, D])
        MW = sb("MW", [P, H0, D])
        MT = sb("MT", [P, H0, P])
        WO = sb("WO", [P, NWO, G0, D])
        ZB = sb("ZB", [P, H0, P])
        ZC = sb("ZC", [P, H0])
        BQ = sb("BQ", [P, H0])
        WR = sb("WR", [P, KC, NE0])
        LA = sb("LA", [P, KC, R0])
        LB = sb("LB", [P, D])
        SEL = sb("SEL", [NE0, R0])
        BB = sb("BB", [P, D])
        ident = sb("ident", [P, P])
        X = sb("XR", [P, NT, D])
        HT = sb("HT", [P, S])
        LG = sb("LG", [P, NT, TOPB])
        LR = sb("LR", [P, NT, TOPB])
        TOP = sb("TOP", [P, NT, 8])
        NM = sb("NM", [P, NT])
        EG = sb("EG", [P, NT, NE0])
        EM = sb("EM", [P, NT, NE0])
        CS = sb("CS", [P, NT])
        CR = sb("CR", [P, NT])
        CB = sb("CB", [P, NT, NE0])
        CT = sb("CT", [NE0, S])
        NEG = sb("NEG", [P, 2, S])
        EX = sb("EX", [P, 2, S])
        RL = sb("RL", [P, 2, S])
        SG = sb("SG", [P, 2, S])
        DN = sb("DN", [P, 2, S])
        SN = sb("SN", [P, 2, S])

        pT = ps("pT", [P, 2, S])
        pQ = ps("pQ", [P, 2, S])
        pO = ps("pO", [P, NT, S])
        nm = Normed(ctx, nc, "a_", ident, pT, sem)
        XT = nm.xt

        ident_in = sem("ident_in")
        mt_in = sem("mt_in")
        w_in = sem("w_in")
        wo_in = [sem(f"wo_in{i}") for i in range(NWO)]
        mw_done = sem("mw_done")
        mw_copied = sem("mw_copied")
        res_loaded = sem("res_loaded")
        router_psum = sem("router_psum")
        top_ready = sem("top_ready")
        shift_ready = sem("shift_ready")
        gates_exp = sem("gates_exp")
        comb_ready = sem("comb_ready")
        comb_psum = sem("comb_psum")
        comb_copied = sem("comb_copied")
        lora_psum = sem("lora_psum")
        lora_copied = sem("lora_copied")
        spread_psum = sem("spread_psum")
        lora_ready = sem("lora_ready")
        q_psum = sem("q_psum")
        neg_ready = sem("neg_ready")
        exp_ready = sem("exp_ready")
        relu_ready = sem("relu_ready")
        sig_ready = sem("sig_ready")
        den_psum = sem("den_psum")
        sign_ready = sem("sign_ready")
        out_psum = sem("out_psum")
        y_ready = sem("y_ready")
        xb_ready = sem("xb_ready")
        y_stored = sem("y_stored")
        dve_step = sem("dve_step")
        pads_set = sem("pads_set")
        ones_set = sem("ones_set")
        zb_ready = sem("zb_ready")

        DVE_PER = 6
        block = ctx.enter_context(nc.Block())

        @block.sync
        def _(sp):
            nm.load(sp, x_v, 0)
            sp.dma_start(ident[:], ident_d).then_inc(ident_in, 16)
            sp.dma_start(MT[:], mt).then_inc(mt_in, 16)
            sp.dma_start(WB[:], wb).then_inc(w_in, 16)
            sp.dma_start(WR[:], wr).then_inc(w_in, 16)
            sp.dma_start(LA[:], la).then_inc(w_in, 16)
            sp.dma_start(LB[:], lb).then_inc(w_in, 16)
            sp.dma_start(SEL[:], sel).then_inc(w_in, 16)
            sp.dma_start(ZC[:], zb).then_inc(w_in, 16)
            sp.dma_start(BQ[:], bq).then_inc(w_in, 16)
            sp.dma_start(WQ[:], wq).then_inc(w_in, 16)
            sp.dma_start(BB[:], bb.partition_broadcast(P)).then_inc(w_in, 16)
            with sp.Fori(0, NB) as b:
                ahead = sp.snap((b + 1) % NB)
                sp.wait_ge(y_stored, b * 16 + 16)
                sp.dma_start(X[:], x_v[bass.ds(b, 1)].rearrange("b p t d -> (b p) t d")).then_inc(res_loaded, 16)
                sp.wait_ge(nm.xn_ready, b * NT + NT)
                nm.load(sp, x_v, ahead)
                sp.wait_ge(y_ready, b * NT + 2 * NT)
                sp.dma_start(y_v[bass.ds(b, 1)].rearrange("b p t d -> (b p) t d"), X[:]).then_inc(y_stored, 16)
            sp.wait_ge(y_stored, 16 * NB + 16)
            sp.wait_ge(nm.x_loaded, 16 * NB + 16)

        @block.scalar
        def _(act):
            for h in range(H0):
                if h >= NWO:
                    act.wait_ge(mw_done, h - NWO + 1)
                act.dma_start(WO[:, h % NWO], wo[:, h]).then_inc(wo_in[h % NWO], 16)
                if h >= NWO:
                    k = h - NWO
                    act.activation(MW[:, k], pO[:, 2 + k % 2], ACT.Copy).then_inc(mw_copied, 1)
            for k in range(H0 - NWO, H0):
                act.wait_ge(mw_done, k + 1)
                act.activation(MW[:, k], pO[:, 2 + k % 2], ACT.Copy).then_inc(mw_copied, 1)
            nm.scalar_part(act, 0)
            with act.Fori(0, NB) as b:
                act.wait_ge(shift_ready, b + 1)
                for t in range(NT):
                    ins = act.activation(EG[:, t], LG[:, t, 0:NE0], ACT.Exp, bias=NM[:, t:t + 1])
                ins.then_inc(gates_exp, 1)
                act.wait_ge(lora_psum, b + 1)
                act.activation(HT[:], pQ[:, 1], ACT.Copy).then_inc(lora_copied, 1)
                for h in range(H0):
                    act.wait_ge(q_psum, b * H0 + h + 1)
                    act.activation(RL[:, h % 2], pQ[:, 0], ACT.Relu, bias=BQ[:, h:h + 1]).then_inc(relu_ready, 1)
                    act.wait_ge(neg_ready, b * H0 + h + 1)
                    act.activation(EX[:, h % 2], NEG[:, h % 2], ACT.Exp).then_inc(exp_ready, 1)
                nm.scalar_part(act, b + 1)

        @block.gpsimd
        def _(pool):
            nm.pool_setup(pool)
            pool.memset(LG[:, :, NE0:TOPB], BIG).then_inc(pads_set, 1)
            pool.wait_ge(pads_set, 1)
            pool.sem_inc(y_stored, 16)
            nm.pool_part(pool, 0)
            pool.wait_ge(w_in, 9 * 16)
            with pool.Fori(0, NB) as b:
                pool.wait_ge(res_loaded, b * 16 + 16)
                for t in range(NT):
                    pool.tensor_tensor(X[:, t], X[:, t], BB[:], ALU.add).then_inc(xb_ready, 1)
                nm.pool_part(pool, b + 1)

        @block.vector
        def _(dve):
            dve.memset(ZB[:], 1.0).then_inc(ones_set, 1)
            dve.wait_ge(ones_set, 1)
            nm.vector_part(dve, 0, first=True)
            dve.wait_ge(pads_set, 1)
            dve.wait_ge(w_in, 9 * 16)
            for h in range(H0):
                dve.tensor_scalar(ZB[:, h], ZB[:, h], ZC[:, h:h + 1], None, ALU.mult).then_inc(zb_ready, 1)
            dve.sem_inc(y_ready, NT)
            with dve.Fori(0, NB) as b:
                link = Chain(dve, dve_step, DVE_PER, b)
                dve.wait_ge(router_psum, b + 1)
                link(dve.tensor_copy(LG[:, :, 0:NE0], pQ[:, 0, 0:NT * NE0].rearrange("p (t e) -> p t e", t=NT)))
                dve.memset(nm.hold[:], 0.0)
                for t in range(NT):
                    dve.max(TOP[:, t], LG[:, t]).then_inc(top_ready, 1)
                dve.wait_ge(top_ready, b * 2 * NT + NT)
                dve.tensor_scalar(NM[:], TOP[:, :, 6], -1.0, None, ALU.mult).then_inc(shift_ready, 1)
                for t in range(NT):
                    dve.match_replace(LR[:, t], TOP[:, t], LG[:, t], -BIG).then_inc(top_ready, 1)
                dve.wait_ge(top_ready, b * 2 * NT + 2 * NT)
                link(dve.tensor_tensor(EM[:], LR[:, :, 0:NE0], LG[:, :, 0:NE0], ALU.not_equal))
                dve.wait_ge(gates_exp, b + 1)
                link(dve.tensor_tensor(EM[:], EM[:], EG[:], ALU.mult))
                link(dve.tensor_reduce(CS[:], EM[:], AX_X, ALU.add))
                link(dve.reciprocal(CR[:], CS[:]))
                link(dve.tensor_scalar(CR[:], CR[:], 2.0, None, ALU.mult))
                for t in range(NT):
                    dve.tensor_scalar(CB[:, t], EM[:, t], CR[:, t:t + 1], None, ALU.mult).then_inc(comb_ready, 1)
                for h in range(H0):
                    dve.wait_ge(relu_ready, b * H0 + h + 1)
                    dve.tensor_scalar(NEG[:, h % 2], pQ[:, 0], BQ[:, h:h + 1], 0.0, ALU.add,
                                      ALU.min).then_inc(neg_ready, 1)
                    dve.wait_ge(exp_ready, b * H0 + h + 1)
                    dve.tensor_tensor(SG[:, h % 2], RL[:, h % 2], EX[:, h % 2], ALU.add).then_inc(sig_ready, 1)
                    if h == 0:
                        dve.wait_ge(comb_psum, b + 1)
                        dve.tensor_copy(CT[:], pT[0:NE0, 0]).then_inc(comb_copied, 1)
                        dve.wait_ge(spread_psum, b + 1)
                        dve.wait_ge(lora_copied, b + 1)
                        dve.tensor_tensor(HT[:], pT[:, 1], HT[:], ALU.mult).then_inc(lora_ready, 1)
                    dve.wait_ge(den_psum, b * H0 + h + 1)
                    dve.tensor_scalar(DN[:, h % 2], pQ[:, 1], 1e-6, None, ALU.add).then_inc(sign_ready, 1)
                    dve.wait_ge(sign_ready, (b * H0 + h) * 3 + 1)
                    dve.reciprocal(DN[:, h % 2], DN[:, h % 2]).then_inc(sign_ready, 1)
                    dve.wait_ge(sign_ready, (b * H0 + h) * 3 + 2)
                    dve.wait_ge(sig_ready, b * H0 + h + 1)
                    dve.tensor_tensor(SN[:, h % 2], SG[:, h % 2], DN[:, h % 2], ALU.mult).then_inc(sign_ready, 1)
                    if h in (2, 3):
                        nm.vector_moments(dve, b + 1, range(2 * h - 4, 2 * h - 2))
                    if h == 3:
                        nm.vector_variance(dve, b + 1)
                    if h == 4:
                        nm.vector_norm(dve, b + 1)
                for t in range(NT):
                    dve.wait_ge(out_psum, b * NT + t + 1)
                    dve.wait_ge(xb_ready, b * NT + t + 1)
                    dve.tensor_tensor(X[:, t], X[:, t], pO[:, t], ALU.add).then_inc(y_ready, 1)
                link.end()

        @block.tensor
        def _(pe):
            pe.wait_ge(mt_in, 16)
            for h in range(H0):
                pe.wait_ge(wo_in[h % NWO], 16 * (h // NWO + 1))
                if h >= 2:
                    pe.wait_ge(mw_copied, h - 1)
                for g in range(G0):
                    ins = pe.matmul(pO[:, 2 + h % 2], MT[:, h], WO[:, h % NWO, g], start=(g == 0), stop=(g == G0 - 1))
                ins.then_inc(mw_done, 1)
            pe.wait_ge(ident_in, 16)
            nm.tensor_part(pe, 0)
            pe.wait_ge(w_in, 9 * 16)
            pe.wait_ge(mw_copied, H0)
            pe.wait_ge(zb_ready, H0)
            with pe.Fori(0, NB) as b:
                def base_products(tiles):
                    for t in tiles:
                        for c in range(KC):
                            pe.matmul(pO[:, t], XT[:, c, t * P:(t + 1) * P], WB[:, c], start=(c == 0), stop=False)

                def queries(h):
                    for c in range(KC):
                        ins = pe.matmul(pQ[:, 0], WQ[:, c, h * P:(h + 1) * P], XT[:, c], start=(c == 0),
                                        stop=(c == KC - 1))
                    ins.then_inc(q_psum, 1)

                pe.wait_ge(nm.xt_ready, b * KC + KC)
                for t in range(NT):
                    for c in range(KC):
                        ins = pe.matmul(pQ[:, 0, t * NE0:(t + 1) * NE0], XT[:, c, t * P:(t + 1) * P], WR[:, c],
                                        start=(c == 0), stop=(c == KC - 1))
                ins.then_inc(router_psum, 1)
                for c in range(KC):
                    ins = pe.matmul(pQ[:, 1], LA[:, c], XT[:, c], start=(c == 0), stop=(c == KC - 1))
                ins.then_inc(lora_psum, 1)
                pe.wait_ge(y_ready, b * NT + NT)
                base_products(range(2))
                pe.wait_ge(dve_step, b * DVE_PER + 1)
                queries(0)
                pe.wait_ge(comb_ready, b * NT + NT)
                for t in range(NT):
                    ins = pe.transpose(pT[0:NE0, 0, t * P:(t + 1) * P], CB[:, t], ident[:])
                ins.then_inc(comb_psum, 1)
                base_products(range(2, NT))
                pe.wait_ge(comb_copied, b + 1)
                pe.matmul(pT[:, 1], SEL[:], CT[:], start=True, stop=True).then_inc(spread_psum, 1)

                def out_products(h):
                    pe.wait_ge(sign_ready, (b * H0 + h + 1) * 3)
                    for t in range(NT):
                        ins = pe.matmul(pO[:, t], SN[:, h % 2, t * P:(t + 1) * P], MW[:, h], start=False,
                                        stop=(h == H0 - 1))
                        if h == H0 - 1:
                            ins.then_inc(out_psum, 1)

                for h in range(H0):
                    if h >= 1:
                        pe.wait_ge(neg_ready, b * H0 + h)
                        queries(h)
                    if h == 1:
                        pe.wait_ge(lora_ready, b + 1)
                        for t in range(NT):
                            pe.matmul(pO[:, t], HT[:, t * P:(t + 1) * P], LB[:], start=False, stop=False)
                    if h >= 2:
                        out_products(h - 2)
                    pe.wait_ge(sig_ready, b * H0 + h + 1)
                    pe.matmul(pQ[:, 1], ZB[:, h], SG[:, h % 2], start=True, stop=True).then_inc(den_psum, 1)
                nm.tensor_part(pe, b + 1)
                out_products(H0 - 2)
                out_products(H0 - 1)

TOP_LAGS = 6
LAGP = S + 2


def layer1(nc, x_in, x_out, dft, cor, inv, w1, b1, a1, bl1, cf, ident_d):
    with ExitStack() as ctx:
        def sb(name, shape, dt=F32):
            return ctx.enter_context(nc.sbuf_tensor("b_" + name, shape, dt))

        def ps(name, shape, dt=F32):
            return ctx.enter_context(nc.psum_tensor("b_" + name, shape, dt))

        sem = Semaphores(ctx, nc, "b_")

        x_v = x_in.rearrange("b (t p) d -> b p t d", p=P)
        y_v = x_out.rearrange("b (t p) d -> b p t d", p=P)

        ident = sb("ident", [P, P])
        DFT = sb("DFT", [P, KC, D])
        COR = sb("COR", [P, KC, D])
        INV = sb("INV", [P, KC, D])
        W = sb("W", [P, KC, D])
        A1 = sb("A1", [P, D])
        BL = sb("BL", [P, D])
        CF = sb("CF", [P, 1])
        BB = sb("BB", [P, D])
        FX = sb("FX", [P, KC, S])
        SQ = sb("SQ", [P, KC, S])
        CO = sb("CO", [P, 2, LAGP])
        RP = sb("RP", [P, 2, LAGP])
        TOP = sb("TOP", [P, NT, 8])
        NM = sb("NM", [P, NT])
        EX = sb("EX", [P, 2, D])
        MK = sb("MK", [P, 2, D])
        WS = sb("WS", [P, NT])
        WR = sb("WR", [P, NT])
        WL = sb("WL", [P, NT, D])
        WT = sb("WT", [P, KC, S])
        FW = sb("FW", [P, KC, S])
        FA = sb("FA", [P, S])
        TM = sb("TM", [P, 2, 4, S])

        pT = ps("pT", [P, 2, S])
        pF = ps("pF", [P, 2, S])
        pO = ps("pO", [P, NT, S])
        nm = Normed(ctx, nc, "b_", ident, pT, sem)
        X = sb("XR", [P, NT, D])
        OH = WL

        ident_in = sem("ident_in")
        w_in = sem("w_in")
        lora_scaled = sem("lora_scaled")
        lora_psum = sem("lora_psum")
        w_ready = sem("w_ready")
        pads_set = sem("pads_set")
        fx_psum = sem("fx_psum")
        fx_ready = sem("fx_ready")
        sq_ready = sem("sq_ready")
        cor_psum = sem("cor_psum")
        cor_ready = sem("cor_ready")
        top_ready = sem("top_ready")
        shift_ready = sem("shift_ready")
        exp_ready = sem("exp_ready")
        lag_step = sem("lag_step")
        weight_ready = sem("weight_ready")
        wt_psum = sem("wt_psum")
        wt_ready = sem("wt_ready")
        fw_psum = sem("fw_psum")
        fw_ready = sem("fw_ready")
        term_ready = sem("term_ready")
        prod_ready = sem("prod_ready")
        out_psum = sem("out_psum")
        res_loaded = sem("res_loaded")
        xb_ready = sem("xb_ready")
        y_ready = sem("y_ready")
        y_stored = sem("y_stored")
        LAG_STEPS = 4
        PAIRED = (0, 2, 1, 3)
        block = ctx.enter_context(nc.Block())

        @block.sync
        def _(sp):
            nm.load(sp, x_v, 0)
            sp.dma_start(ident[:], ident_d).then_inc(ident_in, 16)
            sp.dma_start(A1[:], a1).then_inc(w_in, 16)
            sp.dma_start(BL[:], bl1).then_inc(w_in, 16)
            sp.dma_start(CF[:], cf).then_inc(w_in, 16)
            sp.dma_start(W[:], w1).then_inc(w_in, 16)
            sp.dma_start(DFT[:], dft).then_inc(w_in, 16)
            sp.dma_start(COR[:], cor).then_inc(w_in, 16)
            sp.dma_start(INV[:], inv).then_inc(w_in, 16)
            sp.dma_start(BB[:], b1.partition_broadcast(P)).then_inc(w_in, 16)
            with sp.Fori(0, NB) as b:
                ahead = sp.snap((b + 1) % NB)
                sp.wait_ge(y_stored, b * 16 + 16)
                sp.dma_start(X[:], x_v[bass.ds(b, 1)].rearrange("b p t d -> (b p) t d")).then_inc(res_loaded, 16)
                sp.wait_ge(nm.xn_ready, b * NT + NT)
                nm.load(sp, x_v, ahead)
                sp.wait_ge(y_ready, b * NT + 2 * NT)
                sp.dma_start(y_v[bass.ds(b, 1)].rearrange("b p t d -> (b p) t d"), X[:]).then_inc(y_stored, 16)
            sp.wait_ge(y_stored, 16 * NB + 16)
            sp.wait_ge(nm.x_loaded, 16 * NB + 16)

        @block.scalar
        def _(act):
            nm.scalar_part(act, 0)
            with act.Fori(0, NB) as b:
                for c in range(KC):
                    act.wait_ge(fx_psum, b * KC + c + 1)
                    act.activation(SQ[:, c], pF[:, c % 2], ACT.Square).then_inc(sq_ready, 1)
                    act.activation(FX[:, c], pF[:, c % 2], ACT.Copy).then_inc(fx_ready, 1)
                for t in range(NT):
                    act.wait_ge(cor_psum, b * NT + t + 1)
                    if t >= 2:
                        act.wait_ge(weight_ready, b * NT + t - 1)
                    act.activation(CO[:, t % 2, 0:D], pF[:, t % 2], ACT.Copy).then_inc(cor_ready, 1)
                    act.wait_ge(cor_ready, b * NT + t + 1)
                    act.wait_ge(shift_ready, b * NT + t + 1)
                    act.activation(EX[:, t % 2], CO[:, t % 2, 0:D], ACT.Exp, bias=NM[:, t:t + 1]).then_inc(exp_ready, 1)
                nm.scalar_part(act, b + 1)
                for c in range(KC):
                    act.wait_ge(wt_psum, b * KC + c + 1)
                    act.activation(WT[:, c], pT[:, c % 2], ACT.Copy).then_inc(wt_ready, 1)
                for k, c in enumerate(PAIRED):
                    act.wait_ge(fw_psum, b * KC + k + 1)
                    if c == 0:
                        act.activation(FA[:], pF[:, 0], ACT.Copy).then_inc(fw_ready, 1)
                    act.activation(FW[:, c], pF[:, k % 2], ACT.Copy).then_inc(fw_ready, 1)
                    if c == 2:
                        act.wait_ge(fw_ready, b * 7 + 3)
                        act.activation(FA[0:1, :], FW[0:1, 2], ACT.Copy).then_inc(fw_ready, 1)
                        act.wait_ge(fw_ready, b * 7 + 4)
                        act.activation(FW[0:1, 2], FW[0:1, 2], ACT.Copy, scale=0.0).then_inc(fw_ready, 1)

        @block.gpsimd
        def _(pool):
            pool.memset(CO[:, :, D:LAGP], BIG).then_inc(pads_set, 1)
            nm.pool_setup(pool)
            pool.sem_inc(y_stored, 16)
            nm.pool_part(pool, 0)
            pool.wait_ge(w_in, 8 * 16)
            with pool.Fori(0, NB) as b:
                nm.pool_part(pool, b + 1)
                pool.wait_ge(res_loaded, b * 16 + 16)
                for t in range(NT):
                    pool.tensor_tensor(X[:, t], X[:, t], BB[:], ALU.add).then_inc(xb_ready, 1)
                for k in range(2):
                    pool.wait_ge(term_ready, b * 8 + 4 * k + 4)
                    pool.tensor_tensor(OH[:, k], TM[:, k, 0], TM[:, k, 1], ALU.add).then_inc(prod_ready, 1)
                    pool.tensor_tensor(OH[:, k + 2], TM[:, k, 2], TM[:, k, 3], ALU.subtract).then_inc(prod_ready, 1)

        @block.vector
        def _(dve):
            dve.sem_inc(y_ready, NT)
            nm.vector_part(dve, 0, first=True)
            dve.wait_ge(w_in, 8 * 16)
            dve.tensor_scalar(BL[:], BL[:], CF[:], 2.0, ALU.mult, ALU.mult).then_inc(lora_scaled, 1)
            for c in range(KC):
                dve.wait_ge(lora_psum, c + 1)
                dve.tensor_tensor(W[:, c], W[:, c], pO[:, c], ALU.add).then_inc(w_ready, 1)
            dve.wait_ge(pads_set, 1)
            with dve.Fori(0, NB) as b:
                nm.vector_part(dve, b + 1)
                for t in range(NT):
                    i = t % 2
                    link = Chain(dve, lag_step, LAG_STEPS, b * NT + t)
                    dve.wait_ge(cor_ready, b * NT + t + 1)
                    dve.memset(nm.hold[:], 0.0)
                    dve.max(TOP[:, t], CO[:, i]).then_inc(top_ready, 1)
                    dve.wait_ge(top_ready, b * NT + t + 1)
                    dve.tensor_scalar(NM[:, t:t + 1], TOP[:, t, 2:3], -1.0, None, ALU.mult).then_inc(shift_ready, 1)
                    link(dve.match_replace(RP[:, i], TOP[:, t], CO[:, i], -BIG))
                    link(dve.tensor_tensor(MK[:, i], RP[:, i, 0:D], CO[:, i, 0:D], ALU.not_equal))
                    dve.wait_ge(exp_ready, b * NT + t + 1)
                    link(dve.tensor_tensor_reduce(WL[:, t], EX[:, i], MK[:, i], 1.0, 0.0, ALU.mult, ALU.add,
                                                  WS[:, t:t + 1]))
                    link(dve.reciprocal(WR[:, t:t + 1], WS[:, t:t + 1]))
                    dve.tensor_scalar(WL[:, t], WL[:, t], WR[:, t:t + 1], None, ALU.mult).then_inc(weight_ready, 1)
                    link.end()
                for k in range(2):
                    dve.wait_ge(fw_ready, b * 7 + 5 + 2 * k)
                    re, im = FW[:, k], FW[:, k + 2]
                    alt = FA[:] if k == 0 else FW[:, 1]
                    dve.tensor_tensor(TM[:, k, 0], re, FX[:, k], ALU.mult).then_inc(term_ready, 1)
                    dve.tensor_tensor(TM[:, k, 1], im, FX[:, k + 2], ALU.mult).then_inc(term_ready, 1)
                    dve.tensor_tensor(TM[:, k, 2], alt, FX[:, k + 2], ALU.mult).then_inc(term_ready, 1)
                    dve.tensor_tensor(TM[:, k, 3], im, FX[:, k], ALU.mult).then_inc(term_ready, 1)
                for t in range(NT):
                    dve.wait_ge(out_psum, b * NT + t + 1)
                    dve.wait_ge(xb_ready, b * NT + t + 1)
                    dve.tensor_tensor(X[:, t], X[:, t], pO[:, t], ALU.add).then_inc(y_ready, 1)

        @block.tensor
        def _(pe):
            pe.wait_ge(ident_in, 16)
            nm.tensor_part(pe, 0)
            pe.wait_ge(w_in, 8 * 16)
            pe.wait_ge(lora_scaled, 1)
            for c in range(KC):
                pe.matmul(pO[:, c], A1[:, c * P:(c + 1) * P], BL[:], start=True, stop=True).then_inc(lora_psum, 1)
            pe.wait_ge(w_ready, KC)
            with pe.Fori(0, NB) as b:
                pe.wait_ge(nm.xt_ready, b * KC + KC)
                for m in range(KC):
                    if m >= 2:
                        pe.wait_ge(fx_ready, b * KC + m - 1)
                    for c in range(KC):
                        ins = pe.matmul(pF[:, m % 2], DFT[:, c, m * P:(m + 1) * P], nm.xt[:, c], start=(c == 0),
                                        stop=(c == KC - 1))
                    ins.then_inc(fx_psum, 1)
                pe.wait_ge(fx_ready, b * KC + KC)
                pe.wait_ge(y_ready, b * NT + NT)
                for t in range(NT):
                    if t >= 2:
                        pe.wait_ge(cor_ready, b * NT + t - 1)
                    for c in range(KC):
                        ins = pe.matmul(pF[:, t % 2], SQ[:, c, t * P:(t + 1) * P], COR[:, c], start=(c == 0),
                                        stop=(c == KC - 1))
                    ins.then_inc(cor_psum, 1)
                    for c in range(KC):
                        pe.matmul(pO[:, t], nm.xt[:, c, t * P:(t + 1) * P], W[:, c], start=(c == 0), stop=False)
                nm.tensor_part(pe, b + 1)
                pe.wait_ge(nm.xt_ready, b * KC + 2 * KC)
                for c in range(KC):
                    if c >= 2:
                        pe.wait_ge(wt_ready, b * KC + c - 1)
                    for t in range(NT):
                        if c == 0:
                            pe.wait_ge(weight_ready, b * NT + t + 1)
                        ins = pe.transpose(pT[:, c % 2, t * P:(t + 1) * P], WL[:, t, c * P:(c + 1) * P], ident[:])
                    ins.then_inc(wt_psum, 1)
                pe.wait_ge(wt_ready, b * KC + KC)
                for k, m in enumerate(PAIRED):
                    if k >= 2:
                        pe.wait_ge(fw_ready, b * 7 + k)
                    for c in range(KC):
                        ins = pe.matmul(pF[:, k % 2], DFT[:, c, m * P:(m + 1) * P], WT[:, c], start=(c == 0),
                                        stop=(c == KC - 1))
                    ins.then_inc(fw_psum, 1)
                for k in range(0, KC, 2):
                    pe.wait_ge(prod_ready, b * KC + k + 2)
                    for t in range(NT):
                        for c in PAIRED[k:k + 2]:
                            ins = pe.matmul(pO[:, t], OH[:, c, t * P:(t + 1) * P], INV[:, c], start=False,
                                            stop=(c == KC - 1))
                        if k == KC - 2:
                            ins.then_inc(out_psum, 1)

HD = 16
GH = 4
NG = 8
GW = GH * HD
VW = HD + 1
SW = 4 * HD
SM = 96 + 2 * GH
NCL = 64


def project(nc, tag, nk, x_in, scratch, wqkv, cos_d, sin_d, ident_d, gate=None, xn_d=None):
    xt_d, q_d, k_d, v_d = scratch
    kw = NG * nk * HD
    kc = kw // P
    parts = [(0, D), (D, kw), (D + kw, kw)] if nk == GH else [(0, D), (D, 2 * kw)]
    with ExitStack() as ctx:
        def sb(name, shape, dt=F32):
            return ctx.enter_context(nc.sbuf_tensor(tag + name, shape, dt))

        def ps(name, shape, dt=F32):
            return ctx.enter_context(nc.psum_tensor(tag + name, shape, dt))

        sem = Semaphores(ctx, nc, tag)

        x_v = x_in.rearrange("b (t p) d -> b p t d", p=P)
        ident = sb("ident", [P, P])
        W = sb("W", [P, KC, D + 2 * kw])
        COS = sb("COS", [P, NT, HD // 2])
        SIN = sb("SIN", [P, NT, HD // 2])
        ROT = sb("ROT", [P, 2, 2, 2, D])
        QR = sb("QR", [P, NT, D + kw])
        HI = sb("HI", [P, KC + kc, S], F32R)
        LO = sb("LO", [P, KC + kc, S], F32R)
        V = sb("V", [P, NG, NT, nk, VW])
        pT = ps("pT", [P, 2, S])
        pA = ps("pA", [P, 2, 3, S])
        nm = Normed(ctx, nc, tag, ident, pT, sem)

        ident_in = sem("ident_in")
        w_in = sem("w_in")
        ones_set = sem("ones_set")
        qkv_psum = sem("qkv_psum")
        turned = sem("turned")
        rotated = sem("rotated")
        v_ready = sem("v_ready")
        turn_psum = sem("turn_psum")
        hi_ready = sem("hi_ready")
        lo_ready = sem("lo_ready")
        stored = sem("stored")
        xt_stored = sem("xt_stored")
        xn_stored = sem("xn_stored") if xn_d is not None else None
        v_stored = sem("v_stored")
        NST = 2 * 2 + 2 * (P // (nk * HD))
        if gate:
            cent, asg, cidx, sel_d = gate
            CE = sb("CE", [P, KC, NCL])
            CM = sb("CM", [P, NT])
            CN = sb("CN", [P, NT])
            CX = sb("CX", [P, NT, NCL])
            CS = sb("CS", [P, NT])
            CR = sb("CR", [P, NT])
            CP = sb("CP", [P, NCL])
            CT = sb("CT", [NCL, 2])
            AI = sb("AI", [NCL, D], I32)
            AF = sb("AF", [NCL, D])
            CI = sb("CI", [NCL, 1])
            SR = sb("SR", [1, D])
            logit_psum = sem("logit_psum")
            cmax_ready = sem("cmax_ready")
            cshift_ready = sem("cshift_ready")
            cexp_ready = sem("cexp_ready")
            crec_ready = sem("crec_ready")
            chit_ready = sem("chit_ready")
            best_psum = sem("best_psum")
            hit_ready = sem("hit_ready")
            asg_ready = sem("asg_ready")
            sel_psum = sem("sel_psum")
            sel_ready = sem("sel_ready")
            sel_stored = sem("sel_stored")
        NW = 3 + (3 if gate else 0)
        block = ctx.enter_context(nc.Block())

        @block.sync
        def _(sp):
            nm.load(sp, x_v, 0)
            sp.dma_start(ident[:], ident_d).then_inc(ident_in, 16)
            sp.dma_start(COS[:], cos_d).then_inc(w_in, 16)
            sp.dma_start(SIN[:], sin_d).then_inc(w_in, 16)
            sp.dma_start(W[:], wqkv).then_inc(w_in, 16)
            if gate:
                sp.dma_start(CE[:], cent).then_inc(w_in, 16)
                sp.dma_start(AI[:], asg.partition_broadcast(NCL)).then_inc(w_in, 16)
                sp.dma_start(CI[:], cidx).then_inc(w_in, 16)
            sp.sem_inc(stored, 16)
            sp.sem_inc(v_stored, 16)
            with sp.Fori(0, NB) as b:
                one = bass.ds(b, 1)
                ahead = sp.snap((b + 1) % NB)
                sp.wait_ge(nm.xn_ready, b * NT + NT)
                nm.load(sp, x_v, ahead)
                sp.wait_ge(nm.xt_ready, b * KC + KC)
                sp.dma_start(xt_d[one].rearrange("b p c n -> (b p) c n"), nm.xt[:]).then_inc(xt_stored, 16)
                if xn_d is not None:
                    sp.dma_start(xn_d.rearrange("(b t p) d -> b p t d", b=NB, p=P)[one].rearrange(
                        "b p t d -> (b p) t d"), nm.xn[:]).then_inc(xn_stored, 16)
                sp.wait_ge(v_ready, b * NT + NT)
                sp.dma_start(v_d[one].rearrange("b g p m -> (b p) g m"),
                             V[:].rearrange("p g t j d -> p g (t j d)")).then_inc(v_stored, 16)
                sp.wait_ge(lo_ready, b * (KC + kc) + KC)
                for half in range(2):
                    rows = slice(half * GW, (half + 1) * GW)
                    for part, buf in ((0, HI), (1, LO)):
                        sp.dma_start(q_d[one, :, half, part].rearrange("b c f n -> (b f) c n"),
                                     buf[rows, 0:KC].bitcast(F32)).then_inc(stored, 16)
                sp.wait_ge(lo_ready, b * (KC + kc) + KC + kc)
                for g in range(P // (nk * HD)):
                    rows = slice(g * nk * HD, (g + 1) * nk * HD)
                    for part, buf in ((0, HI), (1, LO)):
                        sp.dma_start(k_d[one, :, g, part].rearrange("b c f n -> (b f) c n"),
                                     buf[rows, KC:KC + kc].bitcast(F32)).then_inc(stored, 16)
            sp.wait_ge(stored, 16 * NST * NB + 16)
            sp.wait_ge(v_stored, 16 * NB + 16)
            sp.wait_ge(xt_stored, 16 * NB)
            if xn_d is not None:
                sp.wait_ge(xn_stored, 16 * NB)
            sp.wait_ge(nm.x_loaded, 16 * NB + 16)
            if gate:
                sp.wait_ge(sel_ready, 1)
                sp.dma_start(sel_d.rearrange("(a d) -> a d", a=1), SR[:]).then_inc(sel_stored, 16)
                sp.wait_ge(sel_stored, 16)

        @block.scalar
        def _(act):
            nm.scalar_part(act, 0)
            act.wait_ge(ones_set, 1)
            with act.Fori(0, NB) as b:
                act.wait_ge(v_stored, b * 16 + 16)
                for t in range(NT):
                    act.wait_ge(turned, (b * NT + t) * 4 + 4)
                    act.wait_ge(qkv_psum, (b * NT + t + 1) * len(parts))
                    src = pA[:, t % 2, 2, 0:kw] if nk == GH else pA[:, t % 2, 1, kw:2 * kw]
                    act.activation(V[:, :, t, :, 0:HD], src.rearrange("p (g j d) -> p g j d", g=NG, j=nk),
                                   ACT.Copy).then_inc(v_ready, 1)
                    if gate:
                        act.wait_ge(cshift_ready, b * NT + t + 1)
                        act.activation(CX[:, t], pA[:, t % 2, 2, 0:NCL], ACT.Exp, bias=CN[:, t:t + 1], scale=10.0,
                                       accum_out=CS[:, t:t + 1]).then_inc(cexp_ready, 1)
                act.wait_ge(xt_stored, b * 16 + 16)
                nm.scalar_part(act, b + 1)
                act.wait_ge(stored, b * 16 * NST + 16)
                for c in range(KC + kc):
                    act.wait_ge(turn_psum, b * (KC + kc) + c + 1)
                    act.activation(HI[:, c], pT[:, c % 2], ACT.Copy).then_inc(hi_ready, 1)

        @block.gpsimd
        def _(pool):
            nm.pool_setup(pool)
            pool.memset(V[:], 1.0).then_inc(ones_set, 1)
            nm.pool_part(pool, 0)
            with pool.Fori(0, NB) as b:
                for t in range(NT):
                    if t == 2:
                        nm.pool_part(pool, b + 1)
                    for u, (at, width) in enumerate(((0, D), (D, kw))):
                        pool.wait_ge(turned, (b * NT + t) * 4 + 2 * u + 2)
                        h = width // NG // 2
                        c_, s_ = (ROT[:, t % 2, u, w, 0:width].rearrange("p (g a m) -> p g a m", g=NG, a=2)
                                  for w in (0, 1))
                        o_ = QR[:, t, at:at + width].rearrange("p (g a m) -> p g a m", g=NG, a=2)
                        pool.tensor_tensor(o_[:, :, 0], c_[:, :, 0], s_[:, :, 1], ALU.subtract).then_inc(rotated, 1)
                        pool.tensor_tensor(o_[:, :, 1], c_[:, :, 1], s_[:, :, 0], ALU.add).then_inc(rotated, 1)

        @block.vector
        def _(dve):
            nm.vector_part(dve, 0, first=True)
            dve.wait_ge(w_in, NW * 16)
            if gate:
                dve.memset(CP[:], 0.0).then_inc(chit_ready, 1)
            with dve.Fori(0, NB) as b:
                for t in range(NT):
                    if t == 2:
                        nm.vector_part(dve, b + 1, stored=xn_stored)
                    for u, width in enumerate((D, kw)):
                        dve.wait_ge(qkv_psum, (b * NT + t) * len(parts) + u + 1)
                        if t >= 2:
                            dve.wait_ge(rotated, (b * NT + t - 2) * 4 + 2 * u + 2)
                        src = pA[:, t % 2, u, 0:width].rearrange("p (m i j) -> p m i j", m=2 * NG, i=HD // 2)
                        for w, table in enumerate((COS, SIN)):
                            tab = table[:, t].unsqueeze(1).unsqueeze(3).to_broadcast(list(src.shape))
                            dve.tensor_tensor(
                                ROT[:, t % 2, u, w, 0:width].rearrange("p (m i j) -> p m i j", m=2 * NG, i=HD // 2),
                                src, tab, ALU.mult).then_inc(turned, 1)
                    if gate:
                        dve.wait_ge(logit_psum, b * NT + t + 1)
                        dve.tensor_reduce(CM[:, t:t + 1], pA[:, t % 2, 2, 0:NCL], AX_X, ALU.max).then_inc(cmax_ready, 1)
                        dve.wait_ge(cmax_ready, b * NT + t + 1)
                        dve.tensor_scalar(CN[:, t:t + 1], CM[:, t:t + 1], -10.0, None,
                                          ALU.mult).then_inc(cshift_ready, 1)
                if gate:
                    dve.wait_ge(cexp_ready, b * NT + NT)
                    dve.reciprocal(CR[:], CS[:]).then_inc(crec_ready, 1)
                    dve.wait_ge(crec_ready, b + 1)
                    for t in range(NT):
                        dve.wait_ge(chit_ready, b * NT + t + 1)
                        dve.scalar_tensor_tensor(CP[:], CX[:, t], CR[:, t:t + 1], CP[:], ALU.mult,
                                                 ALU.max).then_inc(chit_ready, 1)
                for c in range(KC + kc):
                    dve.wait_ge(hi_ready, b * (KC + kc) + c + 1)
                    dve.tensor_tensor(LO[:, c], pT[:, c % 2], HI[:, c].bitcast(F32), ALU.subtract).then_inc(lo_ready, 1)
            if gate:
                dve.wait_ge(best_psum, 1)
                dve.tensor_reduce(CT[:, 0:1], pT[0:NCL, 0, 0:P], AX_X, ALU.max).then_inc(hit_ready, 1)
                dve.wait_ge(hit_ready, 1)
                dve.tensor_scalar(CT[:, 1:2], CT[:, 0:1], 0.01, None, ALU.is_gt).then_inc(hit_ready, 1)
                dve.tensor_copy(AF[:], AI[:]).then_inc(asg_ready, 1)
                dve.wait_ge(asg_ready, 1)
                dve.tensor_scalar(AF[:], AF[:], CI[:], None, ALU.is_equal).then_inc(asg_ready, 1)
                dve.wait_ge(sel_psum, 1)
                dve.tensor_copy(SR[:], pT[0:1, 1]).then_inc(sel_ready, 1)

        @block.tensor
        def _(pe):
            pe.wait_ge(ident_in, 16)
            nm.tensor_part(pe, 0)
            pe.wait_ge(w_in, NW * 16)
            with pe.Fori(0, NB) as b:
                pe.wait_ge(nm.xt_ready, b * KC + KC)
                for t in range(NT):
                    if t >= 2:
                        pe.wait_ge(v_ready, b * NT + t - 1)
                        if gate:
                            pe.wait_ge(cexp_ready, b * NT + t - 1)
                    for n, (at, width) in enumerate(parts):
                        for c in range(KC):
                            ins = pe.matmul(pA[:, t % 2, n, 0:width], nm.xt[:, c, t * P:(t + 1) * P],
                                            W[:, c, at:at + width], start=(c == 0), stop=(c == KC - 1))
                        ins.then_inc(qkv_psum, 1)
                    if gate:
                        for c in range(KC):
                            ins = pe.matmul(pA[:, t % 2, 2, 0:NCL], nm.xt[:, c, t * P:(t + 1) * P], CE[:, c],
                                            start=(c == 0), stop=(c == KC - 1))
                        ins.then_inc(logit_psum, 1)
                nm.tensor_part(pe, b + 1)
                pe.wait_ge(nm.xt_ready, b * KC + 2 * KC)
                for c in range(KC + kc):
                    if c >= 2:
                        pe.wait_ge(lo_ready, b * (KC + kc) + c - 1)
                    for t in range(NT):
                        if c == 0:
                            pe.wait_ge(rotated, (b * NT + t) * 4 + 4)
                        ins = pe.transpose(pT[:, c % 2, t * P:(t + 1) * P], QR[:, t, c * P:(c + 1) * P], ident[:])
                    ins.then_inc(turn_psum, 1)
                pe.wait_ge(lo_ready, (b + 1) * (KC + kc))
                pe.wait_ge(v_ready, b * NT + NT)
                if gate:
                    pe.wait_ge(cexp_ready, b * NT + NT)
            if gate:
                pe.wait_ge(chit_ready, 1 + NB * NT)
                pe.transpose(pT[0:NCL, 0, 0:P], CP[:], ident[:]).then_inc(best_psum, 1)
                pe.wait_ge(hit_ready, 2)
                pe.wait_ge(asg_ready, 2)
                pe.matmul(pT[0:1, 1], CT[:, 1:2], AF[:], start=True, stop=True).then_inc(sel_psum, 1)


def attend(nc, tag, nk, scratch, o_d, mask_q, mask_k, pick_d, ident_d):
    _, q_d, k_d, v_d = scratch
    NGR = NB * NG
    NBUF = 4
    OFF = [0, S, 2 * S - P, 3 * S - 3 * P]
    PTW = 4 * S - 6 * P
    with ExitStack() as ctx:
        def sb(name, shape, dt=F32):
            return ctx.enter_context(nc.sbuf_tensor(tag + name, shape, dt))

        def ps(name, shape, dt=F32):
            return ctx.enter_context(nc.psum_tensor(tag + name, shape, dt))

        sem = Semaphores(ctx, nc, tag)

        ident = sb("ident", [P, P])
        identb = sb("identb", [P, P], BF16)
        MF = sb("MF", [P, 2, P])
        MB = sb("MB", [P, 2, P], BF16)
        PICK = sb("PICK", [SM, GH * S])
        QS = [sb(f"QS{i}", [SM, GH, S], F32R) for i in range(NBUF)]
        KS = [sb(f"KS{i}", [SM, GH, S], F32R) for i in range(NBUF)]
        V = [sb(f"V{i}", [P, NT, nk, VW]) for i in range(2)]
        PT = [sb(f"PT{i}", [P, GH, PTW]) for i in range(2)]
        MX = sb("MX", [P, NT, GH])
        MN = sb("MN", [P, NT, 2 * GH], F32R)
        MR = [sb(f"MR{i}", [2 * GH, S], F32R) for i in range(2)]
        OV = sb("OV", [P, S])
        RC = sb("RC", [P, NT * GH])
        AO = [sb(f"AO{i}", [P, NT, GH, HD]) for i in range(2)]
        pS = ps("pS", [P, 2, 2, S])
        pX = ps("pX", [P, 2, S])
        pM = ps("pM", [P, S])
        pV = ps("pV", [P, S])

        c_in = sem("c_in")
        cast = sem("cast")
        pv_set = sem("pv_set")
        ones_set = [sem(f"ones_set{i}") for i in range(NBUF)]
        loaded = [sem(f"loaded{i}") for i in range(NBUF)]
        v_loaded = [sem("v_loaded_even"), sem("v_loaded_odd")]
        m_loaded = [sem("m_loaded_even"), sem("m_loaded_odd")]
        top_psum = sem("top_psum")
        top_ready = sem("top_ready")
        m_high = sem("m_high")
        m_split = sem("m_split")
        m_psum = sem("m_psum")
        m_ready = sem("m_ready")
        score_psum = sem("score_psum")
        exp_ready = sem("exp_ready")
        pv_done = sem("pv_done")
        ov_ready = sem("ov_ready")
        o_psum = sem("o_psum")
        rec_ready = sem("rec_ready")
        out_ready = sem("out_ready")
        o_stored = [sem("o_stored_even"), sem("o_stored_odd")]
        SCORES = [(j, heads) for j in range(NT) for heads in ([(0, 1), (2, 3)] if S - j * P > S // 2 else [range(GH)])]
        UNITS = len(SCORES)
        MAXIMA = [(t, range(h, h + m)) for t in range(NT - 1, -1, -1) for m in [S // ((t + 1) * P)]
                  for h in range(0, GH, m)]
        TOPS = len(MAXIMA)
        BESIDE = (1, 2, 1, 1, 0, 0)
        AHEAD = 6
        NL = 6
        SCALE = HD ** -0.5

        block = ctx.enter_context(nc.Block())
        q_g = q_d.rearrange("b c h s (r j) n -> (b c h) (s r) (j n)", j=GH)
        k_g = k_d.rearrange("b c h s (r j) n -> (b c h) s r j n", j=nk)
        v_g = v_d.rearrange("b g p m -> (b g) p m")
        o_g = o_d.rearrange("b p t g m -> b g p t m")

        def pick(view, index):
            return view[bass.ds(index, 1)].rearrange("g p n -> (g p) n")

        def load_stacks(sp, i, G):
            for dup in range(2):
                sp.dma_start(QS[i][dup * 2 * HD:(dup + 1) * 2 * HD].bitcast(F32).rearrange("p j n -> p (j n)"),
                             pick(q_g, G)).then_inc(loaded[i], 16)
            for s in range(2):
                for dup in range(2):
                    at = (2 * s + dup) * HD
                    src = k_g[bass.ds(G, 1), s].rearrange("g r j n -> (g r) j n")
                    sp.dma_start(KS[i][at:at + HD].bitcast(F32),
                                 src.to_broadcast([HD, GH, S])).then_inc(loaded[i], 16)

        def load_v(sp, i, G):
            sp.dma_start(V[i][:].rearrange("p t j d -> p (t j d)"), pick(v_g, G)).then_inc(v_loaded[i], 16)


        def scores_of(u):
            j, heads = SCORES[u]
            N = S - j * P
            if N > S // 2:
                return pS[:, u % 2, :, 0:N]
            return pS[:, u % 2].rearrange("p e n -> p (e n)")[:, 0:GH * N].rearrange("p (h n) -> p h n", n=N)

        def maxima_of(parity, u):
            t, heads = MAXIMA[u]
            N = (t + 1) * P
            return pX[:, (parity + u) % 2, 0:len(heads) * N].rearrange("p (h n) -> p h n", n=N)

        @block.sync
        def _(sp):
            sp.dma_start(ident[:], ident_d).then_inc(c_in, 16)
            sp.dma_start(MF[:, 0], mask_q).then_inc(c_in, 16)
            sp.dma_start(MF[:, 1], mask_k).then_inc(c_in, 16)
            sp.dma_start(PICK[SW:SM], pick_d).then_inc(c_in, 16)
            for i in range(NBUF):
                load_stacks(sp, i, i)
            for i in range(2):
                load_v(sp, i, i)
                sp.sem_inc(o_stored[i], 16)
            with sp.Fori(0, NGR // NBUF) as r:
                n0 = NBUF * r
                next_s = [sp.snap((n0 + i + NBUF) % NGR) for i in range(NBUF)]
                next_v = [sp.snap((n0 + i + 2) % NGR) for i in range(NBUF)]
                place = [(sp.snap((n0 + i) // NG), sp.snap((n0 + i) % NG)) for i in range(NBUF)]
                for i in range(NBUF):
                    n = n0 + i
                    sp.wait_ge(score_psum, (n + 1) * UNITS)
                    load_stacks(sp, i, next_s[i])
                    sp.wait_ge(pv_done, n + 3)
                    load_v(sp, i % 2, next_v[i])
                    sp.wait_ge(out_ready, n + 2)
                    sp.dma_start(o_g[bass.ds(place[i][0], 1), bass.ds(place[i][1], 1)].rearrange("b g p t m -> (b g p) t m"),
                                 AO[i % 2][:].rearrange("p t j d -> p t (j d)")).then_inc(o_stored[i % 2], 16)
            for i in range(NBUF):
                sp.wait_ge(loaded[i], 16 * NL * (NGR // NBUF + 1))
            for i in range(2):
                sp.wait_ge(o_stored[i], 16 * (NGR // 2 + 1))
                sp.wait_ge(v_loaded[i], 16 * (NGR // 2 + 1))

        @block.scalar
        def _(act):
            act.sem_inc(exp_ready, 2)

            def maxima(i, n):
                act.wait_ge(m_psum, n + 1)
                act.activation(MR[i % 2][:], pM[0:2 * GH], ACT.Copy).then_inc(m_ready, 1)
                act.wait_ge(m_ready, n + 1)
                act.dma_start(QS[i][SM - 2 * GH:SM].bitcast(F32),
                              MR[i % 2][:].bitcast(F32).unsqueeze(1).to_broadcast([2 * GH, GH, S])
                              ).then_inc(m_loaded[i % 2], 16)

            maxima(0, 0)
            with act.Fori(0, NGR // NBUF) as r:
                for i in range(NBUF):
                    n = NBUF * r + i
                    act.wait_ge(pv_done, n + 1)
                    for u, (j, heads) in enumerate(SCORES):
                        N = S - j * P
                        act.wait_ge(score_psum, n * UNITS + u + 1)
                        act.activation(PT[i % 2][:, heads[0]:heads[-1] + 1, OFF[j]:OFF[j] + N], scores_of(u),
                                       ACT.Exp, scale=SCALE).then_inc(exp_ready, 1)
                    maxima((i + 1) % NBUF, n + 1)
                    act.wait_ge(pv_done, n + 3)
                    act.activation(OV[:], pV[:], ACT.Copy).then_inc(ov_ready, 1)
            act.wait_ge(m_loaded[0], 16 * (NGR // 2 + 1))
            act.wait_ge(m_loaded[1], 16 * (NGR // 2))

        def set_rows(eng, buffers):
            for i in buffers:
                eng.tensor_copy(QS[i][SW:SM - 2 * GH].rearrange("p j n -> p (j n)"),
                                PICK[SW:SM - 2 * GH]).then_inc(ones_set[i], 1)
                eng.tensor_copy(KS[i][SW:SM].rearrange("p j n -> p (j n)"), PICK[SW:SM]).then_inc(ones_set[i], 1)

        @block.gpsimd
        def _(pool):
            pool.wait_ge(c_in, 64)
            set_rows(pool, (2, 3))

        @block.vector
        def _(dve):
            dve.memset(pV[:], 0.0).then_inc(pv_set, 1)
            dve.wait_ge(c_in, 64)
            dve.tensor_copy(identb[:], ident[:]).then_inc(cast, 1)
            dve.tensor_copy(MB[:], MF[:]).then_inc(cast, 1)
            set_rows(dve, (0, 1))
            dve.sem_inc(top_ready, 2)
            dve.sem_inc(out_ready, 1)

            def maxima(i, n, units):
                for u in units:
                    t, heads = MAXIMA[u]
                    dve.wait_ge(top_psum, n * TOPS + u + 1)
                    dve.tensor_reduce(MX[:, t, heads[0]:heads[-1] + 1], maxima_of(i * TOPS, u), AX_X,
                                      ALU.max).then_inc(top_ready, 1)

            def split(n):
                dve.wait_ge(top_ready, (n + 1) * TOPS + 2)
                dve.tensor_scalar(MN[:, :, 0:GH], MX[:], -1.0, None, ALU.mult).then_inc(m_high, 1)
                dve.wait_ge(m_high, n + 1)
                dve.scalar_tensor_tensor(MN[:, :, GH:2 * GH], MX[:], -1.0, MN[:, :, 0:GH].bitcast(F32), ALU.mult,
                                         ALU.subtract).then_inc(m_split, 1)
                dve.wait_ge(m_split, n + 1)

            maxima(0, 0, range(TOPS))
            split(0)
            maxima(1, 1, range(AHEAD))
            with dve.Fori(0, NGR // NBUF) as r:
                for i in range(NBUF):
                    n = NBUF * r + i
                    maxima(i + 1, n + 1, range(AHEAD, TOPS))
                    split(n + 1)
                    maxima(i + 2, n + 2, range(4))
                    dve.wait_ge(o_psum, n + 1)
                    sums = pM[:].rearrange("p (m d) -> p m d", d=2 * HD)
                    dve.reciprocal(RC[:], sums[:, :, HD]).then_inc(rec_ready, 1)
                    dve.wait_ge(rec_ready, n + 1)
                    dve.wait_ge(o_stored[i % 2], 16 * (2 * r + i // 2 + 1))
                    dve.tensor_tensor(AO[i % 2][:].rearrange("p t j d -> p (t j) d"), sums[:, :, 0:HD],
                                      RC[:].unsqueeze(2).to_broadcast([P, NT * GH, HD]),
                                      ALU.mult).then_inc(out_ready, 1)
                    maxima(i + 2, n + 2, range(4, AHEAD))

        @block.tensor
        def _(pe):
            pe.sem_inc(pv_done, 2)
            pe.wait_ge(cast, 2)
            pe.wait_ge(c_in, 64)

            def tops(i, n, units):
                for u in units:
                    t, heads = MAXIMA[u]
                    N = (t + 1) * P
                    out = maxima_of(i * TOPS, u)
                    pe.wait_ge(top_ready, n * TOPS + u + 1)
                    for e, h in enumerate(heads):
                        pe.matmul(out[:, e], QS[i][0:SM - 2 * GH, h, t * P:N], KS[i][0:SM - 2 * GH, h, 0:N],
                                  start=True, stop=False)
                        ins = pe.matmul(out[:, e, t * P:N], identb[:], MB[:, 0], start=False, stop=True)
                    ins.then_inc(top_psum, 1)

            def score_unit(i, n, u):
                j, heads = SCORES[u]
                out = scores_of(u)
                pe.wait_ge(exp_ready, n * UNITS + u + 1)
                for e, h in enumerate(heads):
                    pe.matmul(out[:, e], KS[i][:, h, j * P:(j + 1) * P], QS[i][:, h, j * P:S], start=True, stop=False)
                    ins = pe.matmul(out[:, e, 0:P], identb[:], MB[:, 1], start=False, stop=True)
                ins.then_inc(score_psum, 1)

            def turn_maxima(n):
                pe.wait_ge(m_split, n + 1)
                for t in range(NT):
                    ins = pe.transpose(pM[0:2 * GH, t * P:(t + 1) * P], MN[:, t].bitcast(F32), ident[:])
                ins.then_inc(m_psum, 1)

            def values(i, j):
                for h in range(GH):
                    at = 2 * HD * h
                    ins = pe.matmul(pV[at:at + VW, j * P:S], V[i % 2][:, j, h if nk == GH else 0],
                                    PT[i % 2][:, h, OFF[j]:OFF[j] + S - j * P], start=(j == 0), stop=(j == NT - 1))
                return ins

            pe.wait_ge(ones_set[0], 2)
            pe.wait_ge(loaded[0], 16 * NL)
            tops(0, 0, range(TOPS))
            turn_maxima(0)
            pe.wait_ge(ones_set[1], 2)
            pe.wait_ge(loaded[1], 16 * NL)
            tops(1, 1, range(AHEAD))
            pe.wait_ge(pv_set, 1)
            with pe.Fori(0, NGR // NBUF) as r:
                for i in range(NBUF):
                    n = NBUF * r + i
                    i1, i2 = (i + 1) % NBUF, (i + 2) % NBUF
                    pe.wait_ge(m_loaded[i % 2], 16 * (2 * r + i // 2 + 1))
                    for u in range(UNITS):
                        score_unit(i, n, u)
                        at = AHEAD + sum(BESIDE[:u])
                        tops(i1, n + 1, range(at, at + BESIDE[u]))
                    pe.wait_ge(v_loaded[i % 2], 16 * (2 * r + i // 2 + 1))
                    pe.wait_ge(exp_ready, n * UNITS + 4)
                    values(i, 0)
                    pe.wait_ge(loaded[i2], 16 * NL * (r + 1 + (i + 2) // NBUF))
                    if i2 >= 2:
                        pe.wait_ge(ones_set[i2], 2)
                    tops(i2, n + 2, range(1))
                    pe.wait_ge(out_ready, n + 1)
                    turn_maxima(n + 1)
                    tops(i2, n + 2, range(1, 2))
                    pe.wait_ge(exp_ready, (n + 1) * UNITS + 2)
                    values(i, 1)
                    tops(i2, n + 2, range(2, 3))
                    values(i, 2)
                    values(i, 3).then_inc(pv_done, 1)
                    tops(i2, n + 2, range(3, 4))
                    pe.wait_ge(ov_ready, n + 1)
                    for t in range(NT):
                        ins = pe.transpose(pM[:, t * P:(t + 1) * P], OV[:, t * P:(t + 1) * P], ident[:])
                    ins.then_inc(o_psum, 1)
                    tops(i2, n + 2, range(4, AHEAD))


def finish2(nc, x_in, x_out, xt_d, o_d, sel_d, wo, w2, b2, ident_d):
    with ExitStack() as ctx:
        def sb(name, shape, dt=F32):
            return ctx.enter_context(nc.sbuf_tensor("e_" + name, shape, dt))

        def ps(name, shape, dt=F32):
            return ctx.enter_context(nc.psum_tensor("e_" + name, shape, dt))

        sem = Semaphores(ctx, nc, "e_")

        x_v = x_in.rearrange("b (t p) d -> b p t d", p=P)
        y_v = x_out.rearrange("b (t p) d -> b p t d", p=P)
        ident = sb("ident", [P, P])
        WO = sb("WO", [P, KC, D])
        W = sb("W", [P, KC, D])
        BB = sb("BB", [P, D])
        SB = sb("SB", [P, D])
        X = sb("X", [P, 2, NT, D])
        XT = [sb(f"XT{i}", [P, KC, S]) for i in range(2)]
        O = [sb(f"O{i}", [P, NT, D]) for i in range(2)]
        OT = sb("OT", [P, KC, S])
        pT = ps("pT", [P, 2, S])
        pO = ps("pO", [P, NT, S])
        w_in = sem("w_in")
        w_ready = sem("w_ready")
        loaded = [sem("loaded_even"), sem("loaded_odd")]
        ot_psum = sem("ot_psum")
        ot_ready = sem("ot_ready")
        out_psum = sem("out_psum")
        xb_ready = sem("xb_ready")
        y_ready = sem("y_ready")
        y_stored = [sem("y_stored_even"), sem("y_stored_odd")]
        block = ctx.enter_context(nc.Block())

        @block.sync
        def _(sp):
            sp.dma_start(ident[:], ident_d).then_inc(w_in, 16)
            sp.dma_start(BB[:], b2.partition_broadcast(P)).then_inc(w_in, 16)
            sp.dma_start(SB[:], sel_d.partition_broadcast(P)).then_inc(w_in, 16)
            sp.dma_start(W[:], w2).then_inc(w_in, 16)
            sp.dma_start(WO[:], wo).then_inc(w_in, 16)
            for i in range(2):
                sp.sem_inc(y_stored[i], 16)
            with sp.Fori(0, NB // 2) as r:
                for i in range(2):
                    one = bass.ds(2 * r + i, 1)
                    sp.wait_ge(y_stored[i], 16 * (r + 1))
                    sp.dma_start(O[i][:], o_d[one].rearrange("b p t g m -> (b p) t (g m)")).then_inc(loaded[i], 16)
                    sp.dma_start(XT[i][:], xt_d[one].rearrange("b p c n -> (b p) c n")).then_inc(loaded[i], 16)
                    sp.dma_start(X[:, i], x_v[one].rearrange("b p t d -> (b p) t d")).then_inc(loaded[i], 16)

        @block.scalar
        def _(act):
            with act.Fori(0, NB // 2) as r:
                for i in range(2):
                    n = 2 * r + i
                    for c in range(KC):
                        act.wait_ge(ot_psum, n * KC + c + 1)
                        act.activation(OT[:, c], pT[:, c % 2], ACT.Copy).then_inc(ot_ready, 1)
                    act.wait_ge(y_ready, n * NT + NT)
                    act.dma_start(y_v[bass.ds(n, 1)].rearrange("b p t d -> (b p) t d"),
                                  X[:, i]).then_inc(y_stored[i], 16)
            for i in range(2):
                act.wait_ge(y_stored[i], 16 * (NB // 2 + 1))

        @block.gpsimd
        def _(pool):
            pool.wait_ge(w_ready, KC + 1)
            with pool.Fori(0, NB // 2) as r:
                for i in range(2):
                    pool.wait_ge(loaded[i], 48 * (r + 1))
                    for t in range(NT):
                        pool.tensor_tensor(X[:, i, t], X[:, i, t], BB[:], ALU.add).then_inc(xb_ready, 1)

        @block.vector
        def _(dve):
            dve.wait_ge(w_in, 80)
            for c in range(KC):
                dve.tensor_tensor(W[:, c], W[:, c], SB[:], ALU.mult).then_inc(w_ready, 1)
            dve.tensor_tensor(BB[:], BB[:], SB[:], ALU.mult).then_inc(w_ready, 1)
            with dve.Fori(0, NB // 2) as r:
                for i in range(2):
                    n = 2 * r + i
                    for t in range(NT):
                        dve.wait_ge(out_psum, n * NT + t + 1)
                        dve.wait_ge(xb_ready, n * NT + t + 1)
                        dve.tensor_tensor(X[:, i, t], X[:, i, t], pO[:, t], ALU.add).then_inc(y_ready, 1)

        @block.tensor
        def _(pe):
            pe.wait_ge(w_ready, KC + 1)
            pe.wait_ge(w_in, 80)
            with pe.Fori(0, NB // 2) as r:
                for i in range(2):
                    n = 2 * r + i
                    pe.wait_ge(loaded[i], 48 * (r + 1))
                    for c in range(KC):
                        if c >= 2:
                            pe.wait_ge(ot_ready, n * KC + c - 1)
                        for t in range(NT):
                            ins = pe.transpose(pT[:, c % 2, t * P:(t + 1) * P], O[i][:, t, c * P:(c + 1) * P], ident[:])
                        ins.then_inc(ot_psum, 1)
                    for t in range(NT):
                        for c in range(KC):
                            pe.matmul(pO[:, t], XT[i][:, c, t * P:(t + 1) * P], W[:, c], start=(c == 0), stop=False)
                    pe.wait_ge(ot_ready, n * KC + KC)
                    for t in range(NT):
                        for c in range(KC):
                            ins = pe.matmul(pO[:, t], OT[:, c, t * P:(t + 1) * P], WO[:, c], start=False,
                                            stop=(c == KC - 1))
                        ins.then_inc(out_psum, 1)
                    pe.wait_ge(y_ready, n * NT + NT)


def layer2(nc, x_in, x_out, wqkv, cos_d, sin_d, cent, asg, cidx, wo, w2, b2, mask_q, mask_k, pick_d, ident_d, nk=1):
    kw = NG * nk * HD
    xt_d = nc.dram_tensor("c_xt", (NB, P, KC, S), F32).ap()
    q_d = nc.dram_tensor("c_q", (NB, KC, 2, 2, GW, S), F32).ap()
    k_d = nc.dram_tensor("c_k", (NB, kw // P, P // (nk * HD), 2, nk * HD, S), F32).ap()
    v_d = nc.dram_tensor("c_v", (NB, NG, P, NT * nk * VW), F32).ap()
    o_d = nc.dram_tensor("c_o", (NB, P, NT, NG, GW), F32).ap()
    sel_d = nc.dram_tensor("c_sel", (D,), F32).ap()
    scratch = (xt_d, q_d, k_d, v_d)
    project(nc, "c_", nk, x_in, scratch, wqkv, cos_d, sin_d, ident_d, gate=(cent, asg, cidx, sel_d))
    attend(nc, "d_", nk, scratch, o_d, mask_q, mask_k, pick_d, ident_d)
    finish2(nc, x_in, x_out, xt_d, o_d, sel_d, wo, w2, b2, ident_d)

NE3 = 16
NX = NE3 + 2
GC = 96
NGE, EG3 = 4, 4
WE = 2 * D + D + 2
TT = NB * NT
TOPK = 2
NBLK = (TOPK * NB * S + NE3 * (P - 1)) // P + 1
NBX = NBLK + 2
FAR = 65536.0
ROUND = 1.5 * 2 ** 23


def route(nc, keep, x_in, xt_d, o_d, base_d, wo, wr, rb, rbias, ws, eb3, w12, w3, b12, ident_d):
    W12, W3, B12, GATES, CHOSEN = keep
    with ExitStack() as ctx:
        def sb(name, shape, dt=F32):
            return ctx.enter_context(nc.sbuf_tensor("h_" + name, shape, dt))

        def ps(name, shape, dt=F32):
            return ctx.enter_context(nc.psum_tensor("h_" + name, shape, dt))

        sem = Semaphores(ctx, nc, "h_")

        x_v = x_in.rearrange("b (t p) d -> b p t d", p=P)
        base_v = base_d.rearrange("(b t p) d -> b p t d", p=P, t=NT)
        ident = sb("ident", [P, P])
        WO = sb("WO", [P, KC, D])
        WR = sb("WR", [P, KC, NE3])
        RB = sb("RB", [P, NE3])
        RBIAS = sb("RBIAS", [P, NE3])
        EB3 = sb("EB3", [GC, D])
        WS = sb("WS", [P, 2, WE])
        X = sb("X", [P, NT, D])
        XT = sb("XT", [P, KC, S])
        O = sb("O", [P, NT, D])
        OT = sb("OT", [P, KC, S])
        LG = sb("LG", [P, NT, NE3])
        MX = sb("MX", [P, NT])
        EX = sb("EX", [P, NT, NE3])
        SM3 = sb("SM3", [P, NT])
        RC = sb("RC", [P, NT])
        SC = sb("SC", [P, NT, NE3])
        GM = sb("GM", [P, NT, NGE + 6])
        GR = sb("GR", [P, NT, NGE + 6])
        TG = sb("TG", [P, NT, 8])
        PEN = sb("PEN", [P, NT, NGE])
        MS = sb("MS", [P, NT, NE3 + 6])
        MRP = sb("MRP", [P, NT, NE3 + 6])
        TE = sb("TE", [P, NT, 8])
        GT = sb("GT", [P, NT, GC])
        GTT = sb("GTT", [GC, S])
        A = sb("A", [P, S])
        H = sb("H", [P, 2, S])
        HOLD = sb("HOLD", [P, 1])
        pH = ps("pH", [P, 2, S])
        pT = ps("pT", [P, 2, S])
        pY = ps("pY", [P, NT, S])

        w_in = sem("w_in")
        experts_in = sem("experts_in")
        pads_set = sem("pads_set")
        x_loaded = sem("x_loaded")
        xt_loaded = sem("xt_loaded")
        o_loaded = sem("o_loaded")
        y_stored = sem("y_stored")
        logit_psum = sem("logit_psum")
        route_step = sem("route_step")
        shift_ready = sem("shift_ready")
        exp_ready = sem("exp_ready")
        gmax_ready = sem("gmax_ready")
        masked_ready = sem("masked_ready")
        gate_ready = sem("gate_ready")
        ot_psum = sem("ot_psum")
        ot_ready = sem("ot_ready")
        gt_psum = sem("gt_psum")
        gt_ready = sem("gt_ready")
        h_psum = sem("h_psum")
        act_ready = sem("act_ready")
        h_ready = sem("h_ready")
        y_psum = sem("y_psum")
        y_ready = sem("y_ready")
        ROUTE = 11
        block = ctx.enter_context(nc.Block())

        @block.sync
        def _(sp):
            sp.dma_start(ident[:], ident_d).then_inc(w_in, 16)
            sp.dma_start(RB[:], rb.partition_broadcast(P)).then_inc(w_in, 16)
            sp.dma_start(RBIAS[:], rbias.partition_broadcast(P)).then_inc(w_in, 16)
            sp.dma_start(EB3[:], eb3).then_inc(w_in, 16)
            sp.dma_start(WR[:], wr).then_inc(w_in, 16)
            sp.dma_start(WS[:], ws).then_inc(w_in, 16)
            sp.dma_start(WO[:], wo).then_inc(w_in, 16)
            with sp.Fori(0, NB) as b:
                one = bass.ds(b, 1)
                sp.wait_ge(y_stored, b * 16 + 16)
                sp.dma_start(X[:], x_v[one].rearrange("b p t d -> (b p) t d")).then_inc(x_loaded, 16)
                sp.wait_ge(y_ready, b * NT + NT)
                sp.dma_start(base_v[one].rearrange("b p t d -> (b p) t d"), X[:]).then_inc(y_stored, 16)
            sp.wait_ge(y_stored, 16 * NB + 16)

        @block.scalar
        def _(act):
            act.sem_inc(y_stored, 16)
            act.sem_inc(h_psum, 2)
            act.sem_inc(ot_psum, KC)
            with act.Fori(0, NB) as b:
                one = bass.ds(b, 1)
                act.wait_ge(h_psum, b * 2 + 2)
                act.dma_start(XT[:], xt_d[one].rearrange("b p c n -> (b p) c n")).then_inc(xt_loaded, 16)
                act.wait_ge(ot_psum, b * KC + KC)
                act.dma_start(O[:], o_d[one].rearrange("b p t g m -> (b p) t (g m)")).then_inc(o_loaded, 16)
                for t in range(NT):
                    act.wait_ge(shift_ready, b + 1)
                    act.activation(EX[:, t], LG[:, t], ACT.Exp, bias=MX[:, t:t + 1],
                                   accum_out=SM3[:, t:t + 1]).then_inc(exp_ready, 1)
                for s in range(2):
                    act.wait_ge(h_psum, b * 2 + s + 3)
                    act.activation(A[:], pH[:, 0], ACT.Silu, bias=WS[:, s, WE - 2:WE - 1]).then_inc(act_ready, 1)
                    if s == 0:
                        for c in range(KC):
                            act.wait_ge(ot_psum, b * KC + KC + c + 1)
                            act.activation(OT[:, c], pT[:, (c + 1) % 2], ACT.Copy).then_inc(ot_ready, 1)
                            if c == 1:
                                act.wait_ge(h_ready, b * 2 + 1)

        @block.gpsimd
        def _(pool):
            pool.memset(GM[:, :, NGE:], BIG).then_inc(pads_set, 1)
            pool.memset(MS[:, :, NE3:], BIG).then_inc(pads_set, 1)
            pool.memset(GT[:, :, NE3:NX], 1.0).then_inc(pads_set, 1)
            pool.memset(GT[:, :, NX:], 0.0).then_inc(pads_set, 1)
            pool.wait_ge(w_in, 112)
            pool.wait_ge(o_loaded, 16)
            for e in range(0, NE3, 2):
                pool.dma_start(W12[:, e:e + 2], w12[:, e:e + 2]).then_inc(experts_in, 16)
            for e in range(0, NE3, 4):
                pool.dma_start(W3[:, e:e + 4], w3[:, e:e + 4]).then_inc(experts_in, 16)
            pool.dma_start(B12[:], b12.partition_broadcast(P)).then_inc(experts_in, 16)
            pool.wait_ge(experts_in, 16 * (NE3 // 2 + NE3 // 4 + 1))

        @block.vector
        def _(dve):
            dve.wait_ge(pads_set, 4)
            dve.wait_ge(w_in, 112)
            with dve.Fori(0, NB) as b:
                one = bass.ds(b, 1)
                link = Chain(dve, route_step, ROUTE, b)

                def gated(s):
                    dve.wait_ge(act_ready, b * 2 + s + 1)
                    dve.scalar_tensor_tensor(H[:, s], pH[:, 1], WS[:, s, WE - 1:WE], A[:], ALU.add,
                                             ALU.mult).then_inc(h_ready, 1)

                dve.wait_ge(logit_psum, b + 1)
                lg = pT[:, 0, 0:NT * NE3].rearrange("p (t e) -> p t e", t=NT)
                link(dve.tensor_tensor(LG[:], lg, RB[:].unsqueeze(1).to_broadcast([P, NT, NE3]), ALU.add))
                link(dve.tensor_reduce(MX[:], LG[:], AX_X, ALU.max))
                dve.tensor_scalar(MX[:], MX[:], -1.0, None, ALU.mult).then_inc(shift_ready, 1)
                dve.wait_ge(exp_ready, b * NT + NT)
                link(dve.reciprocal(RC[:], SM3[:]))
                for t in range(NT):
                    link(dve.scalar_tensor_tensor(SC[:, t], EX[:, t], RC[:, t:t + 1], RBIAS[:], ALU.mult, ALU.add))
                link(dve.tensor_reduce(GM[:, :, 0:NGE], SC[:].rearrange("p t (g e) -> p t g e", g=NGE), AX_X,
                                       ALU.max))
                gated(0)
                dve.memset(HOLD[:], 0.0)
                for t in range(NT):
                    dve.max(TG[:, t], GM[:, t]).then_inc(gmax_ready, 1)
                dve.wait_ge(gmax_ready, b * 2 * NT + NT)
                dve.memset(HOLD[:], 0.0)
                for t in range(NT):
                    dve.match_replace(GR[:, t], TG[:, t], GM[:, t], -BIG).then_inc(gmax_ready, 1)
                dve.wait_ge(gmax_ready, b * 2 * NT + 2 * NT)
                link(dve.tensor_tensor(PEN[:], GR[:, :, 0:NGE], GM[:, :, 0:NGE], ALU.not_equal))
                link(dve.tensor_scalar(PEN[:], PEN[:], BIG, -BIG, ALU.mult, ALU.add))
                for t in range(NT):
                    dve.tensor_tensor(MS[:, t, 0:NE3].rearrange("p (g e) -> p g e", g=NGE),
                                      SC[:, t].rearrange("p (g e) -> p g e", g=NGE),
                                      PEN[:, t].unsqueeze(2).to_broadcast([P, NGE, EG3]),
                                      ALU.add).then_inc(masked_ready, 1)
                dve.wait_ge(masked_ready, b * 3 * NT + NT)
                dve.memset(HOLD[:], 0.0)
                for t in range(NT):
                    dve.max(TE[:, t], MS[:, t]).then_inc(masked_ready, 1)
                dve.wait_ge(masked_ready, b * 3 * NT + 2 * NT)
                dve.memset(HOLD[:], 0.0)
                for t in range(NT):
                    dve.match_replace(MRP[:, t], TE[:, t], MS[:, t], -BIG).then_inc(masked_ready, 1)
                dve.wait_ge(masked_ready, b * 3 * NT + 3 * NT)
                chosen = CHOSEN[:, one].rearrange("p b t e -> p (b t) e")
                gates = GATES[:, one].rearrange("p b t e -> p (b t) e")
                link(dve.tensor_tensor(chosen, MRP[:, :, 0:NE3], MS[:, :, 0:NE3], ALU.not_equal))
                dve.tensor_tensor(GT[:, :, 0:NE3], chosen, SC[:], ALU.mult).then_inc(gate_ready, 1)
                dve.tensor_tensor(gates, chosen, SC[:], ALU.mult).then_inc(gate_ready, 1)
                gated(1)
                dve.wait_ge(gt_psum, b + 1)
                dve.tensor_copy(GTT[:], pT[0:GC, 0]).then_inc(gt_ready, 1)
                dve.wait_ge(x_loaded, 16 * (b + 1))
                for t in range(NT):
                    dve.wait_ge(y_psum, b * NT + t + 1)
                    dve.tensor_tensor(X[:, t], X[:, t], pY[:, t], ALU.add).then_inc(y_ready, 1)
                link.end()

        @block.tensor
        def _(pe):
            pe.wait_ge(w_in, 112)
            with pe.Fori(0, NB) as b:
                def up(s):
                    for w in range(2):
                        for c in range(KC):
                            at = (w * KC + c) * P
                            ins = pe.matmul(pH[:, w], WS[:, s, at:at + P], XT[:, c], start=(c == 0),
                                            stop=(c == KC - 1))
                    ins.then_inc(h_psum, 1)

                pe.wait_ge(xt_loaded, 16 * (b + 1))
                for t in range(NT):
                    for c in range(KC):
                        ins = pe.matmul(pT[:, 0, t * NE3:(t + 1) * NE3], XT[:, c, t * P:(t + 1) * P], WR[:, c],
                                        start=(c == 0), stop=(c == KC - 1))
                ins.then_inc(logit_psum, 1)
                up(0)
                pe.wait_ge(o_loaded, 16 * (b + 1))
                for c in range(KC):
                    if c == 1:
                        pe.wait_ge(route_step, b * ROUTE + 1)
                    if c >= 2:
                        pe.wait_ge(ot_ready, b * KC + c - 1)
                    for t in range(NT):
                        ins = pe.transpose(pT[:, (c + 1) % 2, t * P:(t + 1) * P], O[:, t, c * P:(c + 1) * P], ident[:])
                    ins.then_inc(ot_psum, 1)
                pe.wait_ge(h_ready, b * 2 + 1)
                up(1)
                pe.wait_ge(ot_ready, b * KC + KC)
                for t in range(NT):
                    for c in range(KC):
                        pe.matmul(pY[:, t], OT[:, c, t * P:(t + 1) * P], WO[:, c], start=(c == 0), stop=False)
                pe.wait_ge(gate_ready, 2 * b + 2)
                for t in range(NT):
                    ins = pe.transpose(pT[0:GC, 0, t * P:(t + 1) * P], GT[:, t], ident[:])
                ins.then_inc(gt_psum, 1)
                pe.wait_ge(h_ready, b * 2 + 2)
                for t in range(NT):
                    for s in range(2):
                        pe.matmul(pY[:, t], H[:, s, t * P:(t + 1) * P], WS[:, s, 2 * D:3 * D], start=False, stop=False)
                pe.wait_ge(gt_ready, b + 1)
                for t in range(NT):
                    pe.matmul(pY[:, t], GTT[:, t * P:(t + 1) * P], EB3[:], start=False,
                              stop=True).then_inc(y_psum, 1)
                pe.wait_ge(y_ready, b * NT + NT)


def place(nc, keep, places, tri, le, kx, tid):
    GATES, CHOSEN = keep
    SLOT, GATE, TOKEN, EXPERT = places
    with ExitStack() as ctx:
        def sb(name, shape, dt=F32):
            return ctx.enter_context(nc.sbuf_tensor("i_" + name, shape, dt))

        def ps(name, shape, dt=F32):
            return ctx.enter_context(nc.psum_tensor("i_" + name, shape, dt))

        sem = Semaphores(ctx, nc, "i_")

        TRI = sb("TRI", [P, P])
        ONES = sb("ONES", [P, P])
        LE = sb("LE", [P, NE3, NE3])
        KX = sb("KX", [P, P])
        TID = sb("TID", [P, TT])
        COUNT = sb("COUNT", [P, NE3])
        FULL = sb("FULL", [P, NE3])
        CMP = sb("CMP", [P, NE3, NE3])
        BLOCKS = sb("BLOCKS", [P, NE3])
        CUM = sb("CUM", [P, NE3, NE3])
        END = sb("END", [P, NE3])
        FIRST = sb("FIRST", [P, NE3])
        ALL = sb("ALL", [P, TT, NE3])
        OWN = sb("OWN", [P, TT, NE3])
        EQ = sb("EQ", [P, TT, NE3])
        SF = sb("SF", [P, TOPK, TT])
        BLK = sb("BLK", [P, TOPK, TT])
        ROW = sb("ROW", [P, TOPK, TT])
        ATROW = sb("ATROW", [P, TOPK, TT, P])
        ATBLK = sb("ATBLK", [P, TOPK, TT, NBX])
        PAST = sb("PAST", [1, NBX, NE3])
        EF = sb("EF", [1, NBX])
        pR = ps("pR", [P, S])
        pC = ps("pC", [P, S])
        pTok = ps("pTok", [P, S])
        w_in = sem("w_in")
        ones_set = sem("ones_set")
        rank_psum = sem("rank_psum")
        step = sem("step")
        row_ready = sem("row_ready")
        blk_equal = sem("blk_equal")
        blk_ready = sem("blk_ready")
        slot_ready = sem("slot_ready")
        expert_ready = sem("expert_ready")
        tok_psum = sem("tok_psum")
        token_ready = sem("token_ready")
        block = ctx.enter_context(nc.Block())
        chosen = CHOSEN[:].rearrange("p b t e -> p (b t) e")
        gates = GATES[:].rearrange("p b t e -> p (b t) e")

        @block.sync
        def _(sp):
            for buf, src in ((TRI, tri), (KX, kx), (LE, le), (TID, tid)):
                sp.dma_start(buf[:], src).then_inc(w_in, 16)

        @block.gpsimd
        def _(pool):
            pool.memset(ONES[:], 1.0).then_inc(ones_set, 1)
            pool.wait_ge(w_in, 64)
            for k in range(TOPK):
                pool.wait_ge(blk_equal, k + 1)
                pool.tensor_tensor(ATBLK[:, k], ATBLK[:, k], TID[:].unsqueeze(2).to_broadcast([P, TT, NBX]),
                                   ALU.mult).then_inc(blk_ready, 1)

        @block.tensor
        def _(pe):
            pe.wait_ge(w_in, 64)
            pe.wait_ge(ones_set, 1)
            pe.matmul(pC[:, 0:TT * NE3], ONES[:], chosen, start=True, stop=True).then_inc(rank_psum, 1)
            pe.matmul(pR[:, 0:TT * NE3], TRI[:], chosen, start=True, stop=False)
            for t in range(TT - 1):
                later = TT - 1 - t
                ins = pe.matmul(pR[:, (t + 1) * NE3:TT * NE3], ONES[:],
                                chosen[:, t].unsqueeze(1).to_broadcast([P, later, NE3]), start=False,
                                stop=(t == TT - 2))
            ins.then_inc(rank_psum, 1)
            for k in range(TOPK):
                pe.wait_ge(row_ready, k + 1)
                pe.wait_ge(blk_ready, k + 1)
                for t in range(TT):
                    ins = pe.matmul(pTok[:, 0:NBX], ATROW[:, k, t], ATBLK[:, k, t], start=(k == 0 and t == 0),
                                    stop=(k == TOPK - 1 and t == TT - 1))
            ins.then_inc(tok_psum, 1)

        @block.vector
        def _(dve):
            link = Chain(dve, step)
            dve.wait_ge(w_in, 64)
            dve.wait_ge(rank_psum, 1)
            link(dve.tensor_reduce(COUNT[:], pC[:, 0:TT * NE3].rearrange("p (t e) -> p e t", t=TT), AX_X, ALU.add))
            link(dve.tensor_scalar(FULL[:], KX[:, 0:NE3], float(P), None, ALU.mult))
            link(dve.tensor_tensor(CMP[:], COUNT[:].unsqueeze(2).to_broadcast([P, NE3, NE3]),
                                   FULL[:].unsqueeze(1).to_broadcast([P, NE3, NE3]), ALU.is_gt))
            link(dve.tensor_reduce(BLOCKS[:], CMP[:], AX_X, ALU.add))
            link(dve.tensor_tensor(CUM[:], LE[:], BLOCKS[:].unsqueeze(1).to_broadcast([P, NE3, NE3]), ALU.mult))
            link(dve.tensor_reduce(END[:], CUM[:], AX_X, ALU.add))
            link(dve.tensor_tensor(FIRST[:], END[:], BLOCKS[:], ALU.subtract))
            link(dve.tensor_scalar(FIRST[:], FIRST[:], float(P), None, ALU.mult))
            dve.wait_ge(rank_psum, 2)
            link(dve.tensor_tensor(ALL[:], pR[:, 0:TT * NE3].rearrange("p (t e) -> p t e", t=TT),
                                   FIRST[:].unsqueeze(1).to_broadcast([P, TT, NE3]), ALU.add))
            link(dve.scalar_tensor_tensor(OWN[:], chosen, -FAR, ALL[:], ALU.mult, ALU.add))
            link(dve.tensor_reduce(SF[:, 0], OWN[:], AX_X, ALU.min))
            link(dve.tensor_scalar(SF[:, 0], SF[:, 0], FAR, None, ALU.add))
            link(dve.tensor_tensor(OWN[:], chosen, ALL[:], ALU.mult))
            link(dve.tensor_reduce(SF[:, 1], OWN[:], AX_X, ALU.max))
            link(dve.tensor_scalar(BLK[:], SF[:], 1.0 / P, -0.498, ALU.mult, ALU.add))
            link(dve.tensor_scalar(BLK[:], BLK[:], ROUND, None, ALU.add))
            link(dve.tensor_scalar(BLK[:], BLK[:], -ROUND, None, ALU.add))
            link(dve.scalar_tensor_tensor(ROW[:], BLK[:], -float(P), SF[:], ALU.mult, ALU.add))
            for k in range(TOPK):
                dve.tensor_tensor(ATBLK[:, k], BLK[:, k].unsqueeze(2).to_broadcast([P, TT, NBX]),
                                  KX[:, 0:NBX].unsqueeze(1).to_broadcast([P, TT, NBX]),
                                  ALU.is_equal).then_inc(blk_equal, 1)
                dve.tensor_tensor(ATROW[:, k], ROW[:, k].unsqueeze(2).to_broadcast([P, TT, P]),
                                  KX[:].unsqueeze(1).to_broadcast([P, TT, P]), ALU.is_equal).then_inc(row_ready, 1)
            dve.tensor_copy(SLOT[:], SF[:]).then_inc(slot_ready, 1)
            link(dve.tensor_tensor(PAST[:], END[0:1].unsqueeze(1).to_broadcast([1, NBX, NE3]),
                                   KX[0:1, 0:NBX].unsqueeze(2).to_broadcast([1, NBX, NE3]), ALU.is_le))
            link(dve.tensor_reduce(EF[:], PAST[:], AX_X, ALU.add))
            link(dve.tensor_scalar(EF[:], EF[:], float(NE3 - 1), None, ALU.min))
            dve.tensor_copy(EXPERT[:], EF[:]).then_inc(expert_ready, 1)
            for k in range(TOPK):
                link(dve.tensor_tensor(EQ[:], ALL[:], SF[:, k].unsqueeze(2).to_broadcast([P, TT, NE3]), ALU.is_equal))
                link(dve.tensor_tensor(EQ[:], EQ[:], gates, ALU.mult))
                link(dve.tensor_reduce(GATE[:, k], EQ[:], AX_X, ALU.add))
            dve.wait_ge(tok_psum, 1)
            dve.tensor_copy(TOKEN[:], pTok[:, 0:NBX]).then_inc(token_ready, 1)


def carry_wait(pool, hold, at):
    pool.tensor_tensor(hold[:, at:at + 1], hold[:, 0:1], hold[:, 0:1], ALU.add)


def experts(nc, keep, places, xn_d, ys_d, ident_d):
    W12, W3, B12 = keep
    TOKEN, EXPERT = places
    UN = 4
    with ExitStack() as ctx:
        def sb(name, shape, dt=F32):
            return ctx.enter_context(nc.sbuf_tensor("j_" + name, shape, dt))

        def ps(name, shape, dt=F32):
            return ctx.enter_context(nc.psum_tensor("j_" + name, shape, dt))

        sem = Semaphores(ctx, nc, "j_")

        ident = sb("ident", [P, P])
        X = [sb(f"X{i}", [P, D]) for i in range(UN)]
        IX = [sb(f"IX{i}", [P, 1], I32) for i in range(UN)]
        HOLD = sb("HOLD", [1, 3])
        XT = [sb(f"XT{i}", [P, KC, P]) for i in range(2)]
        U = sb("U", [P, 2, 2, P])
        A = sb("A", [P, 2, P])
        H = sb("H", [P, 2, P])
        HT = sb("HT", [P, 2, P])
        Y = [sb(f"Y{i}", [P, D]) for i in range(2)]
        pT = ps("pT", [P, 2, S])
        pU = ps("pU", [P, 2, S])
        pHT = ps("pHT", [P, 2, S])
        pY = ps("pY", [P, 2, S])
        w_in = sem("w_in")
        gathered = [sem(f"gathered{i}") for i in range(UN)]
        ix_ready = sem("ix_ready")
        xt_psum = sem("xt_psum")
        xt_ready = sem("xt_ready")
        u_psum = sem("u_psum")
        u_ready = sem("u_ready")
        a_ready = sem("a_ready")
        h_ready = sem("h_ready")
        ht_psum = sem("ht_psum")
        ht_ready = sem("ht_ready")
        y_psum = sem("y_psum")
        y_ready = sem("y_ready")
        stored = [sem("stored_even"), sem("stored_odd")]
        ys_v = ys_d.rearrange("(k p) d -> k p d", p=P)
        block = ctx.enter_context(nc.Block())

        @block.sync
        def _(sp):
            sp.dma_start(ident[:], ident_d).then_inc(w_in, 16)
            for i in range(2):
                sp.sem_inc(stored[i], 16)
            with sp.Fori(0, NBLK // UN) as r:
                for i in range(UN):
                    n = UN * r + i
                    sp.wait_ge(y_ready, n + 3)
                    sp.dma_start(ys_v[bass.ds(n, 1)].rearrange("k p d -> (k p) d"),
                                 Y[i % 2][:]).then_inc(stored[i % 2], 16)
            for i in range(2):
                sp.wait_ge(stored[i], 16 * (NBLK // 2 + 1))

        @block.gpsimd
        def _(pool):
            def gather(i, n):
                pool.tensor_copy(IX[i][:], TOKEN[:, bass.ds(n, 1)]).then_inc(ix_ready, 1)
                pool.wait_ge(ix_ready, n + 2)
                carry_wait(pool, HOLD, 2)
                pool.indirect_dma_start(X[i][:], None, xn_d, bass.IndirectOffsetOnAxis(ap=IX[i][:], axis=0)
                                        ).then_inc(gathered[i], 16)

            pool.memset(HOLD[:], 0.0).then_inc(ix_ready, 1)
            pool.wait_ge(ix_ready, 1)
            for i in range(2):
                gather(i, i)
            pool.sem_inc(xt_psum, 2)
            with pool.Fori(0, NBLK // UN) as r:
                for i in range(UN):
                    n = UN * r + i
                    pool.wait_ge(xt_psum, n + 1)
                    carry_wait(pool, HOLD, 1)
                    gather((i + 2) % UN, n + 2)
            for i in range(UN):
                pool.wait_ge(gathered[i], 16 * (NBLK // UN + (i < 2)))

        @block.scalar
        def _(act):
            def features(i, n):
                act.wait_ge(xt_psum, n + 3)
                act.activation(XT[i % 2][:].rearrange("p c n -> p (c n)"), pT[:, i % 2],
                               ACT.Copy).then_inc(xt_ready, 1)

            def gate(i, n):
                act.wait_ge(u_ready, n + 1)
                act.activation(A[:, i % 2], U[:, i % 2, 0], ACT.Silu).then_inc(a_ready, 1)

            features(0, 0)
            features(1, 1)
            gate(0, 0)
            with act.Fori(0, NBLK // UN) as r:
                for i in range(UN):
                    n = UN * r + i
                    act.wait_ge(ht_psum, n + 1)
                    act.activation(HT[:, i % 2], pHT[:, i % 2, 0:P], ACT.Copy).then_inc(ht_ready, 1)
                    features(i, n + 2)
                    gate(i + 1, n + 1)

        @block.vector
        def _(dve):
            dve.sem_inc(y_ready, 2)

            def biased(i, n):
                e = dve.value_load(EXPERT[0:1, bass.ds(n, 1)], min_val=0, max_val=NE3 - 1)
                dve.wait_ge(u_psum, n + 1)
                dve.tensor_tensor(U[:, i % 2].rearrange("p w m -> p (w m)"), pU[:, i % 2, 0:2 * P],
                                  B12[:, bass.ds(e, 1)].rearrange("p e m -> p (e m)"), ALU.add).then_inc(u_ready, 1)

            def gated(i, n):
                dve.wait_ge(a_ready, n + 1)
                dve.tensor_tensor(H[:, i % 2], U[:, i % 2, 1], A[:, i % 2], ALU.mult).then_inc(h_ready, 1)

            biased(0, 0)
            gated(0, 0)
            with dve.Fori(0, NBLK // UN) as r:
                for i in range(UN):
                    n = UN * r + i
                    biased(i + 1, n + 1)
                    dve.wait_ge(stored[i % 2], 16 * (2 * r + i // 2 + 1))
                    dve.wait_ge(y_psum, n + 1)
                    dve.tensor_copy(Y[i % 2][:], pY[:, i % 2]).then_inc(y_ready, 1)
                    gated(i + 1, n + 1)

        @block.tensor
        def _(pe):
            pe.wait_ge(w_in, 16)

            def turn(i, n, passes):
                pe.wait_ge(gathered[i], 16 * passes)
                for c in range(KC):
                    ins = pe.transpose(pT[:, i % 2, c * P:(c + 1) * P], X[i][:, c * P:(c + 1) * P], ident[:])
                ins.then_inc(xt_psum, 1)

            def up(i, n):
                e = pe.value_load(EXPERT[0:1, bass.ds(n, 1)], min_val=0, max_val=NE3 - 1)
                pe.wait_ge(xt_ready, n + 1)
                for c in range(KC):
                    ins = pe.matmul(pU[:, i % 2, 0:2 * P], XT[i % 2][:, c],
                                    W12[:, bass.ds(e, 1), c].rearrange("p e m -> p (e m)"), start=(c == 0),
                                    stop=(c == KC - 1))
                ins.then_inc(u_psum, 1)
                return e

            turn(0, 0, 1)
            turn(1, 1, 1)
            up(0, 0)
            with pe.Fori(0, NBLK // UN) as r:
                for i in range(UN):
                    n = UN * r + i
                    up(i + 1, n + 1)
                    pe.wait_ge(h_ready, n + 1)
                    pe.transpose(pHT[:, i % 2, 0:P], H[:, i % 2], ident[:]).then_inc(ht_psum, 1)
                    turn((i + 2) % UN, n + 2, r + 1 + (i + 2) // UN)
                    e = pe.value_load(EXPERT[0:1, bass.ds(n, 1)], min_val=0, max_val=NE3 - 1)
                    pe.wait_ge(ht_ready, n + 1)
                    pe.wait_ge(y_ready, n + 1)
                    pe.matmul(pY[:, i % 2], HT[:, i % 2], W3[:, bass.ds(e, 1)].rearrange("p e m -> p (e m)"),
                              start=True, stop=True).then_inc(y_psum, 1)


def combine(nc, places, base_d, ys_d, x_out):
    SLOT, GATE = places
    UN = 4
    with ExitStack() as ctx:
        sem = Semaphores(ctx, nc, "k_")

        B = [ctx.enter_context(nc.sbuf_tensor(f"k_B{i}", [P, D], F32)) for i in range(UN)]
        Y = [ctx.enter_context(nc.sbuf_tensor(f"k_Y{i}", [P, TOPK, D], F32)) for i in range(UN)]
        IX = [ctx.enter_context(nc.sbuf_tensor(f"k_IX{i}", [P, TOPK], I32)) for i in range(UN)]
        HOLD = ctx.enter_context(nc.sbuf_tensor("k_HOLD", [1, 3], F32))
        ix_ready = sem("ix_ready")
        base_loaded = [sem(f"base_loaded{i}") for i in range(UN)]
        gathered = [sem(f"gathered{i}") for i in range(UN)]
        added = sem("added")
        stored = [sem(f"stored{i}") for i in range(UN)]
        base_v = base_d.rearrange("(t p) d -> t p d", p=P)
        out_v = x_out.rearrange("b (t p) d -> (b t) p d", p=P)
        block = ctx.enter_context(nc.Block())

        @block.sync
        def _(sp):
            for i in range(UN):
                sp.sem_inc(stored[i], 16)
            with sp.Fori(0, TT // UN) as r:
                for i in range(UN):
                    sp.wait_ge(stored[i], 16 * (r + 1))
                    sp.dma_start(B[i][:], base_v[bass.ds(UN * r + i, 1)].rearrange("t p d -> (t p) d")
                                 ).then_inc(base_loaded[i], 16)

        @block.gpsimd
        def _(pool):
            pool.memset(HOLD[:], 0.0).then_inc(ix_ready, 1)
            pool.wait_ge(ix_ready, 1)
            pool.sem_inc(added, TOPK * UN)
            with pool.Fori(0, TT // UN) as r:
                for i in range(UN):
                    n = UN * r + i
                    pool.wait_ge(added, TOPK * (n + 1))
                    carry_wait(pool, HOLD, 1)
                    pool.tensor_copy(IX[i][:], SLOT[:, :, bass.ds(n, 1)].rearrange("p k a -> p (k a)")).then_inc(ix_ready, 1)
                    pool.wait_ge(ix_ready, n + 2)
                    carry_wait(pool, HOLD, 2)
                    for k in range(TOPK):
                        pool.indirect_dma_start(Y[i][:, k], None, ys_d,
                                                bass.IndirectOffsetOnAxis(ap=IX[i][:, k:k + 1], axis=0)
                                                ).then_inc(gathered[i], 16)

        @block.vector
        def _(dve):
            with dve.Fori(0, TT // UN) as r:
                for i in range(UN):
                    n = UN * r + i
                    dve.wait_ge(base_loaded[i], 16 * (r + 1))
                    dve.wait_ge(gathered[i], 16 * TOPK * (r + 1))
                    for k in range(TOPK):
                        dve.scalar_tensor_tensor(B[i][:], Y[i][:, k], GATE[:, k, bass.ds(n, 1)], B[i][:], ALU.mult,
                                                 ALU.add).then_inc(added, 1)
                        dve.wait_ge(added, TOPK * (n + UN) + k + 1)

        @block.scalar
        def _(act):
            with act.Fori(0, TT // UN) as r:
                for i in range(UN):
                    n = UN * r + i
                    act.wait_ge(added, TOPK * (n + UN + 1))
                    act.dma_start(out_v[bass.ds(n, 1)].rearrange("t p d -> (t p) d"), B[i][:]).then_inc(stored[i], 16)
            for i in range(UN):
                act.wait_ge(stored[i], 16 * (TT // UN + 1))


def layer3(nc, x_in, x_out, wqkv, cos_d, sin_d, wo, wr, rb, rbias, ws, eb3, w12, w3, b12, tri, le, kx, tid, mask_q,
           mask_k, pick_d, ident_d):
    nk = GH
    kw = NG * nk * HD
    xt_d = nc.dram_tensor("f_xt", (NB, P, KC, S), F32).ap()
    xn_d = nc.dram_tensor("f_xn", (NB * S, D), F32).ap()
    q_d = nc.dram_tensor("f_q", (NB, KC, 2, 2, GW, S), F32).ap()
    k_d = nc.dram_tensor("f_k", (NB, kw // P, P // (nk * HD), 2, nk * HD, S), F32).ap()
    v_d = nc.dram_tensor("f_v", (NB, NG, P, NT * nk * VW), F32).ap()
    o_d = nc.dram_tensor("f_o", (NB, P, NT, NG, GW), F32).ap()
    base_d = nc.dram_tensor("h_base", (NB * S, D), F32).ap()
    ys_d = nc.dram_tensor("j_ys", (NBLK * P, D), F32).ap()
    scratch = (xt_d, q_d, k_d, v_d)
    project(nc, "f_", nk, x_in, scratch, wqkv, cos_d, sin_d, ident_d, xn_d=xn_d)
    attend(nc, "g_", nk, scratch, o_d, mask_q, mask_k, pick_d, ident_d)
    with ExitStack() as ctx:
        def sb(name, shape, dt=F32):
            return ctx.enter_context(nc.sbuf_tensor("m_" + name, shape, dt))

        W12 = sb("W12", [P, NE3, KC, 2 * P])
        W3 = sb("W3", [P, NE3, D])
        B12 = sb("B12", [P, NE3, 2 * P])
        GATES = sb("GATES", [P, NB, NT, NE3])
        CHOSEN = sb("CHOSEN", [P, NB, NT, NE3])
        SLOT = sb("SLOT", [P, TOPK, TT], I32)
        GATE = sb("GATE", [P, TOPK, TT])
        TOKEN = sb("TOKEN", [P, NBX], I32)
        EXPERT = sb("EXPERT", [1, NBX], I32)
        route(nc, (W12, W3, B12, GATES, CHOSEN), x_in, xt_d, o_d, base_d, wo, wr, rb, rbias, ws, eb3, w12, w3,
              b12, ident_d)
        place(nc, (GATES, CHOSEN), (SLOT, GATE, TOKEN, EXPERT), tri, le, kx, tid)
        experts(nc, (W12, W3, B12), (TOKEN, EXPERT), xn_d, ys_d, ident_d)
        combine(nc, (SLOT, GATE), base_d, ys_d, x_out)


def _chunks(w):
    k, n = w.shape
    return w.reshape(k // P, P, n).transpose(1, 0, 2)


def _layout0(i):
    wq = i["L0_attn_Wq"].reshape(H0, G0, P, D)[:, 0].reshape(H0 * P, D).T
    return {
        "wq": _chunks(wq),
        "bq": i["L0_attn_bq"].reshape(H0, G0, P)[:, 0].T,
        "zb": i["L0_attn_z"].T,
        "mt": i["L0_attn_M"].transpose(2, 0, 1),
        "wo": i["L0_attn_Wo"].T.reshape(H0, G0, P, D).transpose(2, 0, 1, 3),
        "wb": _chunks(i["L0_ffn_W_base"].T),
        "bb": i["L0_ffn_b_base"],
        "wr": _chunks(i["L0_ffn_W_router"].T),
        "la": _chunks(i["L0_ffn_A"].reshape(R0, D).T),
        "lb": i["L0_ffn_B"].transpose(0, 2, 1).reshape(R0, D),
        "sel": np.repeat(np.eye(NE0, dtype=np.float32), R0 // NE0, axis=1),
        "ident": np.eye(P, dtype=np.float32),
    }


def _fourier():
    n = np.arange(D)
    f = np.arange(D // 2)
    cos = np.cos(2 * np.pi * ((n[:, None] * f) % D) / D)
    sin = np.sin(2 * np.pi * ((n[:, None] * f) % D) / D)
    sin[:, 0] = np.cos(np.pi * n)
    fwd = np.concatenate([cos, sin], axis=1)
    lag = np.minimum(n, D - n)
    scale = np.full(D // 2, 2.0 / D)
    scale[0] = 1.0 / D
    power = scale[:, None] * np.cos(2 * np.pi * ((f[:, None] * lag) % D) / D)
    power_i = power.copy()
    power_i[0] = np.cos(np.pi * lag) / D
    inv = np.concatenate([scale, scale])[:, None] * fwd.T
    cor = np.concatenate([power, power_i])
    return [_chunks(a.astype(np.float32)) for a in (fwd, cor, inv)]


def _layout1(i):
    fwd, cor, inv = _fourier()
    return {
        "dft": fwd, "cor": cor, "inv": inv,
        "w1": _chunks(i["L1_ffn_W"].T),
        "b1": i["L1_ffn_bias"],
        "a1": i["L1_ffn_lora_A"].reshape(P, D),
        "bl1": i["L1_ffn_lora_B"].transpose(0, 2, 1).reshape(P, D),
        "cf": np.repeat(i["L1_ffn_lora_weights"], 16).reshape(P, 1),
        "ident": np.eye(P, dtype=np.float32),
    }


def _rotary():
    inv = np.float32(1.0) / np.float32(10000.0) ** (np.arange(0, HD, 2, dtype=np.float32) / np.float32(HD))
    ang = np.arange(S, dtype=np.float32)[:, None] * inv[None, :].astype(np.float32)
    return [np.ascontiguousarray(f(ang.astype(np.float64)).astype(np.float32).reshape(NT, P, HD // 2).transpose(1, 0, 2))
            for f in (np.cos, np.sin)]


def _masks():
    row = np.arange(P)
    late = np.where(row[None, :] > row[:, None], np.float32(-1e30), np.float32(0.0))
    return late, np.ascontiguousarray(late.T)


def _pick():
    own = np.broadcast_to(np.eye(GH, dtype=np.float32)[None, :, :, None], (2, GH, GH, S)).reshape(2 * GH, GH * S)
    return np.concatenate([np.zeros((SM - 2 * GH - SW, GH * S), np.float32), own])


def _group_columns(w, heads, pairs_first):
    w = w.reshape(D, NG, heads, *((HD // 2, 2) if pairs_first else (2, HD // 2)))
    return w.transpose(0, 1, *((4, 3) if pairs_first else (3, 4)), 2).reshape(D, NG * heads * HD)


def _layout2(i):
    w = i["L2_attn_w_qkv"]
    cos, sin = _rotary()
    mq, mk = _masks()
    return {
        "wqkv": _chunks(np.concatenate([_group_columns(w[:, :D], GH, True), _group_columns(w[:, D:D + P], 1, True),
                                        w[:, D + P:]], axis=1)),
        "cos": cos, "sin": sin,
        "cent": _chunks(i["L2_ffn_centroids"].T),
        "asg": i["L2_ffn_assignments"],
        "cidx": np.arange(NCL, dtype=np.float32).reshape(NCL, 1),
        "wo": _chunks(i["L2_attn_w_o"]),
        "w2": _chunks(i["L2_ffn_weight"].T),
        "b2": i["L2_ffn_bias"],
        "mq": mq, "mk": mk, "pick": _pick(),
        "ident": np.eye(P, dtype=np.float32),
    }


def _layout3(i):
    cos, sin = _rotary()
    mq, mk = _masks()
    halves = [slice(0, P), slice(P, 2 * P)]
    sw = [np.stack([i[name][:, h] for h in halves]) for name in ("L3_ffn_sw1", "L3_ffn_sw2")]
    up = [w.reshape(2, KC, P, P).transpose(0, 2, 1, 3).reshape(2, P, D) for w in sw]
    ws = np.concatenate([*up, i["L3_ffn_sw3"].reshape(2, P, D),
                         i["L3_ffn_sb1"].reshape(2, P, 1), i["L3_ffn_sb2"].reshape(2, P, 1)], axis=2)
    w12 = np.concatenate([i["L3_ffn_ew1"], i["L3_ffn_ew2"]], axis=2)
    row = np.arange(P)
    expert = np.arange(NE3)
    return {
        "wqkv": _chunks(np.concatenate([_group_columns(i["L3_attn_wq"].T, GH, False),
                                        _group_columns(i["L3_attn_wk"].T, GH, False), i["L3_attn_wv"].T], axis=1)),
        "cos": cos, "sin": sin,
        "wo": _chunks(i["L3_attn_wo"].T),
        "wr": _chunks(i["L3_ffn_router_w"]),
        "rb": i["L3_ffn_router_b"],
        "rbias": i["L3_ffn_router_bias"],
        "ws": ws.transpose(1, 0, 2),
        "eb3": np.concatenate([i["L3_ffn_eb3"], i["L3_ffn_sb3"][None], np.zeros((GC - NE3 - 1, D), np.float32)]),
        "w12": w12.reshape(NE3, KC, P, 2 * P).transpose(2, 0, 1, 3),
        "w3": i["L3_ffn_ew3"].transpose(1, 0, 2),
        "b12": np.concatenate([i["L3_ffn_eb1"], i["L3_ffn_eb2"]], axis=1),
        "tri": (row[:, None] < row[None, :]).astype(np.float32),
        "le": np.broadcast_to((expert[None, :] <= expert[:, None]).astype(np.float32), (P, NE3, NE3)),
        "kx": np.broadcast_to(np.arange(P, dtype=np.float32), (P, P)),
        "tid": np.arange(TT * P, dtype=np.float32).reshape(TT, P).T,
        "mq": mq, "mk": mk, "pick": _pick(),
        "ident": np.eye(P, dtype=np.float32),
    }


def build(nc, x, out, arrays):
    between = [nc.dram_tensor(f"x{n}", (NB, S, D), F32).ap() for n in (1, 2, 3)]
    for layer, x_in, x_out, ins in zip((layer0, layer1, layer2, layer3), (x, *between), (*between, out), arrays):
        layer(nc, x_in, x_out, *ins)


def kernel(**inputs):
    import concourse.bacc as _bacc
    from concourse.bass_utils import run_bass_kernel_spmd as _run

    inputs = {k: np.asarray(v) for k, v in inputs.items()}
    nc = _bacc.Bacc("TRN2", target_bir_lowering=False, num_devices=1)
    arrays = {}

    def given(name, a):
        arrays[name] = np.ascontiguousarray(a)
        return nc.dram_tensor(name, arrays[name].shape, mybir.dt.from_np(arrays[name].dtype),
                              kind="ExternalInput").ap()

    x = given("in_x", inputs["L0_attn_hidden_states"])
    layers = [[given(f"in_{n}_{name}", a) for name, a in layout(inputs).items()]
              for n, layout in enumerate((_layout0, _layout1, _layout2, _layout3))]
    out = nc.dram_tensor("out", (NB, S, D), F32, kind="ExternalOutput").ap()
    build(nc, x, out, layers)
    return _run(nc, [arrays], core_ids=[0]).results[0]["out"]
```
